# Optimizing a Trainium2 kernel written in Bass

```python
import numpy as np
import jax
import jax.numpy as jnp

def _softmax(x, axis=-1):
    return jax.nn.softmax(x, axis=axis)

def _gelu(x):
    return jax.nn.gelu(x, approximate=True)

def _silu(x):
    return jax.nn.silu(x)

def _sigmoid(x):
    return jax.nn.sigmoid(x)

def _layernorm(x, axis=-1, eps=1e-05):
    m = jnp.mean(x, axis=axis, keepdims=True)
    v = jnp.var(x, axis=axis, keepdims=True)
    return (x - m) / jnp.sqrt(v + eps)

def _scatter_add(tgt, idx, src, axis=0):
    return tgt.at[idx].add(src)

def _segment_sum(src, seg, n):
    return jax.ops.segment_sum(src, seg, n)
kernel_name = 'mk_macaron_d2_jaxref_r4_8089a6'

def setup_inputs(seed: int=0):
    np.random.seed(seed)
    _w = jnp.asarray

    def _L0_attn_setup():
        import jax, jax.numpy as jnp
        import numpy as np
        D_MODEL = 256
        N_HEADS = 16
        LATENT_HEADS = 8
        LATENT_DIM = 128
        N_LATENTS = 64
        WINDOW = 64
        HEAD_DIM = D_MODEL // N_HEADS
        LAT_HD = LATENT_DIM // LATENT_HEADS
        B, S = (2, 1024)

        def _pool_to_latents(x):
            Bx, Sx, C = x.shape
            chunk = max(1, Sx // N_LATENTS)
            return x.reshape(Bx, N_LATENTS, chunk, C).mean(axis=2)

        def _local_window_attn(Q, K, V):
            Bx, H, Sx, D = Q.shape
            W = WINDOW
            nb = Sx // W
            Qb = Q.reshape(Bx, H, nb, W, D)
            Kp = jnp.pad(K, ((0, 0), (0, 0), (W, 0), (0, 0))).reshape(Bx, H, nb + 1, W, D)
            Vp = jnp.pad(V, ((0, 0), (0, 0), (W, 0), (0, 0))).reshape(Bx, H, nb + 1, W, D)
            Kw = jnp.concatenate([Kp[:, :, :-1], Kp[:, :, 1:]], axis=3)
            Vw = jnp.concatenate([Vp[:, :, :-1], Vp[:, :, 1:]], axis=3)
            i = jnp.arange(W)[:, None]
            j = jnp.arange(2 * W)[None, :]
            base = (j > i) & (j <= i + W)
            blk0 = (jnp.arange(nb) > 0)[:, None, None] | (j >= W)[None, :, :]
            mask = base[None, :, :] & blk0
            sc = jnp.einsum('bhnid,bhnjd->bhnij', Qb, Kw) / np.sqrt(D).astype(np.float32)
            sc = jnp.where(mask[None, None], sc, -jnp.inf)
            p = jax.nn.softmax(sc, axis=-1)
            out = jnp.einsum('bhnij,bhnjd->bhnid', p, Vw)
            return out.reshape(Bx, H, Sx, D)
        key = jax.random.key(seed)
        ks = jax.random.split(key, 11)
        std = 0.02
        w = lambda k, shp: jax.random.normal(k, shp, jnp.float32) * std
        return {'x': jax.random.normal(ks[0], (B, S, D_MODEL), jnp.float32), 'wq': w(ks[1], (D_MODEL, D_MODEL)), 'wk': w(ks[2], (D_MODEL, D_MODEL)), 'wv': w(ks[3], (D_MODEL, D_MODEL)), 'wgq': w(ks[4], (D_MODEL, LATENT_DIM)), 'wgk': w(ks[5], (D_MODEL, LATENT_DIM)), 'wgv': w(ks[6], (D_MODEL, LATENT_DIM)), 'r_out_w': w(ks[7], (LATENT_DIM, D_MODEL)), 'gate_local_w': w(ks[8], (N_HEADS, HEAD_DIM)), 'gate_remote_w': w(ks[9], (N_HEADS, HEAD_DIM)), 'w_out': w(ks[10], (D_MODEL, D_MODEL))}
    _L0_attn_in = _L0_attn_setup()

    def _L0_ffn_setup():
        import jax, jax.numpy as jnp
        import numpy as np

        def _binarize(w):
            alpha = jax.lax.stop_gradient(jnp.mean(jnp.abs(w), axis=1, keepdims=True))
            bw = alpha * jnp.sign(w)
            return w + jax.lax.stop_gradient(bw - w)
        key = jax.random.key(seed)
        k1, k2, k3, k4, k5 = jax.random.split(key, 5)
        D, H = (256, 1024)
        x = jax.random.normal(k1, (64, 196, D), dtype=jnp.float32)
        w1 = jax.random.normal(k2, (H, D), dtype=jnp.float32) * 0.02
        b1 = jax.random.normal(k3, (H,), dtype=jnp.float32) * 0.02
        w2 = jax.random.normal(k4, (D, H), dtype=jnp.float32) * 0.02
        b2 = jax.random.normal(k5, (D,), dtype=jnp.float32) * 0.02
        return {'x': x, 'w1': w1, 'b1': b1, 'w2': w2, 'b2': b2}
    _L0_ffn_in = _L0_ffn_setup()

    def _L1_attn_setup():
        import jax, jax.numpy as jnp
        import numpy as np
        NUM_BUCKETS = 63

        def _rp_bucket(N):
            rel = jnp.arange(N)[None, :] - jnp.arange(N)[:, None]
            half = NUM_BUCKETS // 2
            return (jnp.clip(rel, -half, half) + half).astype(jnp.int32)
        key = jax.random.key(seed)
        ks = jax.random.split(key, 7)
        B, N, C, H = (4, 256, 256, 16)
        hd = C // H
        g = lambda k, shp, sc: jax.random.normal(k, shp, jnp.float32) * sc
        return {'x': g(ks[0], (B, N, C), 1.0), 'w_qkv': g(ks[1], (3 * C, C), C ** (-0.5)), 'w_proj': g(ks[2], (C, C), C ** (-0.5)), 'b_proj': jnp.zeros((C,), jnp.float32), 'rpe_q_table': g(ks[3], (H, hd, NUM_BUCKETS), 0.02), 'rpe_k_table': g(ks[4], (H, hd, NUM_BUCKETS), 0.02), 'rpe_v_table': g(ks[5], (H, NUM_BUCKETS, hd), 0.02)}
    _L1_attn_in = _L1_attn_setup()

    def _L1_ffn_setup():
        import jax, jax.numpy as jnp
        import numpy as np
        LN_EPS = 0.001
        EPS = 1e-05
        QB = 128.0

        def ste_round(x):
            return x + jax.lax.stop_gradient(jnp.round(x) - x)
        key = jax.random.key(seed)
        k1, k2 = jax.random.split(key)
        x = jax.random.normal(k1, (4, 2048, 256), dtype=jnp.float32)
        weight = jax.random.normal(k2, (256, 256), dtype=jnp.float32) * 0.02
        ln_gamma = jnp.ones((256,), dtype=jnp.float32)
        ln_beta = jnp.zeros((256,), dtype=jnp.float32)
        return {'x': x, 'weight': weight, 'ln_gamma': ln_gamma, 'ln_beta': ln_beta}
    _L1_ffn_in = _L1_ffn_setup()
    _d = {'L0_attn_x': _L0_attn_in['x'], 'L0_attn_wq': _L0_attn_in['wq'], 'L0_attn_wk': _L0_attn_in['wk'], 'L0_attn_wv': _L0_attn_in['wv'], 'L0_attn_wgq': _L0_attn_in['wgq'], 'L0_attn_wgk': _L0_attn_in['wgk'], 'L0_attn_wgv': _L0_attn_in['wgv'], 'L0_attn_r_out_w': _L0_attn_in['r_out_w'], 'L0_attn_gate_local_w': _L0_attn_in['gate_local_w'], 'L0_attn_gate_remote_w': _L0_attn_in['gate_remote_w'], 'L0_attn_w_out': _L0_attn_in['w_out'], 'L0_ffn_w1': _L0_ffn_in['w1'], 'L0_ffn_b1': _L0_ffn_in['b1'], 'L0_ffn_w2': _L0_ffn_in['w2'], 'L0_ffn_b2': _L0_ffn_in['b2'], 'L1_attn_w_qkv': _L1_attn_in['w_qkv'], 'L1_attn_w_proj': _L1_attn_in['w_proj'], 'L1_attn_b_proj': _L1_attn_in['b_proj'], 'L1_attn_rpe_q_table': _L1_attn_in['rpe_q_table'], 'L1_attn_rpe_k_table': _L1_attn_in['rpe_k_table'], 'L1_attn_rpe_v_table': _L1_attn_in['rpe_v_table'], 'L1_ffn_weight': _L1_ffn_in['weight'], 'L1_ffn_ln_gamma': _L1_ffn_in['ln_gamma'], 'L1_ffn_ln_beta': _L1_ffn_in['ln_beta']}
    _x0 = _d['L0_attn_x']
    _d['L0_attn_x'] = jax.random.normal(jax.random.fold_in(jax.random.key(seed), 1), (4, 1024, 256), dtype=_x0.dtype)
    del _x0
    return _d

def reference(L0_attn_x, L0_attn_wq, L0_attn_wk, L0_attn_wv, L0_attn_wgq, L0_attn_wgk, L0_attn_wgv, L0_attn_r_out_w, L0_attn_gate_local_w, L0_attn_gate_remote_w, L0_attn_w_out, L0_ffn_w1, L0_ffn_b1, L0_ffn_w2, L0_ffn_b2, L1_attn_w_qkv, L1_attn_w_proj, L1_attn_b_proj, L1_attn_rpe_q_table, L1_attn_rpe_k_table, L1_attn_rpe_v_table, L1_ffn_weight, L1_ffn_ln_gamma, L1_ffn_ln_beta):

    def _L0_attn_ref(x, wq, wk, wv, wgq, wgk, wgv, r_out_w, gate_local_w, gate_remote_w, w_out):
        import jax, jax.numpy as jnp
        import numpy as np
        D_MODEL = 256
        N_HEADS = 16
        LATENT_HEADS = 8
        LATENT_DIM = 128
        N_LATENTS = 64
        WINDOW = 64
        HEAD_DIM = D_MODEL // N_HEADS
        LAT_HD = LATENT_DIM // LATENT_HEADS
        B, S = (2, 1024)

        def _pool_to_latents(x):
            Bx, Sx, C = x.shape
            chunk = max(1, Sx // N_LATENTS)
            return x.reshape(Bx, N_LATENTS, chunk, C).mean(axis=2)

        def _local_window_attn(Q, K, V):
            Bx, H, Sx, D = Q.shape
            W = WINDOW
            nb = Sx // W
            Qb = Q.reshape(Bx, H, nb, W, D)
            Kp = jnp.pad(K, ((0, 0), (0, 0), (W, 0), (0, 0))).reshape(Bx, H, nb + 1, W, D)
            Vp = jnp.pad(V, ((0, 0), (0, 0), (W, 0), (0, 0))).reshape(Bx, H, nb + 1, W, D)
            Kw = jnp.concatenate([Kp[:, :, :-1], Kp[:, :, 1:]], axis=3)
            Vw = jnp.concatenate([Vp[:, :, :-1], Vp[:, :, 1:]], axis=3)
            i = jnp.arange(W)[:, None]
            j = jnp.arange(2 * W)[None, :]
            base = (j > i) & (j <= i + W)
            blk0 = (jnp.arange(nb) > 0)[:, None, None] | (j >= W)[None, :, :]
            mask = base[None, :, :] & blk0
            sc = jnp.einsum('bhnid,bhnjd->bhnij', Qb, Kw) / np.sqrt(D).astype(np.float32)
            sc = jnp.where(mask[None, None], sc, -jnp.inf)
            p = jax.nn.softmax(sc, axis=-1)
            out = jnp.einsum('bhnij,bhnjd->bhnid', p, Vw)
            return out.reshape(Bx, H, Sx, D)
        Bx, Sx, _ = x.shape
        chunk = max(1, Sx // N_LATENTS)
        Q = (x @ wq).reshape(Bx, Sx, N_HEADS, HEAD_DIM).transpose(0, 2, 1, 3)
        K = (x @ wk).reshape(Bx, Sx, N_HEADS, HEAD_DIM).transpose(0, 2, 1, 3)
        V = (x @ wv).reshape(Bx, Sx, N_HEADS, HEAD_DIM).transpose(0, 2, 1, 3)
        local = _local_window_attn(Q, K, V)
        GQ = (x @ wgq).reshape(Bx, Sx, LATENT_HEADS, LAT_HD).transpose(0, 2, 1, 3)
        GK = _pool_to_latents(x @ wgk).reshape(Bx, N_LATENTS, LATENT_HEADS, LAT_HD).transpose(0, 2, 1, 3)
        GV = _pool_to_latents(x @ wgv).reshape(Bx, N_LATENTS, LATENT_HEADS, LAT_HD).transpose(0, 2, 1, 3)
        lsc = jnp.einsum('bhsd,bhnd->bhsn', GQ, GK) / np.sqrt(LAT_HD).astype(np.float32)
        lmask = jnp.arange(N_LATENTS)[None, :] <= (jnp.arange(Sx) // chunk)[:, None]
        lsc = jnp.where(lmask[None, None], lsc, -jnp.inf)
        lp = jax.nn.softmax(lsc, axis=-1)
        rem = jnp.einsum('bhsn,bhnd->bhsd', lp, GV)
        rem = rem.transpose(0, 2, 1, 3).reshape(Bx, Sx, LATENT_DIM) @ r_out_w
        rem = rem.reshape(Bx, Sx, N_HEADS, HEAD_DIM).transpose(0, 2, 1, 3)
        gl = jax.nn.sigmoid(jnp.einsum('bhsd,hd->bhs', Q, gate_local_w))[..., None]
        gr = jax.nn.sigmoid(jnp.einsum('bhsd,hd->bhs', Q, gate_remote_w))[..., None]
        out = gl * local + gr * rem
        out = out.transpose(0, 2, 1, 3).reshape(Bx, Sx, D_MODEL)
        return out @ w_out

    def _L0_ffn_ref(x, w1, b1, w2, b2):
        import jax, jax.numpy as jnp
        import numpy as np

        def _binarize(w):
            alpha = jax.lax.stop_gradient(jnp.mean(jnp.abs(w), axis=1, keepdims=True))
            bw = alpha * jnp.sign(w)
            return w + jax.lax.stop_gradient(bw - w)
        bw1 = _binarize(w1)
        h = jnp.einsum('bsd,hd->bsh', x, bw1) + b1
        h = jax.nn.gelu(h, approximate=False)
        bw2 = _binarize(w2)
        out = jnp.einsum('bsh,dh->bsd', h, bw2) + b2
        return out

    def _L1_attn_ref(x, w_qkv, w_proj, b_proj, rpe_q_table, rpe_k_table, rpe_v_table):
        import jax, jax.numpy as jnp
        import numpy as np
        NUM_BUCKETS = 63

        def _rp_bucket(N):
            rel = jnp.arange(N)[None, :] - jnp.arange(N)[:, None]
            half = NUM_BUCKETS // 2
            return (jnp.clip(rel, -half, half) + half).astype(jnp.int32)
        B, N, C = x.shape
        H = rpe_k_table.shape[0]
        hd = C // H
        scale = hd ** (-0.5)
        qkv = (x @ w_qkv.T).reshape(B, N, 3, H, hd).transpose(2, 0, 3, 1, 4)
        q, k, v = (qkv[0] * scale, qkv[1], qkv[2])
        attn = jnp.einsum('bhid,bhjd->bhij', q, k)
        rp = _rp_bucket(N)
        idx = rp[None, None]
        qL = jnp.einsum('bhid,hdm->bhim', q, rpe_k_table)
        attn = attn + jnp.take_along_axis(qL, idx, axis=-1)
        kL = jnp.einsum('bhjd,hdm->bhjm', k * scale, rpe_q_table)
        attn = attn + jnp.swapaxes(jnp.take_along_axis(kL, idx, axis=-1), 2, 3)
        attn = jax.nn.softmax(attn, axis=-1)
        out = jnp.einsum('bhij,bhjd->bhid', attn, v)
        a_t = attn.transpose(2, 3, 0, 1)
        S = jax.vmap(lambda a, seg: jax.ops.segment_sum(a, seg, num_segments=NUM_BUCKETS))(a_t, rp)
        out = out + jnp.einsum('inbh,hnd->bhid', S, rpe_v_table)
        x_out = out.transpose(0, 2, 1, 3).reshape(B, N, C)
        return x_out @ w_proj.T + b_proj

    def _L1_ffn_ref(x, weight, ln_gamma, ln_beta):
        import jax, jax.numpy as jnp
        import numpy as np
        LN_EPS = 0.001
        EPS = 1e-05
        QB = 128.0

        def ste_round(x):
            return x + jax.lax.stop_gradient(jnp.round(x) - x)
        mu = jnp.mean(x, axis=-1, keepdims=True)
        var = jnp.var(x, axis=-1, keepdims=True)
        xn = (x - mu) * jax.lax.rsqrt(var + LN_EPS) * ln_gamma + ln_beta
        beta = jnp.mean(jnp.abs(weight))
        w_q = jnp.clip(ste_round(weight / (beta + EPS)), -1.0, 1.0)
        gamma = jnp.max(jnp.abs(xn))
        xq = jnp.clip(xn * QB / gamma, -QB + EPS, QB - EPS)
        y = jnp.einsum('bsd,du->bsu', xq, w_q)
        return y * (gamma * beta / QB)
    x = L0_attn_x
    x = x + 0.5 * _L0_ffn_ref(_layernorm(x, axis=-1), L0_ffn_w1, L0_ffn_b1, L0_ffn_w2, L0_ffn_b2)
    x = x + _L0_attn_ref(_layernorm(x, axis=-1), L0_attn_wq, L0_attn_wk, L0_attn_wv, L0_attn_wgq, L0_attn_wgk, L0_attn_wgv, L0_attn_r_out_w, L0_attn_gate_local_w, L0_attn_gate_remote_w, L0_attn_w_out)
    x = x + 0.5 * _L0_ffn_ref(_layernorm(x, axis=-1), L0_ffn_w1, L0_ffn_b1, L0_ffn_w2, L0_ffn_b2)
    x = x + 0.5 * _L1_ffn_ref(_layernorm(x, axis=-1), L1_ffn_weight, L1_ffn_ln_gamma, L1_ffn_ln_beta)
    x = x + _L1_attn_ref(_layernorm(x, axis=-1), L1_attn_w_qkv, L1_attn_w_proj, L1_attn_b_proj, L1_attn_rpe_q_table, L1_attn_rpe_k_table, L1_attn_rpe_v_table)
    x = x + 0.5 * _L1_ffn_ref(_layernorm(x, axis=-1), L1_ffn_weight, L1_ffn_ln_gamma, L1_ffn_ln_beta)
    return x

_drawn_inputs = setup_inputs


def setup_inputs(seed=0):
    import zlib

    import numpy as np

    out = dict(_drawn_inputs(seed))
    spreads = {'L1_attn_b_proj': (0.0, 0.1),
     'L1_ffn_ln_gamma': (1.0, 0.6),
     'L1_ffn_ln_beta': (0.0, 0.991)}
    factors = {'L0_attn_wq': 8.0,
     'L0_attn_wk': 8.0,
     'L0_attn_wv': 7.291,
     'L0_attn_wgq': 8.0,
     'L0_attn_wgk': 8.0,
     'L0_attn_wgv': 8.0,
     'L0_attn_r_out_w': 8.0,
     'L0_attn_gate_local_w': 8.0,
     'L0_attn_gate_remote_w': 8.0,
     'L0_attn_w_out': 7.187,
     'L0_ffn_b1': 8.0,
     'L1_attn_rpe_q_table': 56.328,
     'L1_attn_rpe_k_table': 64.0,
     'L1_attn_rpe_v_table': 9.969}
    for name, (base, spread) in spreads.items():
        noise = np.random.default_rng([zlib.crc32(name.encode()), seed]).standard_normal(out[name].shape)
        drawn = base * np.exp(spread * noise) if base else spread * noise
        out[name] = jnp.asarray(drawn.astype(out[name].dtype))
    for name, factor in factors.items():
        out[name] = (out[name] * factor).astype(out[name].dtype)
    return out
```

```python
import numpy as np
import concourse.bass as bass
from concourse import mybir
from contextlib import ExitStack

F32 = mybir.dt.float32
F16 = mybir.dt.float16
ALU = mybir.AluOpType
ACT = mybir.ActivationFunctionType
AX = mybir.AxisListType
P = 128
B, S, D = 4, 1024, 256
NT = B * S // P
TPB = S // P
KD = D // P
HID = 1024
MH = HID // P
CT = 4
NC = NT // CT
CW = CT * P


ONE = 16


class Count:

    def __init__(self, sem, base=0, it=None, per=0):
        self.sem, self.k, self.it, self.per = sem, base, it, per

    def value(self):
        return ONE + self.k if self.it is None else ONE + self.it * self.per + self.k


def step(eng, ins, c):
    ins.then_inc(c.sem, 1)
    c.k += 1
    eng.wait_ge(c.sem, c.value())


def arm(sp, s):
    for x in s.values():
        sp.sem_inc(x, ONE)


def sems(nc, ctx, prefix, names):
    s = {n: nc.alloc_semaphore(f"{prefix}_{n}") for n in names.split()}

    def clear():
        with nc.Block() as block:
            @block.sync
            def _(sp):
                for x in s.values():
                    sp.sem_clear(x)
        for x in s.values():
            nc.release_semaphore(x)
    ctx.callback(clear)
    return s


STW = 1 + 4 * 6 + 4 * 2


def token_stats(nc, dve, rows, st, mv_out, n, c):
    sums = st[:, 1:25].rearrange("p (t s) -> p t s", t=4)
    agg = st[:, 25:33].rearrange("p (t s) -> p t s", t=4)
    for t in range(n):
        last = nc.vector.bn_stats(sums[:, t, :], rows[:, t, :])
    step(dve, last, c)
    nc.vector.memset(st[:, 0:1], 0.0)
    for t in range(n):
        last = nc.vector.bn_aggr(agg[:, t, :], sums[:, t, :])
    step(dve, last, c)
    step(dve, nc.vector.tensor_scalar(mv_out, agg[:, 0:n, :], 1.0, None, ALU.mult), c)


def prep_phase(nc, G, A):
    with ExitStack() as ctx:
        sb = lambda n, s, d=F32: ctx.enter_context(nc.sbuf_tensor(n, s, d))
        w1n = sb("w1n", [P, MH, D])
        w2n = sb("w2n", [P, KD, HID])
        pos = sb("pos", [P, 2048])
        sg1 = sb("sg1", [P, MH, D])
        sg2 = sb("sg2", [P, KD, HID])
        a2 = sb("a2", [P, KD])
        diag = sb("diag", [P, KD, P])
        row = sb("row0", [P, 1, D])
        st = sb("st0", [P, STW])
        pt = ctx.enter_context(nc.psum_tensor("pt0", [P, 4, 512], F32))
        pa = ctx.enter_context(nc.psum_tensor("pa0", [P, 512], F32))
        s = sems(nc, ctx, "prep", "x_in w1_in w2_in b_in dve zero ident ones signs diag tr evac bcast")
        block = ctx.enter_context(nc.Block())

        @block.sync
        def _(sp):
            arm(sp, s)
            sp.dma_start(G.x[:, :, :], A["x"].rearrange("b (t p) d -> p (b t) d", p=P)).then_inc(s["x_in"], 16)
            sp.dma_start(w1n[:, :, :], A["w1"].rearrange("(m p) d -> p m d", p=P)).then_inc(s["w1_in"], 16)
            sp.dma_start(w2n[:, :, :], A["w2"].rearrange("(k p) h -> p k h", p=P)).then_inc(s["w2_in"], 16)
            sp.dma_start(G.b1[:, :], A["b1"].rearrange("(m p) -> p m", p=P),
                         allow_slow_non_contiguous=True).then_inc(s["b_in"], 16)
            sp.dma_start(G.b2h[:, :], A["b2"].partition_broadcast(P)).then_inc(s["b_in"], 16)
            sp.wait_ge(s["b_in"], ONE + 32)

        @block.gpsimd
        def _(pool):
            nc.gpsimd.memset(G.ident[:, :], 0.0).then_inc(s["zero"], 1)
            nc.gpsimd.memset(G.ones[:, :], 1.0).then_inc(s["ones"], 1)
            pool.wait_ge(s["zero"], ONE + 1)
            nc.gpsimd.affine_select(out=G.ident[:, :], in_=G.ident[:, :], compare_op=ALU.not_equal, fill=1.0,
                                    base=0, pattern=[[-1, P]], channel_multiplier=1).then_inc(s["ident"], 1)

        @block.vector
        def _(dve):
            c = Count(s["dve"])

            def do(ins):
                step(dve, ins, c)

            def sign(w, out, n):
                flat = pos[:, 0:n]
                do(nc.vector.tensor_scalar(flat, w, 0.0, None, ALU.is_lt))
                do(nc.vector.scalar_tensor_tensor(out, w, 0.0, flat, ALU.is_gt, ALU.subtract))
            dve.wait_ge(s["w1_in"], ONE + 16)
            do(nc.vector.tensor_reduce(G.a1[:, :], w1n[:, :, :], AX.X, ALU.add, apply_absolute_value=True))
            do(nc.vector.tensor_scalar(G.a1[:, :], G.a1[:, :], 1.0 / D, None, ALU.mult))
            sign(w1n[:, :, :].rearrange("p m d -> p (m d)"), sg1[:, :, :].rearrange("p m d -> p (m d)"), MH * D)
            dve.wait_ge(s["w2_in"], ONE + 16)
            do(nc.vector.tensor_reduce(a2[:, :], w2n[:, :, :], AX.X, ALU.add, apply_absolute_value=True))
            do(nc.vector.tensor_scalar(a2[:, :], a2[:, :], 0.5 / HID, None, ALU.mult))
            sign(w2n[:, :, :].rearrange("p m d -> p (m d)"), sg2[:, :, :].rearrange("p m d -> p (m d)"), KD * HID)
            nc.vector.memset(pos[:, 0:1], 0.0).then_inc(s["signs"], 1)
            dve.wait_ge(s["ident"], ONE + 1)
            for k in range(KD):
                do(nc.vector.tensor_scalar(diag[:, k, :], G.ident[:, :], a2[:, k:k + 1], None, ALU.mult))
            nc.vector.memset(pos[:, 0:1], 0.0).then_inc(s["diag"], 1)
            for g in range(8):
                dve.wait_ge(s["tr"], ONE + g + 1)
                if g < 4:
                    dst = G.sw1T[:, g // 2, (g % 2) * 512:(g % 2) * 512 + 512]
                else:
                    dst = G.sw2T[:, 2 * (g - 4):2 * (g - 4) + 2, :].rearrange("p m d -> p (m d)")
                step(dve, nc.vector.tensor_copy(dst, pt[:, g % 4, :]), Count(s["evac"], g))
            dve.wait_ge(s["bcast"], ONE + 1)
            do(nc.vector.tensor_copy(G.a2h[:, :], pa[:, 0:D]))
            dve.wait_ge(s["b_in"], ONE + 32)
            do(nc.vector.tensor_scalar(G.b2h[:, :], G.b2h[:, :], 0.5, None, ALU.mult))
            dve.wait_ge(s["x_in"], ONE + 16)
            with dve.Fori(0, NT) as t:
                cl = Count(s["dve"], c.k, t, 4)
                step(dve, nc.vector.tensor_scalar(row[:, 0, :], G.x[:, t, :], 1.0, None, ALU.mult), cl)
                token_stats(nc, dve, row, st, G.mv[:, bass.ds(t, 1), :], 1, cl)

        @block.tensor
        def _(pe):
            pe.wait_ge(s["ident"], ONE + 1)
            pe.wait_ge(s["signs"], ONE + 1)
            for g in range(8):
                if g >= 4:
                    pe.wait_ge(s["evac"], ONE + g - 3)
                for q in range(4):
                    if g < 4:
                        src = sg1[:, (g % 2) * 4 + q, (g // 2) * P:(g // 2) * P + P]
                    else:
                        m = 2 * (g - 4) + q // 2
                        src = sg2[:, q % 2, m * P:m * P + P]
                    last = nc.tensor.transpose(pt[:, g % 4, q * P:q * P + P], src, G.ident[:, :])
                last.then_inc(s["tr"], 1)
            pe.wait_ge(s["diag"], ONE + 1)
            pe.wait_ge(s["ones"], ONE + 1)
            for k in range(KD):
                last = nc.tensor.matmul(pa[:, k * P:k * P + P], G.ones[:, :], diag[:, k, :], start=True, stop=True)
            last.then_inc(s["bcast"], 1)


def ffn_phase(nc, G, r):
    with ExitStack() as ctx:
        sb = lambda n, s, d=F32: ctx.enter_context(nc.sbuf_tensor(f"f{r}_{n}", s, d))
        ps = lambda n, s: ctx.enter_context(nc.psum_tensor(f"f{r}_{n}", s, F32))
        sd = sb("sd", [P, NT])
        rstd = sb("rstd", [P, NT])
        eps = sb("eps", [P, 1])
        xn = sb("xn", [P, CT, D])
        xhi = sb("xhi", [P, KD, CW], F16)
        xlo = sb("xlo", [P, KD, CW], F16)
        h = sb("h", [P, 2, CW])
        hhi = sb("hhi", [P, 2, CW], F16)
        hlo = sb("hlo", [P, 2, CW], F16)
        y = sb("y", [P, CT, D])
        st = sb("st", [P, STW])
        psT = ps("psT", [P, KD, 512])
        psH = ps("psH", [P, 2, 512])
        psY = ps("psY", [P, CT, 512])
        s = sems(nc, ctx, f"ffn{r}", "eps sd dve xn xT xhi xlo H h hhi hlo Y out")
        block = ctx.enter_context(nc.Block())
        OUT_PER = 7

        @block.sync
        def _(sp):
            arm(sp, s)

        @block.scalar
        def _(act):
            act.wait_ge(s["eps"], ONE + 1)
            nc.scalar.activation(sd[:, :], G.mv[:, :, 1], ACT.Sqrt, bias=eps[:, :]).then_inc(s["sd"], 1)
            with act.Fori(0, NC) as i:
                for k in range(KD):
                    act.wait_ge(s["xT"], ONE + i * KD + k + 1)
                    if k == 0:
                        act.wait_ge(s["H"], ONE + i * MH)
                    nc.scalar.activation(xhi[:, k, :], psT[:, k, :], ACT.Copy).then_inc(s["xhi"], 1)
                for m in range(MH):
                    act.wait_ge(s["H"], ONE + i * MH + m + 1)
                    if m >= 2:
                        act.wait_ge(s["hlo"], ONE + i * MH + m - 1)
                    nc.scalar.activation(h[:, m % 2, :], psH[:, m % 2, :], ACT.Gelu, bias=G.b1[:, m:m + 1],
                                         scale=G.a1[:, m:m + 1]).then_inc(s["h"], 1)
                    act.wait_ge(s["h"], ONE + i * MH + m + 1)
                    if m >= 2:
                        act.wait_ge(s["Y"], ONE + i * MH + m - 1)
                    nc.scalar.activation(hhi[:, m % 2, :], h[:, m % 2, :], ACT.Copy).then_inc(s["hhi"], 1)

        @block.vector
        def _(dve):
            step(dve, nc.vector.memset(eps[:, :], 1e-5), Count(s["eps"]))
            dve.wait_ge(s["sd"], ONE + 1)
            c = Count(s["dve"])
            step(dve, nc.vector.reciprocal(rstd[:, :], sd[:, :]), c)
            with dve.Fori(0, NC) as i:
                dve.wait_ge(s["xT"], ONE + i * KD)
                for t in range(CT):
                    nc.vector.tensor_scalar(xn[:, t, :], G.x[:, i * CT + t, :], G.mv[:, i * CT + t, 0:1],
                                            rstd[:, bass.ds(i * CT + t, 1)], ALU.subtract,
                                            ALU.mult).then_inc(s["xn"], 1)
                for k in range(KD):
                    dve.wait_ge(s["xhi"], ONE + i * KD + k + 1)
                    nc.vector.tensor_tensor(xlo[:, k, :], psT[:, k, :], xhi[:, k, :], ALU.subtract).then_inc(s["xlo"], 1)
                for m in range(MH):
                    dve.wait_ge(s["hhi"], ONE + i * MH + m + 1)
                    nc.vector.tensor_tensor(hlo[:, m % 2, :], h[:, m % 2, :], hhi[:, m % 2, :],
                                            ALU.subtract).then_inc(s["hlo"], 1)
                dve.wait_ge(s["Y"], ONE + i * MH + MH)
                cl = Count(s["out"], 0, i, OUT_PER)
                rows = G.x[:, bass.ds(i * CT, CT), :]
                step(dve, nc.vector.tensor_tensor(y[:, :, :], psY[:, :, 0:D],
                                                  G.a2h[:, :].unsqueeze(1).to_broadcast([P, CT, D]), ALU.mult), cl)
                step(dve, nc.vector.tensor_tensor(y[:, :, :], y[:, :, :],
                                                  G.b2h[:, :].unsqueeze(1).to_broadcast([P, CT, D]), ALU.add), cl)
                step(dve, nc.vector.tensor_tensor(y[:, :, :], y[:, :, :], rows, ALU.add), cl)
                step(dve, nc.vector.tensor_scalar(rows, y[:, :, :], 1.0, None, ALU.mult), cl)
                token_stats(nc, dve, y, st, G.mv[:, bass.ds(i * CT, CT), :], CT, cl)
                assert cl.k == OUT_PER



        @block.tensor
        def _(pe):
            def hidden(i, m):
                if m < 2:
                    pe.wait_ge(s["h"], ONE + i * MH)
                else:
                    pe.wait_ge(s["h"], ONE + i * MH + m - 1)
                for k in range(KD):
                    for part, x in enumerate((xhi, xlo)):
                        last = nc.tensor.matmul(psH[:, m % 2, :], G.sw1T[:, k, m * P:m * P + P], x[:, k, :],
                                                start=(k + part == 0), stop=(k == KD - 1 and part == 1))
                last.then_inc(s["H"], 1)

            def down(i, m):
                pe.wait_ge(s["hlo"], ONE + i * MH + m + 1)
                for t in range(CT):
                    for part, x in enumerate((hhi, hlo)):
                        last = nc.tensor.matmul(psY[:, t, 0:D], x[:, m % 2, t * P:t * P + P], G.sw2T[:, m, :],
                                                start=(m + part == 0), stop=(m == MH - 1 and part == 1))
                last.then_inc(s["Y"], 1)

            with pe.Fori(0, NC) as i:
                pe.wait_ge(s["xn"], ONE + i * CT + CT)
                pe.wait_ge(s["xlo"], ONE + i * KD)
                for k in range(KD):
                    for t in range(CT):
                        last = nc.tensor.transpose(psT[:, k, t * P:t * P + P], xn[:, t, k * P:k * P + P],
                                                   G.ident[:, :])
                    last.then_inc(s["xT"], 1)
                pe.wait_ge(s["xlo"], ONE + i * KD + KD)
                pe.wait_ge(s["out"], ONE + i * OUT_PER)
                hidden(i, 0)
                for m in range(MH):
                    if m + 1 < MH:
                        hidden(i, m + 1)
                    down(i, m)


NEG = -1e30
WIN = 64
NH, HD = 16, 16
HQ = NH // 4
LH, NL = 8, 64
CHUNK = S // NL
LW = 192


def rstd_phase(nc, G, name, eps_value):
    with ExitStack() as ctx:
        sd = ctx.enter_context(nc.sbuf_tensor(f"{name}_sd", [P, NT], F32))
        eps = ctx.enter_context(nc.sbuf_tensor(f"{name}_eps", [P, 1], F32))
        s = sems(nc, ctx, name, "eps sd rstd")
        block = ctx.enter_context(nc.Block())

        @block.sync
        def _(sp):
            arm(sp, s)

        @block.scalar
        def _(act):
            act.wait_ge(s["eps"], ONE + 1)
            nc.scalar.activation(sd[:, :], G.mv[:, :, 1], ACT.Sqrt, bias=eps[:, :]).then_inc(s["sd"], 1)

        @block.vector
        def _(dve):
            step(dve, nc.vector.memset(eps[:, :], eps_value), Count(s["eps"]))
            dve.wait_ge(s["sd"], ONE + 1)
            step(dve, nc.vector.reciprocal(G.rstd[:, :], sd[:, :]), Count(s["rstd"]))


def local_phase(nc, G, A):
    rstd_phase(nc, G, "a0n", 1e-5)
    with ExitStack() as ctx:
        sb = lambda n, s, d=F32: ctx.enter_context(nc.sbuf_tensor(f"a0_{n}", s, d))
        ps = lambda n, s: ctx.enter_context(nc.psum_tensor(f"a0_{n}", s, F32))
        wq = sb("wq", [P, KD, NH, 32])
        wk = sb("wk", [P, KD, NH, 32])
        wgq = sb("wgq", [P, KD, LH, 32])
        wgk = sb("wgk", [P, KD, LH, 32])
        wv = sb("wv", [P, KD, D])
        wgv = sb("wgv", [P, KD, P])
        wr = sb("wr", [P, D])
        wo = sb("wo", [P, KD, D])
        gates = sb("gates", [P, HQ, 2, NH])
        mask = sb("mask", [P, 2, LW])
        lmask = sb("lmask", [P, TPB, NL])
        xn = sb("xn", [P, TPB, D])
        xT = sb("xT", [P, KD, S])
        xp = sb("xp", [P, KD, 2, NL])
        QT = sb("QT", [P, HQ, S])
        KT = sb("KT", [P, HQ, P + S])
        V = sb("V", [P, TPB, D])
        GQT = sb("GQT", [P, 2, S])
        GKT = sb("GKT", [P, 2, NL])
        GV = sb("GV", [P, LH // 2, 32])
        gt = sb("gt", [P, TPB, 2 * NH])
        Sm = sb("Sm", [P, 2, 4, LW])
        mx = sb("mx", [P, 2, 4])
        nb = sb("nb", [P, 2, 4])
        Pe = sb("Pe", [P, 2, 4, 256])
        rs = sb("rs", [P, 2, 4])
        ri = sb("ri", [P, 2, 4])
        PT = sb("PT", [P, 2, 1024])
        loc = sb("loc", [P, TPB, D])
        sl = sb("sl", [P, 4, LH, NL])
        lm = sb("lm", [P, 4, LH])
        slT = sb("slT", [P, 4, 512])
        rem = sb("rem", [P, 4, P])
        remT = sb("remT", [P, 4, P])
        o = sb("o", [P, 4, D])
        o2 = sb("o2", [P, 4, D])
        oT = sb("oT", [P, 4, D])
        st = sb("st", [P, STW])
        R = ps("R", [P, 4, 512])
        Z = ps("Z", [P, 4, 512])
        s = sems(nc, ctx, "a0", "w_in zero masks pool xn tr xT pooled pj pj_a pj_d S masked max shift exp T PTa PTd O recip norm "
                 "gexp gates lS lmasked lmax lsub lexp lsum lrecip B Bev C rem Dt Dev E gated o F Fev out stat")
        block = ctx.enter_context(nc.Block())
        PROJ = ([("q", m, c) for c in range(2) for m in range(HQ)] + [("k", m, c) for c in range(2) for m in range(HQ)]
                + [("gq", m, c) for m in range(2) for c in range(2)] + [("v", t, 0) for t in range(0, TPB, 2)]
                + [("g", 0, 0), ("gate", 0, 0)])
        NPJ = len(PROJ)
        UNITS = [(t, hq) for t in range(TPB) for hq in range(HQ)]
        NU = len(UNITS)

        def pj_done(i, j):
            return i * ((NPJ + 1) // 2) + (j + 2) // 2, i * (NPJ // 2) + (j + 1) // 2

        @block.sync
        def _(sp):
            arm(sp, s)
            sp.wait_ge(s["zero"], ONE + 1)
            with nc.allow_non_contiguous_dma("weights by head, once"):
                for dst, src in ((wq, "wq"), (wk, "wk"), (wgq, "wgq"), (wgk, "wgk")):
                    for k in range(KD):
                        sp.dma_start(dst[:, k, :, 0:HD],
                                     A[src][k * P:(k + 1) * P, :].rearrange("p (h d) -> p h d", d=HD)).then_inc(s["w_in"], 16)
                sp.dma_start(wv[:, :, :], A["wv"].rearrange("(k p) d -> p k d", p=P)).then_inc(s["w_in"], 16)
                sp.dma_start(wgv[:, :, :], A["wgv"].rearrange("(k p) d -> p k d", p=P)).then_inc(s["w_in"], 16)
                sp.dma_start(wr[:, :], A["r_out_w"]).then_inc(s["w_in"], 16)
                sp.dma_start(wo[:, :, :], A["w_out"].rearrange("(k p) d -> p k d", p=P)).then_inc(s["w_in"], 16)
                for n, g in enumerate(("gl", "gr")):
                    for h in range(NH):
                        sp.dma_start(gates[32 * (h % 4):32 * (h % 4) + HD, h // 4, n, h:h + 1],
                                     A[g][h:h + 1, :].rearrange("a d -> d a")).then_inc(s["w_in"], 16)

        NWIN = 16 * (8 + 4 + 2 * NH)

        @block.gpsimd
        def _(pool):
            c = Count(s["pool"])
            nc.gpsimd.memset(wq[:, :, :, :], 0.0)
            nc.gpsimd.memset(wk[:, :, :, :], 0.0)
            nc.gpsimd.memset(wgq[:, :, :, :], 0.0)
            nc.gpsimd.memset(wgk[:, :, :, :], 0.0)
            nc.gpsimd.memset(gates[:, :, :, :], 0.0).then_inc(s["zero"], 1)
            nc.gpsimd.memset(KT[:, :, 0:P], 0.0)
            nc.gpsimd.memset(Pe[:, :, :, 0:WIN], 0.0)
            nc.gpsimd.memset(GV[:, :, :], 0.0)
            nc.gpsimd.memset(lmask[:, :, :], 0.0)
            step(pool, nc.gpsimd.memset(mask[:, :, :], 0.0), c)
            step(pool, nc.gpsimd.affine_select(out=mask[:, :, :], in_=mask[:, :, :], compare_op=ALU.is_gt, fill=NEG,
                                               base=0, pattern=[[0, 2], [1, LW]], channel_multiplier=-1), c)
            step(pool, nc.gpsimd.affine_select(out=mask[:, :, :], in_=mask[:, :, :], compare_op=ALU.is_ge, fill=NEG,
                                               base=WIN, pattern=[[0, 2], [-1, LW]], channel_multiplier=1), c)
            step(pool, nc.gpsimd.affine_select(out=mask[:, 0, :], in_=mask[:, 0, :], compare_op=ALU.is_ge, fill=NEG,
                                               base=-WIN, pattern=[[1, LW]], channel_multiplier=0), c)
            nc.gpsimd.affine_select(out=lmask[:, :, :], in_=lmask[:, :, :], compare_op=ALU.is_ge, fill=NEG, base=0,
                                    pattern=[[P, TPB], [-CHUNK, NL]], channel_multiplier=1).then_inc(s["masks"], 1)

        def evacuate(i, copy, j, kind, m, c):
            bank = R[:, j % 4, :]
            cols = slice(c * 512, c * 512 + 512)
            if kind == "q":
                return copy(QT[:, m, cols], bank)
            if kind == "k":
                return copy(KT[:, m, P + c * 512:P + c * 512 + 512], bank)
            if kind == "gq":
                return copy(GQT[:, m, cols], bank)
            if kind == "v":
                return copy(V[:, m:m + 2, :].rearrange("p t d -> p (t d)"), bank)
            if kind == "g":
                copy(GKT[:, :, :].rearrange("p m n -> p (m n)"), bank[:, 0:2 * NL])
                gv = bank[:, P:2 * P].rearrange("p (q a d) -> p q a d", a=2, d=HD)
                copy(GV[0:NL, :, 0:HD], gv[0:NL, :, 0, :])
                return copy(GV[NL:P, :, HD:32], gv[NL:P, :, 1, :])
            return copy(gt[:, :, :].rearrange("p t n -> p (t n)"), bank[:, 0:TPB * 2 * NH])

        @block.scalar
        def _(act):
            copy = lambda o_, i_: nc.scalar.activation(o_, i_, ACT.Copy)
            with act.Fori(0, B) as i:
                for g in range(4):
                    act.wait_ge(s["tr"], ONE + i * 4 + g + 1)
                    copy(xT[:, g // 2, (g % 2) * 512:(g % 2) * 512 + 512], Z[:, g, :]).then_inc(s["xT"], 1)
                for j, (kind, m, c) in enumerate(PROJ):
                    if j % 2 == 0:
                        act.wait_ge(s["pj"], ONE + i * NPJ + j + 1)
                        evacuate(i, copy, j, kind, m, c).then_inc(s["pj_a"], 1)
                for u in range(NU + 1):
                    if u < NU:
                        act.wait_ge(s["shift"], ONE + i * NU + u + 1)
                        if u >= 2:
                            act.wait_ge(s["T"], ONE + 2 * (i * NU + u - 1))
                            act.wait_ge(s["recip"], ONE + i * NU + u - 1)
                        for c in range(4):
                            last = nc.scalar.activation(Pe[:, u % 2, c, WIN:256], Sm[:, u % 2, c, :], ACT.Exp,
                                                        bias=nb[:, u % 2, c:c + 1], scale=0.25,
                                                        accum_out=rs[:, u % 2, c:c + 1])
                        last.then_inc(s["exp"], 1)
                    if u >= 1:
                        v = u - 1
                        act.wait_ge(s["T"], ONE + 2 * (i * NU + v) + 1)
                        if v >= 2:
                            act.wait_ge(s["O"], ONE + i * NU + v - 1)
                        copy(PT[:, v % 2, 0:512], Z[:, 0, :]).then_inc(s["PTa"], 1)
                for g in range(2):
                    if g == 0:
                        act.wait_ge(s["pj_d"], ONE + i * (NPJ // 2) + NPJ // 2)
                        act.wait_ge(s["pj_a"], ONE + (i + 1) * ((NPJ + 1) // 2))
                        nc.scalar.activation(gt[:, :, :], gt[:, :, :], ACT.Exp, scale=-1.0).then_inc(s["gexp"], 1)
                    for t in range(4 * g, 4 * g + 4):
                        act.wait_ge(s["lsub"], ONE + i * TPB + t + 1)
                        nc.scalar.activation(sl[:, t % 4, :, :], sl[:, t % 4, :, :], ACT.Exp,
                                             scale=0.25).then_inc(s["lexp"], 1)
                    for t in range(4 * g, 4 * g + 4):
                        act.wait_ge(s["B"], ONE + i * TPB + t + 1)
                        copy(slT[:, t % 4, :], Z[:, t % 4, :]).then_inc(s["Bev"], 1)
                    for t in range(4 * g, 4 * g + 4):
                        act.wait_ge(s["Dt"], ONE + i * TPB + t + 1)
                        copy(remT[:, t % 4, :], Z[:, t % 4, 0:P]).then_inc(s["Dev"], 1)
                    for t in range(4 * g, 4 * g + 4):
                        act.wait_ge(s["F"], ONE + i * TPB + t + 1)
                        copy(oT[:, t % 4, :], Z[:, t % 4, 0:D]).then_inc(s["Fev"], 1)

        @block.vector
        def _(dve):
            copy = lambda o_, i_: nc.vector.tensor_copy(o_, i_)

            def do(ins, name, value):
                ins.then_inc(s[name], 1)
                dve.wait_ge(s[name], ONE + value)

            dve.wait_ge(s["masks"], ONE + 1)
            with dve.Fori(0, B) as i:
                for t in range(TPB):
                    nc.vector.tensor_scalar(xn[:, t, :], G.x[:, i * TPB + t, :], G.mv[:, i * TPB + t, 0:1],
                                            G.rstd[:, bass.ds(i * TPB + t, 1)], ALU.subtract,
                                            ALU.mult).then_inc(s["xn"], 1)
                dve.wait_ge(s["xT"], ONE + i * 4 + 4)
                for k in range(KD):
                    ins = nc.vector.tensor_reduce(xp[:, k, 0, :], xT[:, k, :].rearrange("p (n c) -> p n c", c=CHUNK),
                                                  AX.X, ALU.add)
                do(ins, "pooled", i * 3 + 1)
                do(nc.vector.tensor_scalar(xp[:, :, 0, :], xp[:, :, 0, :], 1.0 / CHUNK, None, ALU.mult), "pooled", i * 3 + 2)
                do(nc.vector.tensor_copy(xp[:, :, 1, :], xp[:, :, 0, :]), "pooled", i * 3 + 3)
                for j, (kind, m, c) in enumerate(PROJ):
                    if j % 2 == 1:
                        dve.wait_ge(s["pj"], ONE + i * NPJ + j + 1)
                        evacuate(i, copy, j, kind, m, c).then_inc(s["pj_d"], 1)
                for u in range(NU + 2):
                    if u < NU:
                        t, hq = UNITS[u]
                        b = u % 2
                        dve.wait_ge(s["S"], ONE + i * NU + u + 1)
                        if u >= 2:
                            dve.wait_ge(s["exp"], ONE + i * NU + u - 1)
                        do(nc.vector.tensor_tensor(Sm[:, b, :, :], R[:, :, 0:LW],
                                                   mask[:, min(t, 1), :].unsqueeze(1).to_broadcast([P, 4, LW]),
                                                   ALU.add), "masked", i * NU + u + 1)
                        do(nc.vector.tensor_reduce(mx[:, b, :], Sm[:, b, :, :], AX.X, ALU.max), "max", i * NU + u + 1)
                        nc.vector.tensor_scalar(nb[:, b, :], mx[:, b, :], -0.25, None, ALU.mult).then_inc(s["shift"], 1)
                    if 1 <= u <= NU:
                        v = u - 1
                        dve.wait_ge(s["T"], ONE + 2 * (i * NU + v) + 2)
                        if v >= 2:
                            dve.wait_ge(s["O"], ONE + i * NU + v - 1)
                        copy(PT[:, v % 2, 512:1024], Z[:, 1, :]).then_inc(s["PTd"], 1)
                    if u >= 2:
                        v = u - 2
                        t, hq = UNITS[v]
                        dve.wait_ge(s["O"], ONE + i * NU + v + 1)
                        do(nc.vector.reciprocal(ri[:, v % 2, :], rs[:, v % 2, :]), "recip", i * NU + v + 1)
                        dst = loc[:, t, hq * 64:hq * 64 + 64].rearrange("p (c d) -> p c d", c=4)
                        nc.vector.tensor_tensor(dst, Z[:, 2, 0:64].rearrange("p (c d) -> p c d", c=4),
                                                ri[:, v % 2, :].unsqueeze(2).to_broadcast([P, 4, HD]),
                                                ALU.mult).then_inc(s["norm"], 1)
                dve.wait_ge(s["gexp"], ONE + i + 1)
                do(nc.vector.tensor_scalar(gt[:, :, :], gt[:, :, :], 1.0, None, ALU.add), "gates", i * 2 + 1)
                do(nc.vector.reciprocal(gt[:, :, :], gt[:, :, :]), "gates", i * 2 + 2)
                for g in range(2):
                    tiles = range(4 * g, 4 * g + 4)
                    for t in tiles:
                        q, n = t % 4, i * TPB + t + 1
                        dve.wait_ge(s["lS"], ONE + i * TPB + 4 * g + 4)
                        for m in range(2):
                            ins = nc.vector.tensor_tensor(sl[:, q, 4 * m:4 * m + 4, :],
                                                          R[:, :, (2 * q + m) * NL:(2 * q + m) * NL + NL],
                                                          lmask[:, t, :].unsqueeze(1).to_broadcast([P, 4, NL]), ALU.add)
                        do(ins, "lmasked", n)
                        do(nc.vector.tensor_reduce(lm[:, q, :], sl[:, q, :, :], AX.X, ALU.max), "lmax", n)
                        nc.vector.tensor_tensor(sl[:, q, :, :], sl[:, q, :, :],
                                                lm[:, q, :].unsqueeze(2).to_broadcast([P, LH, NL]),
                                                ALU.subtract).then_inc(s["lsub"], 1)
                    for t in tiles:
                        q, n = t % 4, i * TPB + t + 1
                        dve.wait_ge(s["lexp"], ONE + n)
                        do(nc.vector.tensor_reduce(lm[:, q, :], sl[:, q, :, :], AX.X, ALU.add), "lsum", n)
                        do(nc.vector.reciprocal(lm[:, q, :], lm[:, q, :]), "lrecip", n)
                    for t in tiles:
                        q, n = t % 4, i * TPB + t + 1
                        dve.wait_ge(s["C"], ONE + n)
                        nc.vector.tensor_tensor(rem[:, q, :].rearrange("p (h d) -> p h d", h=LH),
                                                R[:, q, 0:P].rearrange("p (h d) -> p h d", h=LH),
                                                lm[:, q, :].unsqueeze(2).to_broadcast([P, LH, HD]),
                                                ALU.mult).then_inc(s["rem"], 1)
                    for t in tiles:
                        q, n = t % 4, i * TPB + t + 1
                        heads = lambda a: a.rearrange("p (h d) -> p h d", h=NH)
                        gate = lambda w: gt[:, t, w * NH:(w + 1) * NH].unsqueeze(2).to_broadcast([P, NH, HD])
                        dve.wait_ge(s["E"], ONE + n)
                        if t >= 4:
                            dve.wait_ge(s["F"], ONE + n - 4)
                        nc.vector.tensor_tensor(heads(o2[:, q, :]), heads(loc[:, t, :]), gate(0), ALU.mult)
                        do(nc.vector.tensor_tensor(heads(o[:, q, :]), heads(R[:, q, 0:D]), gate(1), ALU.mult), "gated", n)
                        nc.vector.tensor_tensor(o[:, q, :], o[:, q, :], o2[:, q, :], ALU.add).then_inc(s["o"], 1)
                    for t in tiles:
                        q, n = t % 4, i * TPB + t + 1
                        dve.wait_ge(s["out"], ONE + n)
                        cs = Count(s["stat"], 5 * t, i, 5 * TPB)
                        row = G.x[:, i * TPB + t, :]
                        step(dve, nc.vector.tensor_tensor(o2[:, q, :], R[:, q, 0:D], row, ALU.add), cs)
                        step(dve, nc.vector.tensor_scalar(row, o2[:, q, :], 1.0, None, ALU.mult), cs)
                        token_stats(nc, dve, o2[:, q:q + 1, :], st, G.mv[:, bass.ds(i * TPB + t, 1), :], 1, cs)

        @block.tensor
        def _(pe):
            pe.wait_ge(s["w_in"], ONE + NWIN)
            pe.wait_ge(s["masks"], ONE + 1)
            mm = nc.tensor.matmul
            with pe.Fori(0, B) as i:
                pe.wait_ge(s["xn"], ONE + i * TPB + TPB)
                pe.wait_ge(s["Fev"], ONE + i * TPB)
                for g in range(4):
                    for q in range(4):
                        t = (g % 2) * 4 + q
                        ins = nc.tensor.transpose(Z[:, g, q * P:q * P + P], xn[:, t, (g // 2) * P:(g // 2) * P + P],
                                                  G.ident[:, :])
                    ins.then_inc(s["tr"], 1)
                pe.wait_ge(s["xT"], ONE + i * 4 + 4)
                pe.wait_ge(s["stat"], ONE + i * 5 * TPB)
                for j, (kind, m, c) in enumerate(PROJ):
                    if j >= 4:
                        na, nd = pj_done(i, j - 4)
                        pe.wait_ge(s["pj_a"], ONE + na) if j % 2 == 0 else pe.wait_ge(s["pj_d"], ONE + nd)
                    bank = R[:, j % 4, :]
                    for k in range(KD):
                        fl = dict(start=k == 0, stop=k == KD - 1)
                        cols = slice(c * 512, c * 512 + 512)
                        if kind in ("q", "k", "gq"):
                            w = {"q": wq, "k": wk, "gq": wgq}[kind]
                            ins = mm(bank, w[:, k, 4 * m:4 * m + 4, :].rearrange("p h d -> p (h d)"), xT[:, k, cols], **fl)
                    if kind == "v":
                        for t in (m, m + 1):
                            for k in range(KD):
                                ins = mm(bank[:, (t - m) * D:(t - m) * D + D], xT[:, k, t * P:t * P + P], wv[:, k, :],
                                         start=k == 0, stop=k == KD - 1)
                    if kind == "g":
                        pe.wait_ge(s["pooled"], ONE + i * 3 + 3)
                        for mg in range(2):
                            for k in range(KD):
                                ins = mm(bank[:, mg * NL:mg * NL + NL],
                                         wgk[:, k, 4 * mg:4 * mg + 4, :].rearrange("p h d -> p (h d)"), xp[:, k, 0, :],
                                         start=k == 0, stop=k == KD - 1)
                        for k in range(KD):
                            ins = mm(bank[:, P:2 * P], xp[:, k, :, :].rearrange("p a n -> p (a n)"), wgv[:, k, :],
                                     start=k == 0, stop=k == KD - 1)
                    if kind == "gate":
                        for t in range(TPB):
                            for mq in range(HQ):
                                ins = mm(bank[:, t * 32:t * 32 + 32], QT[:, mq, t * P:t * P + P],
                                         gates[:, mq, :, :].rearrange("p a h -> p (a h)"),
                                         start=mq == 0, stop=mq == HQ - 1)
                    ins.then_inc(s["pj"], 1)
                na, nd = pj_done(i, NPJ - 1)
                pe.wait_ge(s["pj_a"], ONE + na)
                pe.wait_ge(s["pj_d"], ONE + nd)
                for u in range(NU + 2):
                    if u < NU:
                        t, hq = UNITS[u]
                        if u >= 1:
                            pe.wait_ge(s["masked"], ONE + i * NU + u)
                        for c in range(4):
                            rows = slice(32 * c, 32 * c + HD)
                            ins = mm(R[:, c, 0:LW],
                                     QT[rows, hq, t * P:t * P + P], KT[rows, hq, t * P + WIN:t * P + WIN + LW],
                                     start=True, stop=True)
                        ins.then_inc(s["S"], 1)
                    if 1 <= u <= NU:
                        v = u - 1
                        pe.wait_ge(s["exp"], ONE + i * NU + v + 1)
                        for half in range(2):
                            if v >= 1:
                                pe.wait_ge(s["PTa"] if half == 0 else s["PTd"], ONE + i * NU + v)
                            for n in range(4):
                                c, w = 2 * half + n // 2, n % 2
                                ins = nc.tensor.transpose(Z[:, half, n * P:n * P + P],
                                                          Pe[:, v % 2, c, w * P:w * P + P], G.ident[:, :])
                            ins.then_inc(s["T"], 1)
                    if u >= 2:
                        v = u - 2
                        t, hq = UNITS[v]
                        pe.wait_ge(s["PTa"], ONE + i * NU + v + 1)
                        pe.wait_ge(s["PTd"], ONE + i * NU + v + 1)
                        if v >= 1:
                            pe.wait_ge(s["norm"], ONE + i * NU + v)
                        for c in range(4):
                            cols = slice((4 * hq + c) * HD, (4 * hq + c) * HD + HD)
                            if t > 0:
                                mm(Z[:, 2, c * HD:c * HD + HD], PT[:, v % 2, c * 256:c * 256 + P], V[:, t - 1, cols],
                                   start=True, stop=False)
                            ins = mm(Z[:, 2, c * HD:c * HD + HD], PT[:, v % 2, c * 256 + P:c * 256 + 256], V[:, t, cols],
                                     start=t == 0, stop=True)
                        ins.then_inc(s["O"], 1)
                pe.wait_ge(s["norm"], ONE + i * NU + NU)
                for g in range(2):
                    tiles = range(4 * g, 4 * g + 4)
                    if g:
                        pe.wait_ge(s["Fev"], ONE + i * TPB + 4)
                    for t in tiles:
                        q = t % 4
                        if g:
                            pe.wait_ge(s["stat"], ONE + i * 5 * TPB + 5 * 3 + 1)
                        for h in range(LH):
                            rows = slice(32 * (h % 4), 32 * (h % 4) + HD)
                            at = (2 * q + h // 4) * NL
                            ins = mm(R[:, h % 4, at:at + NL], GQT[rows, h // 4, t * P:t * P + P],
                                     GKT[rows, h // 4, :], start=True, stop=True)
                        ins.then_inc(s["lS"], 1)
                    for t in tiles:
                        q, n = t % 4, i * TPB + t + 1
                        pe.wait_ge(s["lexp"], ONE + n)
                        for a in range(LH // 2):
                            ins = nc.tensor.transpose(Z[:, q, a * P:a * P + P],
                                                      sl[:, q, 2 * a:2 * a + 2, :].rearrange("p h n -> p (h n)"),
                                                      G.ident[:, :])
                        ins.then_inc(s["B"], 1)
                    for t in tiles:
                        q, n = t % 4, i * TPB + t + 1
                        pe.wait_ge(s["Bev"], ONE + n)
                        pe.wait_ge(s["lmasked"], ONE + i * TPB + 4 * g + 4)
                        for a in range(LH // 2):
                            ins = mm(R[:, q, a * 32:a * 32 + 32], slT[:, q, a * P:a * P + P], GV[:, a, :],
                                     start=True, stop=True)
                        ins.then_inc(s["C"], 1)
                    for t in tiles:
                        q, n = t % 4, i * TPB + t + 1
                        pe.wait_ge(s["rem"], ONE + n)
                        nc.tensor.transpose(Z[:, q, 0:P], rem[:, q, :], G.ident[:, :]).then_inc(s["Dt"], 1)
                    for t in tiles:
                        q, n = t % 4, i * TPB + t + 1
                        pe.wait_ge(s["Dev"], ONE + n)
                        mm(R[:, q, 0:D], remT[:, q, :], wr[:, :], start=True, stop=True).then_inc(s["E"], 1)
                    for t in tiles:
                        q, n = t % 4, i * TPB + t + 1
                        pe.wait_ge(s["o"], ONE + n)
                        for k in range(KD):
                            ins = nc.tensor.transpose(Z[:, q, k * P:k * P + P], o[:, q, k * P:k * P + P], G.ident[:, :])
                        ins.then_inc(s["F"], 1)
                    for t in tiles:
                        q, n = t % 4, i * TPB + t + 1
                        pe.wait_ge(s["Fev"], ONE + n)
                        for k in range(KD):
                            ins = mm(R[:, q, 0:D], oT[:, q, k * P:k * P + P], wo[:, k, :],
                                     start=k == 0, stop=k == KD - 1)
                        ins.then_inc(s["out"], 1)


def bit_phase(nc, G, A, r, out=None):
    rstd_phase(nc, G, f"b{r}n", 1e-5)
    QB, CLIP = 128.0, float(np.float32(128.0 - 1e-5))
    with ExitStack() as ctx:
        sb = lambda n, sh, d=F32: ctx.enter_context(nc.sbuf_tensor(f"b{r}_{n}", sh, d))
        ps = lambda n, sh: ctx.enter_context(nc.psum_tensor(f"b{r}_{n}", sh, F32))
        w = sb("w", [P, KD, D])
        wt = sb("wt", [P, KD, D])
        wq = sb("wq", [P, KD, D], F16)
        gm = sb("gm", [P, D])
        bt = sb("bt", [P, D])
        wsum = sb("wsum", [P, 1])
        wall = sb("wall", [P, 1])
        thr = sb("thr", [P, 2])
        scl = sb("scl", [P, NT])
        tmp = sb("tmp", [P, NT])
        tmax = sb("tmax", [P, NT])
        pmax = sb("pmax", [P, 1])
        gall = sb("gall", [P, 1])
        gi = sb("gi", [P, 1])
        osc = sb("osc", [P, 1])
        eps3 = sb("eps3", [P, 1])
        xn = sb("xn", [P, NT, D])
        xq = sb("xq", [P, CT, D])
        xhi = sb("xhi", [P, KD, CW], F16)
        xlo = sb("xlo", [P, KD, CW], F16)
        y = sb("y", [P, CT, D])
        st = sb("st", [P, STW])
        psT = ps("psT", [P, KD, 512])
        psY = ps("psY", [P, CT, 512])
        s = sems(nc, ctx, f"bit{r}", "w_in gb_in wsum wall prep var sd max1 gmax gdve xq xT xhi xlo Y out")
        block = ctx.enter_context(nc.Block())
        OUT_PER = 5

        @block.sync
        def _(sp):
            arm(sp, s)
            sp.dma_start(w[:, :, :], A["weight"].rearrange("(k p) d -> p k d", p=P)).then_inc(s["w_in"], 16)
            sp.dma_start(gm[:, :], A["gamma"].partition_broadcast(P)).then_inc(s["gb_in"], 16)
            sp.dma_start(bt[:, :], A["beta"].partition_broadcast(P)).then_inc(s["gb_in"], 16)
            sp.wait_ge(s["gb_in"], ONE + 32)

        @block.gpsimd
        def _(pool):
            pool.wait_ge(s["wsum"], ONE + 1)
            nc.gpsimd.partition_all_reduce(wall[:, :], wsum[:, :], P, bass.bass_isa.ReduceOp.add).then_inc(s["wall"], 1)
            pool.wait_ge(s["max1"], ONE + 1)
            nc.gpsimd.partition_all_reduce(gall[:, :], pmax[:, :], P, bass.bass_isa.ReduceOp.max).then_inc(s["gmax"], 1)

        @block.scalar
        def _(act):
            act.wait_ge(s["var"], ONE + 1)
            nc.scalar.activation(scl[:, :], tmp[:, :], ACT.Sqrt, bias=eps3[:, :]).then_inc(s["sd"], 1)
            with act.Fori(0, NC) as i:
                for k in range(KD):
                    act.wait_ge(s["xT"], ONE + i * KD + k + 1)
                    nc.scalar.activation(xhi[:, k, :], psT[:, k, :], ACT.Copy).then_inc(s["xhi"], 1)

        @block.vector
        def _(dve):
            c = Count(s["prep"])

            def do(ins):
                step(dve, ins, c)
            dve.wait_ge(s["w_in"], ONE + 16)
            step(dve, nc.vector.tensor_reduce(wsum[:, :], w[:, :, :], AX.XY, ALU.add, apply_absolute_value=True),
                 Count(s["wsum"]))
            do(nc.vector.memset(eps3[:, :], 1e-3))
            do(nc.vector.tensor_tensor(tmp[:, :], G.rstd[:, :], G.rstd[:, :], ALU.mult))
            step(dve, nc.vector.tensor_tensor(tmp[:, :], tmp[:, :], G.mv[:, :, 1], ALU.mult), Count(s["var"]))
            dve.wait_ge(s["wall"], ONE + 1)
            do(nc.vector.tensor_scalar(wall[:, :], wall[:, :], 1.0 / (D * D), None, ALU.mult))
            do(nc.vector.tensor_scalar(thr[:, 0:1], wall[:, :], 1e-5, 0.5, ALU.add, ALU.mult))
            do(nc.vector.tensor_scalar(thr[:, 1:2], thr[:, 0:1], -1.0, None, ALU.mult))
            do(nc.vector.tensor_scalar(wt[:, :, :], w[:, :, :], thr[:, 1:2], None, ALU.is_lt))
            do(nc.vector.scalar_tensor_tensor(wq[:, :, :], w[:, :, :], thr[:, 0:1], wt[:, :, :], ALU.is_gt, ALU.subtract))
            dve.wait_ge(s["sd"], ONE + 1)
            do(nc.vector.reciprocal(scl[:, :], scl[:, :]))
            do(nc.vector.tensor_tensor(scl[:, :], scl[:, :], G.rstd[:, :], ALU.mult))
            dve.wait_ge(s["gb_in"], ONE + 32)
            base = c.k
            with dve.Fori(0, NT) as t:
                cl = Count(s["prep"], base, t, 4)
                row = xn[:, t, :]
                step(dve, nc.vector.tensor_scalar(row, G.x[:, t, :], G.mv[:, t, 0:1], scl[:, bass.ds(t, 1)],
                                                  ALU.subtract, ALU.mult), cl)
                step(dve, nc.vector.tensor_tensor(row, row, gm[:, :], ALU.mult), cl)
                step(dve, nc.vector.tensor_tensor(row, row, bt[:, :], ALU.add), cl)
                step(dve, nc.vector.tensor_reduce(tmax[:, bass.ds(t, 1)], row, AX.X, ALU.max,
                                                  apply_absolute_value=True), cl)
            step(dve, nc.vector.tensor_reduce(pmax[:, :], tmax[:, :], AX.X, ALU.max), Count(s["max1"]))
            dve.wait_ge(s["gmax"], ONE + 1)
            g = Count(s["gdve"])
            step(dve, nc.vector.reciprocal(gi[:, :], gall[:, :]), g)
            step(dve, nc.vector.tensor_scalar(gi[:, :], gi[:, :], QB, None, ALU.mult), g)
            step(dve, nc.vector.tensor_tensor(osc[:, :], gall[:, :], wall[:, :], ALU.mult), g)
            step(dve, nc.vector.tensor_scalar(osc[:, :], osc[:, :], 0.5 / QB, None, ALU.mult), g)
            with dve.Fori(0, NC) as i:
                cl = Count(s["xq"], 0, i, 2)
                dve.wait_ge(s["xT"], ONE + i * KD)
                step(dve, nc.vector.tensor_scalar(xq[:, :, :], xn[:, bass.ds(i * CT, CT), :], gi[:, :], CLIP,
                                                  ALU.mult, ALU.min), cl)
                step(dve, nc.vector.tensor_scalar(xq[:, :, :], xq[:, :, :], -CLIP, None, ALU.max), cl)
                dve.wait_ge(s["Y"], ONE + i)
                for k in range(KD):
                    dve.wait_ge(s["xhi"], ONE + i * KD + k + 1)
                    nc.vector.tensor_tensor(xlo[:, k, :], psT[:, k, :], xhi[:, k, :], ALU.subtract).then_inc(s["xlo"], 1)
                dve.wait_ge(s["Y"], ONE + i + 1)
                co = Count(s["out"], 0, i, OUT_PER)
                rows = G.x[:, bass.ds(i * CT, CT), :]
                step(dve, nc.vector.scalar_tensor_tensor(y[:, :, :], psY[:, :, 0:D], osc[:, :], rows, ALU.mult, ALU.add), co)
                step(dve, nc.vector.tensor_scalar(rows, y[:, :, :], 1.0, None, ALU.mult), co)
                token_stats(nc, dve, y, st, G.mv[:, bass.ds(i * CT, CT), :], CT, co)
                assert co.k == OUT_PER

        @block.tensor
        def _(pe):
            with pe.Fori(0, NC) as i:
                pe.wait_ge(s["xq"], ONE + i * 2 + 2)
                pe.wait_ge(s["xlo"], ONE + i * KD)
                for k in range(KD):
                    for t in range(CT):
                        last = nc.tensor.transpose(psT[:, k, t * P:t * P + P], xq[:, t, k * P:k * P + P],
                                                   G.ident[:, :])
                    last.then_inc(s["xT"], 1)
                pe.wait_ge(s["xlo"], ONE + i * KD + KD)
                pe.wait_ge(s["out"], ONE + i * OUT_PER)
                for t in range(CT):
                    for k in range(KD):
                        for part, x in enumerate((xhi, xlo)):
                            last = nc.tensor.matmul(psY[:, t, 0:D], x[:, k, t * P:t * P + P], wq[:, k, :],
                                                    start=(k + part == 0), stop=(k == KD - 1 and part == 1))
                last.then_inc(s["Y"], 1)


NM = 63
HALF = NM // 2
BW = 96
GW = 192
KPAD = B * S + 64
YW = 128
KQ = 70
PADW = 32 + S + 32


def rel_phase(nc, G, A):
    rstd_phase(nc, G, "a1n", 1e-5)
    with ExitStack() as ctx:
        sb = lambda n, sh, d=F32: ctx.enter_context(nc.sbuf_tensor(f"a1_{n}", sh, d))
        V = sb("V", [P, NT, NH, HD + 1])
        wpT = sb("wpT", [P, KD, D])
        BDv = sb("BDv", [P, NH // 2, 32])
        rvd = sb("rvd", [P, NH, HD])
        rv62 = sb("rv62", [P, NH, HD])
        QKD = nc.dram_tensor("a1_qk", [4, D, B * S], F16, kind="Internal").ap()
        END = nc.dram_tensor("a1_ends", [2, 2, 32, B * S], F16, kind="Internal").ap()
        GD = nc.dram_tensor("a1_bias", [B * S, NH, BW], F32, kind="Internal").ap()
        PW = nc.dram_tensor("a1_band", [B * S, NH, GW], F32, kind="Internal").ap()
        with ExitStack() as parts:
            psb = lambda n, sh, d=F32: parts.enter_context(nc.sbuf_tensor(f"a1_{n}", sh, d))
            QH = psb("QH", [P, KD, B * S], F16)
            QL = psb("QL", [P, KD, B * S], F16)
            KH = psb("KH", [P, KD, KPAD], F16)
            KL = psb("KL", [P, KD, KPAD], F16)
            tabs = [psb(n, [P, KD, 8, YW], F16) for n in ("TQH", "TQL", "TKH", "TKL")]
            rel_project(nc, G, A, V, wpT, BDv, rvd, rv62, QH, QL, KH, KL, tabs, QKD, END)
            rel_bias(nc, QH, QL, KH, KL, tabs, GD)
        rel_attend(nc, G, A, V, wpT, BDv, rvd, rv62, QKD, END, GD, PW)


def rel_project(nc, G, A, V, wpT, BDv, rvd, rv62, QH, QL, KH, KL, tabs, QKD, END):
    with ExitStack() as ctx:
        sb = lambda n, sh, d=F32: ctx.enter_context(nc.sbuf_tensor(f"a1p_{n}", sh, d))
        ps = lambda n, sh: ctx.enter_context(nc.psum_tensor(f"a1p_{n}", sh, F32))
        wn = sb("wn", [P, 6, D])
        wpn = sb("wpn", [P, KD, D])
        wT = sb("wT", [P, KD, 3 * D])
        rqk = sb("rqk", [P, 2, KD, NM])
        blk = sb("blk", [P, 8])
        dev = sb("dev", [P, 2, KD, YW])
        full = sb("full", [P, 8, YW])
        BDu = sb("BDu", [P, 2, KD, 2, NH])
        vend = sb("vend", [P, NH // 2, 32])
        xn = sb("xn", [P, CT, D])
        xT = sb("xT", [P, KD, CW])
        qf = sb("qf", [P, 4, CW])
        ehl = sb("ehl", [32, 2, 2, CW], F16)
        psT = ps("psT", [P, 2, 512])
        psQ = ps("psQ", [P, 4, 512])
        psE = ps("psE", [P, 2, 512])
        s = sems(nc, ctx, "a1p", "w_in tab_in rv_in zero const tab wtr wev fullsem xn xT xTev Q Qf Qhi Qlo V Vev E Ehi Elo e_out q_out")
        block = ctx.enter_context(nc.Block())

        @block.sync
        def _(sp):
            arm(sp, s)
            with nc.allow_non_contiguous_dma("tables, once"):
                sp.dma_start(wn[:, :, :], A["w_qkv"].rearrange("(n p) k -> p n k", p=P)).then_inc(s["w_in"], 16)
                sp.dma_start(wpn[:, :, :], A["w_proj"].rearrange("(n p) k -> p n k", p=P)).then_inc(s["w_in"], 16)
                for n, src in enumerate(("rk", "rq")):
                    sp.dma_start(rqk[:, n, :, :], A[src].rearrange("(k h) d m -> (h d) k m", k=KD)).then_inc(s["tab_in"], 16)
                sp.wait_ge(s["zero"], ONE + 1)
                for a in range(2):
                    sp.dma_start(BDv[64 * a:64 * a + NM, :, HD * a:HD * a + HD],
                                 A["rv"].rearrange("(q a) m d -> m a q d", a=2)[:, a, :, :]).then_inc(s["rv_in"], 16)
                    for e in range(2):
                        rows = 32 - e
                        sp.dma_start(vend[64 * a + 32 * e:64 * a + 32 * e + rows, :, HD * a:HD * a + HD],
                                     A["rv"].rearrange("(q a) m d -> m a q d", a=2)[e * (NM - 1), a, :, :].partition_broadcast(rows)
                                     ).then_inc(s["rv_in"], 16)
                sp.dma_start(rvd[:, :, :], A["rv"][:, 0, :].partition_broadcast(P)).then_inc(s["rv_in"], 16)
                sp.dma_start(rv62[:, :, :], A["rv"][:, NM - 1, :].partition_broadcast(P)).then_inc(s["rv_in"], 16)
            with sp.Fori(0, B) as b:
                for half in range(2):
                    sp.wait_ge(s["Elo"], ONE + b * 4 + half * 2 + 2)
                    for n in range(2):
                        sp.dma_start(END[n, :, :, bass.ds(b * S + half * CW, CW)].rearrange("l e t -> e l t"),
                                     ehl[:, n, :, :]).then_inc(s["e_out"], 16)
            sp.wait_ge(s["Qlo"], ONE + 4 * NC)
            for n, src in enumerate((QH, QL)):
                sp.dma_start(QKD[n, :, :].rearrange("(k p) t -> p k t", p=P), src[:, :, :]).then_inc(s["q_out"], 16)
            for n, src in enumerate((KH, KL)):
                sp.dma_start(QKD[2 + n, :, :].rearrange("(k p) t -> p k t", p=P),
                             src[:, :, 32:32 + B * S]).then_inc(s["q_out"], 16)
            sp.wait_ge(s["q_out"], ONE + 16 * 4)
            sp.wait_ge(s["e_out"], ONE + 16 * 2 * NC)

        @block.gpsimd
        def _(pool):
            nc.gpsimd.memset(vend[:, :, :], 0.0)
            nc.gpsimd.memset(BDv[:, :, :], 0.0).then_inc(s["zero"], 1)
            nc.gpsimd.memset(KH[:, :, :], 0.0)
            nc.gpsimd.memset(KL[:, :, :], 0.0)
            nc.gpsimd.memset(dev[:, :, :, :], 0.0)
            nc.gpsimd.memset(BDu[:, :, :, :, :], 0.0)
            nc.gpsimd.memset(V[:, :, :, :], 1.0)
            c = Count(s["const"])
            step(pool, nc.gpsimd.memset(blk[:, :], 1.0), c)
            step(pool, nc.gpsimd.affine_select(out=blk[:, :], in_=blk[:, :], compare_op=ALU.is_ge, fill=0.0, base=0,
                                               pattern=[[-HD, 8]], channel_multiplier=1), c)
            step(pool, nc.gpsimd.affine_select(out=blk[:, :], in_=blk[:, :], compare_op=ALU.is_ge, fill=0.0,
                                               base=HD - 1, pattern=[[HD, 8]], channel_multiplier=-1), c)

        @block.scalar
        def _(act):
            with act.Fori(0, B) as b:
                for half in range(2):
                    n = b * 2 + half
                    for k in range(KD):
                        act.wait_ge(s["xT"], ONE + n * KD + k + 1)
                        nc.scalar.activation(xT[:, k, :], psT[:, k, :], ACT.Copy).then_inc(s["xTev"], 1)
                    for m in range(4):
                        act.wait_ge(s["Q"], ONE + n * 4 + m + 1)
                        act.wait_ge(s["E"], ONE + n * 2)
                        nc.scalar.activation(qf[:, m, :], psQ[:, m, :], ACT.Copy,
                                             scale=0.25 if m < 2 else 1.0).then_inc(s["Qf"], 1)
                    for t in range(CT):
                        act.wait_ge(s["V"], ONE + n * CT + t + 1)
                        nc.scalar.activation(V[:, n * CT + t, :, 0:HD],
                                             psQ[:, t, 0:D].rearrange("p (h d) -> p h d", h=NH),
                                             ACT.Copy).then_inc(s["Vev"], 1)

        @block.vector
        def _(dve):
            c = Count(s["tab"])

            def do(ins):
                step(dve, ins, c)
            dve.wait_ge(s["const"], ONE + 3)
            dve.wait_ge(s["tab_in"], ONE + 32)
            do(nc.vector.tensor_scalar(rqk[:, 1, :, :], rqk[:, 1, :, :], 0.25, None, ALU.mult))
            for n in range(2):
                lowend, highend, split = (0, NM - 1, HALF + 1) if n == 0 else (0, NM - 1, HALF)
                for k in range(KD):
                    t = rqk[:, n, k, :]
                    do(nc.vector.tensor_scalar(dev[:, n, k, 32:32 + split], t[:, 0:split], t[:, lowend:lowend + 1], None,
                                               ALU.subtract))
                    do(nc.vector.tensor_scalar(dev[:, n, k, 32 + split:32 + NM], t[:, split:NM],
                                               t[:, highend:highend + 1], None, ALU.subtract))
                    do(nc.vector.tensor_tensor(full[:, :, :], dev[:, n, k, :].unsqueeze(1).to_broadcast([P, 8, YW]),
                                               blk[:, :].unsqueeze(2).to_broadcast([P, 8, YW]), ALU.mult))
                    do(nc.vector.tensor_copy(tabs[2 * n][:, k, :, :], full[:, :, :]))
                    do(nc.vector.tensor_tensor(tabs[2 * n + 1][:, k, :, :], full[:, :, :], tabs[2 * n][:, k, :, :],
                                               ALU.subtract))
                    for e in range(2):
                        col = (0 if e == 0 else NM - 1) if n == 0 else (NM - 1 if e == 0 else 0)
                        do(nc.vector.tensor_scalar(BDu[:, n, k, e, 8 * k:8 * k + 8], blk[:, :], t[:, col:col + 1], None,
                                                   ALU.mult))
            for g in range(4):
                dve.wait_ge(s["wtr"], ONE + g + 1)
                dst = wT[:, :, g * D:g * D + D] if g < 3 else wpT[:, :, :]
                nc.vector.tensor_copy(dst.rearrange("p k (n c) -> p n k c", n=2),
                                      psQ[:, g, :].rearrange("p (n k c) -> p n k c", n=2, k=2)).then_inc(s["wev"], 1)
            dve.wait_ge(s["rv_in"], ONE + 16 * 8)
            do(nc.vector.tensor_tensor(BDv[:, :, :], BDv[:, :, :], vend[:, :, :], ALU.subtract))
            do(nc.vector.tensor_tensor(rvd[:, :, :], rvd[:, :, :], rv62[:, :, :], ALU.subtract))
            with dve.Fori(0, B) as b:
                for half in range(2):
                    n = b * 2 + half
                    dve.wait_ge(s["xT"], ONE + n * KD)
                    for t in range(CT):
                        nc.vector.tensor_scalar(xn[:, t, :], G.x[:, n * CT + t, :], G.mv[:, n * CT + t, 0:1],
                                                G.rstd[:, bass.ds(n * CT + t, 1)], ALU.subtract,
                                                ALU.mult).then_inc(s["xn"], 1)
                    for m in range(4):
                        dve.wait_ge(s["Qf"], ONE + n * 4 + m + 1)
                        if m < 2:
                            hi, lo = (a[:, m, bass.ds(n * CW, CW)] for a in (QH, QL))
                        else:
                            hi, lo = (a[:, m - 2, bass.ds(n * CW + 32, CW)] for a in (KH, KL))
                        ins = nc.vector.tensor_scalar(hi, qf[:, m, :], 1.0, None, ALU.mult)
                        ins.then_inc(s["Qhi"], 1)
                        dve.wait_ge(s["Qhi"], ONE + n * 4 + m + 1)
                        nc.vector.tensor_tensor(lo, qf[:, m, :], hi, ALU.subtract).then_inc(s["Qlo"], 1)
                    for m in range(2):
                        dve.wait_ge(s["E"], ONE + n * 2 + m + 1)
                        dve.wait_ge(s["e_out"], ONE + n * 32)
                        nc.vector.tensor_copy(ehl[:, m, 0, :], psE[0:32, m, :]).then_inc(s["Ehi"], 1)
                        dve.wait_ge(s["Ehi"], ONE + n * 2 + m + 1)
                        nc.vector.tensor_tensor(ehl[:, m, 1, :], psE[0:32, m, :], ehl[:, m, 0, :],
                                                ALU.subtract).then_inc(s["Elo"], 1)

        @block.tensor
        def _(pe):
            mm = nc.tensor.matmul
            pe.wait_ge(s["w_in"], ONE + 32)
            for g in range(4):
                for n in range(2):
                    for k in range(KD):
                        src = wn[:, 2 * g + n, k * P:k * P + P] if g < 3 else wpn[:, n, k * P:k * P + P]
                        ins = nc.tensor.transpose(psQ[:, g, (2 * n + k) * P:(2 * n + k) * P + P], src, G.ident[:, :])
                ins.then_inc(s["wtr"], 1)
            pe.wait_ge(s["wev"], ONE + 4)
            pe.wait_ge(s["tab"], ONE + 31)
            with pe.Fori(0, B) as b:
                for half in range(2):
                    n = b * 2 + half
                    pe.wait_ge(s["xn"], ONE + n * CT + CT)
                    pe.wait_ge(s["xTev"], ONE + n * KD)
                    for k in range(KD):
                        for t in range(CT):
                            ins = nc.tensor.transpose(psT[:, k, t * P:t * P + P], xn[:, t, k * P:k * P + P], G.ident[:, :])
                        ins.then_inc(s["xT"], 1)
                    pe.wait_ge(s["xTev"], ONE + n * KD + KD)
                    pe.wait_ge(s["Vev"], ONE + n * CT)
                    for m in range(4):
                        for k in range(KD):
                            ins = mm(psQ[:, m, :], wT[:, k, m * P:m * P + P], xT[:, k, :], start=k == 0, stop=k == KD - 1)
                        ins.then_inc(s["Q"], 1)
                    for t in range(CT):
                        pe.wait_ge(s["Qf"], ONE + n * 4 + t + 1)
                        for k in range(KD):
                            ins = mm(psQ[:, t, 0:D], xT[:, k, t * P:t * P + P], wT[:, k, 2 * D:3 * D],
                                     start=k == 0, stop=k == KD - 1)
                        ins.then_inc(s["V"], 1)
                    pe.wait_ge(s["Elo"], ONE + n * 2)
                    for m in range(2):
                        for k in range(KD):
                            ins = mm(psE[0:32, m, :], BDu[:, m, k, :, :].rearrange("p e h -> p (e h)"), qf[:, 2 * m + k, :],
                                     start=k == 0, stop=k == KD - 1)
                        ins.then_inc(s["E"], 1)


def rel_bias(nc, QH, QL, KH, KL, tabs, GD):
    with ExitStack() as ctx:
        Gt = ctx.enter_context(nc.sbuf_tensor("a1b_G", [P, 2, 32, 2, BW], F32))
        pq = ctx.enter_context(nc.psum_tensor("a1b_q", [P, 4, 512], F32))
        pk = ctx.enter_context(nc.psum_tensor("a1b_k", [P, 4, 512], F32))
        s = sems(nc, ctx, "a1b", "q qev k kev out0 out1")
        block = ctx.enter_context(nc.Block())
        TQH, TQL, TKH, TKL = tabs
        QB_, KB_ = 16, 12

        @block.sync
        def _(sp):
            arm(sp, s)
            with sp.Fori(0, KD) as m:
                for pair in range(4):
                    sp.wait_ge(s["kev"], ONE + (m * 4 + pair + 1) * KB_)
                    sp.dma_start(GD[:, bass.ds(8 * m + 2 * pair, 2), :].rearrange("(p r) h x -> p r (h x)", r=32),
                                 Gt[:, pair % 2, :, :, :].rearrange("p r h x -> p r (h x)")).then_inc(s[f"out{pair % 2}"], 16)
            for n in range(2):
                sp.wait_ge(s[f"out{n}"], ONE + 16 * 4)

        @block.scalar
        def _(act):
            with act.Fori(0, KD) as m:
                for pair in range(4):
                    n = m * 4 + pair
                    for r in range(QB_):
                        act.wait_ge(s[f"out{pair % 2}"], ONE + 16 * (m * 2 + pair // 2))
                        act.wait_ge(s["q"], ONE + n * QB_ + r + 1)
                        nc.scalar.activation(Gt[:, pair % 2, 2 * r:2 * r + 2, :, :].rearrange("p r h x -> p (r h x)"),
                                             pq[:, r % 4, 0:4 * BW], ACT.Copy).then_inc(s["qev"], 1)

        @block.vector
        def _(dve):
            with dve.Fori(0, KD) as m:
                for pair in range(4):
                    n = m * 4 + pair
                    for x in range(KB_):
                        dve.wait_ge(s["k"], ONE + n * KB_ + x + 1)
                        dve.wait_ge(s["qev"], ONE + (n + 1) * QB_)
                        for h in range(2):
                            g = Gt[:, pair % 2, :, h, 8 * x:8 * x + 8]
                            ins = nc.vector.tensor_tensor(
                                g, pk[:, x % 4, :].rearrange("p (x h r) -> p h r x", x=8, h=2)[:, h, :, :], g, ALU.add)
                        ins.then_inc(s["kev"], 1)

        @block.tensor
        def _(pe):
            mm = nc.tensor.matmul
            with pe.Fori(0, KD) as m:
                for pair in range(4):
                    n = m * 4 + pair
                    hs = slice(2 * pair, 2 * pair + 2)
                    for r in range(QB_):
                        if r < 4:
                            pe.wait_ge(s["qev"], ONE + n * QB_)
                        else:
                            pe.wait_ge(s["qev"], ONE + n * QB_ + r - 3)
                        for e in range(2):
                            tok = 2 * r + e
                            for p, (a, w) in enumerate(((QH, TQH), (QL, TQH), (QH, TQL))):
                                ins = mm(pq[:, r % 4, 2 * BW * e:2 * BW * e + 2 * BW],
                                         a[:, bass.ds(m, 1), tok:tok + 32 * (P - 1) + 1:32].rearrange("p k t -> p (k t)"),
                                         w[:, bass.ds(m, 1), hs, 31 - tok:31 - tok + BW].rearrange("p k h x -> p (k h) x"),
                                         start=p == 0, stop=p == 2)
                        ins.then_inc(s["q"], 1)
                    for x in range(KB_):
                        if x < 4:
                            pe.wait_ge(s["kev"], ONE + n * KB_)
                        else:
                            pe.wait_ge(s["kev"], ONE + n * KB_ + x - 3)
                        for e in range(8):
                            key = 8 * x + e
                            for p, (a, w) in enumerate(((KH, TKH), (KL, TKH), (KH, TKL))):
                                ins = mm(pk[:, x % 4, 64 * e:64 * e + 64],
                                         a[:, bass.ds(m, 1), key:key + 32 * (P - 1) + 1:32].rearrange("p k t -> p (k t)"),
                                         w[:, bass.ds(m, 1), hs, BW - 1 - key:BW - 1 - key + 32].rearrange("p k h x -> p (k h) x"),
                                         start=p == 0, stop=p == 2)
                        ins.then_inc(s["k"], 1)


def skewed(PW, I):
    pitch = NH * GW
    return bass.AP(PW.tensor, I * P * pitch + 1, [[S * pitch, B], [pitch + 1, P], [GW, NH], [1, 64]])


def rel_attend(nc, G, A, V, wpT, BDv, rvd, rv62, QKD, END, GD, PW):
    with ExitStack() as ctx:
        sb = lambda n, sh, d=F32: ctx.enter_context(nc.sbuf_tensor(f"a1c_{n}", sh, d))
        ps = lambda n, sh: ctx.enter_context(nc.psum_tensor(f"a1c_{n}", sh, F32))
        Qs = sb("Qs", [KQ, 2, S], F16)
        KLt = sb("KLt", [KQ, 2, S], F16)
        KRt = sb("KRt", [KQ, 2, S], F16)
        Gw = sb("Gw", [P, 2, TPB, GW])
        upper = sb("upper", [P, P], mybir.dt.int32)
        upf = sb("upf", [P, P])
        lowf = sb("lowf", [P, P])
        spare = sb("spare", [P, 1])
        mx = sb("mx", [P, 2])
        nb = sb("nb", [P, 2])
        Pb = sb("Pb", [P, 4, PADW])
        PT = sb("PT", [P, 2, TPB, P])
        junk = sb("junk", [P, P])
        rsl = sb("rsl", [P, 16])
        sdl = sb("sdl", [P, 16])
        RS = sb("RS", [P, TPB, NH])
        SD = sb("SD", [P, TPB, NH])
        XO = sb("XO", [P, TPB, NH, HD + 1])
        Dt = sb("Dt", [P, TPB, NH, 64])
        DT = sb("DT", [P, NH // 2, P])
        t1 = sb("t1", [P, NH, HD])
        t2 = sb("t2", [P, NH, HD])
        s0 = sb("s0", [P, NH])
        xoT = sb("xoT", [P, D])
        bp = sb("bp", [P, D])
        row = sb("row", [P, 1, D])
        st = sb("st", [P, STW])
        SP = ps("S", [P, 2, S])
        DG = ps("DG", [P, 512])
        TP = ps("T", [P, 2, 512])
        OP = ps("O", [P, 512])
        s = sems(nc, ctx, "a1c", "const qin0 qin1 gin0 gin1 bp_in S sel bias max shift exp pw0 pw1 pw2 pw3 T Ta Td O Od diag coll "
                 "din Dtr Da Dd Dm comb Xtr Xev proj fin xz spare")
        block = ctx.enter_context(nc.Block())
        TURNS = B * NH // 2
        NS = 2 * TPB
        STEPS = [(hh, I) for hh in range(2) for I in range(TPB)]
        QIN, GIN = 16 * 16, 16 * 4
        TPT = NH // 2

        @block.sync
        def _(sp):
            arm(sp, s)
            sp.dma_start(bp[:, :], A["b_proj"].partition_broadcast(P)).then_inc(s["bp_in"], 16)
            sp.wait_ge(s["const"], ONE + 1)

            with sp.Fori(0, B) as b:
                with sp.Fori(0, TPT) as hp:
                    turn = b * TPT + hp
                    for hh in range(2):
                        h, toks = hp * 2 + hh, bass.ds(b * S, S)
                        rows = bass.ds(h * HD, HD)
                        inc = s[f"qin{hh}"]
                        sp.wait_ge(s["S"], ONE + turn * NS - TPB * (1 - hh))
                        for d in range(2):
                            for p in range(2):
                                at = 32 * d + 16 * p
                                sp.dma_start(Qs[at:at + HD, hh, :], QKD[p, rows, toks]).then_inc(inc, 16)
                                for K in (KLt, KRt):
                                    sp.dma_start(K[at:at + HD, hh, :], QKD[2 + d, rows, toks]).then_inc(inc, 16)
                        for e, K in enumerate((KLt, KRt)):
                            end = bass.ds(h + NH * e, 1)
                            sp.dma_start(Qs[64 + 2 * e:66 + 2 * e, hh, :],
                                         END[0, :, end, toks].rearrange("l e t -> (l e) t")).then_inc(inc, 16)
                            sp.dma_start(K[68:70, hh, :],
                                         END[1, :, end, toks].rearrange("l e t -> (l e) t")).then_inc(inc, 16)
                        sp.wait_ge(s["bias"], ONE + turn * NS - TPB * (1 - hh))
                        for g in range(4):
                            src = GD[toks, bass.ds(h, 1), :].rearrange("(i g r) h x -> g r i (h x)", g=4, r=32)
                            sp.dma_start(Gw[32 * g:32 * g + 32, hh, :, 32 * g:32 * g + BW],
                                         src[g]).then_inc(s[f"gin{hh}"], 16)
            sp.wait_ge(s["bp_in"], ONE + 16)

        @block.gpsimd
        def _(pool):
            c = Count(s["spare"])
            for t in (Qs, KLt, KRt):
                nc.gpsimd.memset(t[:, :, :], 1.0)
            nc.gpsimd.memset(Pb[:, :, 0:32], 0.0)
            nc.gpsimd.memset(Pb[:, :, 32 + S:PADW], 0.0)
            nc.gpsimd.memset(Gw[:, :, :, :], 0.0)
            nc.gpsimd.memset(XO[:, :, :, :], 0.0)
            step(pool, nc.gpsimd.memset(upf[:, :], 1.0), c)
            step(pool, nc.gpsimd.affine_select(out=KLt[:, :, :], in_=KLt[:, :, :], compare_op=ALU.is_ge, fill=0.0,
                                               base=65, pattern=[[0, 2], [0, S]], channel_multiplier=-1), c)
            step(pool, nc.gpsimd.affine_select(out=KRt[:, :, :], in_=KRt[:, :, :], compare_op=ALU.is_ge, fill=0.0,
                                               base=-66, pattern=[[0, 2], [0, S]], channel_multiplier=1), c)
            nc.gpsimd.affine_select(out=upf[:, :], in_=upf[:, :], compare_op=ALU.is_gt, fill=0.0, base=0,
                                    pattern=[[1, P]], channel_multiplier=-1).then_inc(s["const"], 1)

        @block.scalar
        def _(act):
            with act.Fori(0, B) as b:
                with act.Fori(0, TPT) as hp:
                    T = b * TPT + hp
                    for k in range(NS + 1):
                        if k < NS:
                            hh, I = STEPS[k]
                            n = T * NS + k
                            act.wait_ge(s["shift"], ONE + n + 1)
                            act.wait_ge(s["T"], ONE + (n - 3) * 2)
                            act.wait_ge(s["diag"], ONE + n - 3)
                            act.wait_ge(s[f"pw{k % 4}"], ONE + 16 * (T * 4 + k // 4))
                            if k == 0:
                                act.wait_ge(s["coll"], ONE + T)
                            nc.scalar.activation(Pb[:, k % 4, 32:32 + S], SP[:, k % 2, :], ACT.Exp,
                                                 bias=nb[:, k % 2:k % 2 + 1], accum_out=rsl[:, k:k + 1]).then_inc(s["exp"], 1)
                        if k >= 1:
                            v = T * NS + k - 1
                            act.wait_ge(s["T"], ONE + 2 * v + 1)
                            act.wait_ge(s["O"], ONE + v - 1)
                            nc.scalar.activation(PT[:, (k - 1) % 2, 0:4, :].rearrange("p j q -> p (j q)"), TP[:, 0, :],
                                                 ACT.Copy).then_inc(s["Ta"], 1)
                        if k < NS:
                            act.wait_ge(s["exp"], ONE + n + 1)
                            act.dma_start(PW[bass.ds(b * S + I * P, P), bass.ds(hp * 2 + hh, 1), :],
                                          Pb[:, k % 4, I * P:I * P + GW].unsqueeze(1)).then_inc(s[f"pw{k % 4}"], 16)
                for q in range(4):
                    act.wait_ge(s[f"pw{q}"], ONE + 16 * 4 * TPT * (b + 1))
                for I in range(TPB):
                    act.dma_start(Dt[:, I, :, :], skewed(PW, I)[bass.ds(b, 1)].rearrange(
                        "b p h m -> (b p) h m")).then_inc(s["din"], 16)
                for I in range(TPB):
                    m = b * TPB + I
                    for half in range(2):
                        act.wait_ge(s["Dtr"], ONE + 2 * m + half + 1)
                        if half == 0:
                            act.wait_ge(s["Dm"], ONE + m)
                        nc.scalar.activation(DT[:, 4 * half:4 * half + 4, :].rearrange("p j q -> p (j q)"), TP[:, half, :],
                                             ACT.Copy).then_inc(s["Da"], 1)
                    act.wait_ge(s["Xtr"], ONE + m + 1)
                    nc.scalar.activation(xoT[:, :], DG[:, 0:D], ACT.Copy).then_inc(s["Xev"], 1)

        @block.vector
        def _(dve):
            def do(ins, name, value):
                ins.then_inc(s[name], 1)
                dve.wait_ge(s[name], ONE + value)
            dve.wait_ge(s["const"], ONE + 1)
            nc.vector.tensor_copy(upper[:, :], upf[:, :])
            do(nc.vector.tensor_scalar(lowf[:, :], upf[:, :], -1.0, 1.0, ALU.mult, ALU.add), "xz", 1)
            with dve.Fori(0, B) as b:
                with dve.Fori(0, TPT) as hp:
                    T = b * TPT + hp
                    for k in range(NS + 2):
                        if k < NS:
                            hh, I = STEPS[k]
                            n = T * NS + k
                            p2 = k % 2
                            if I == 0:
                                dve.wait_ge(s[f"gin{hh}"], ONE + GIN * (T + 1))
                            dve.wait_ge(s["S"], ONE + n + 1)
                            nc.vector.memset(spare[:, :], 0.0)
                            do(nc.vector.copy_predicated(SP[:, p2, I * P:I * P + P], upper[:, :], DG[:, 0:P]), "sel", n + 1)
                            w0, w1 = (32 if I == 0 else 0), (160 if I == TPB - 1 else GW)
                            band = SP[:, p2, I * P - 32 + w0:I * P - 32 + w1]
                            do(nc.vector.tensor_tensor(band, band, Gw[:, hh, I, w0:w1], ALU.add), "bias", n + 1)
                            do(nc.vector.tensor_reduce(mx[:, p2:p2 + 1], SP[:, p2, :], AX.X, ALU.max), "max", n + 1)
                            dve.wait_ge(s["exp"], ONE + n - 1)
                            nc.vector.tensor_scalar(nb[:, p2:p2 + 1], mx[:, p2:p2 + 1], -1.0, None,
                                                    ALU.mult).then_inc(s["shift"], 1)
                        if 1 <= k <= NS:
                            v = T * NS + k - 1
                            I = STEPS[k - 1][1]
                            dve.wait_ge(s["exp"], ONE + v + 1)
                            dve.wait_ge(s["diag"], ONE + v)
                            nc.vector.tensor_tensor_reduce(out=junk[:, :], in0=Pb[:, (k - 1) % 4, 32 + I * P:32 + I * P + P],
                                                           in1=lowf[:, :], scale=1.0, scalar=0.0, op0=ALU.mult,
                                                           op1=ALU.add, accum_out=sdl[:, k - 1:k]).then_inc(s["diag"], 1)
                            dve.wait_ge(s["T"], ONE + 2 * v + 2)
                            dve.wait_ge(s["O"], ONE + v - 1)
                            nc.vector.tensor_copy(PT[:, (k - 1) % 2, 4:8, :].rearrange("p j q -> p (j q)"),
                                                  TP[:, 1, :]).then_inc(s["Td"], 1)
                        if k >= 2:
                            v = T * NS + k - 2
                            hh, I = STEPS[k - 2]
                            w = HD + 1 if I else HD
                            dve.wait_ge(s["O"], ONE + v + 1)
                            nc.vector.tensor_scalar(XO[:, I, bass.ds(hp * 2 + hh, 1), 0:w].rearrange("p a w -> p (a w)"),
                                                    OP[:, 0:w], 1.0, None, ALU.mult).then_inc(s["Od"], 1)
                    dve.wait_ge(s["diag"], ONE + T * NS + NS)
                    for hh in range(2):
                        for src, dst in ((rsl, RS), (sdl, SD)):
                            ins = nc.vector.tensor_scalar(dst[:, :, bass.ds(hp * 2 + hh, 1)],
                                                          src[:, hh * TPB:hh * TPB + TPB].unsqueeze(2), 1.0, None, ALU.mult)
                    do(ins, "coll", T + 1)
                dve.wait_ge(s["Od"], ONE + (b + 1) * TPT * NS)
                for I in range(TPB):
                    m = b * TPB + I
                    cf = Count(s["fin"], I * 11, b, TPB * 11)
                    bc = lambda a: a.unsqueeze(2).to_broadcast([P, NH, HD])
                    f = lambda ins: step(dve, ins, cf)
                    f(nc.vector.tensor_tensor(s0[:, :], XO[:, I, :, HD], SD[:, I, :], ALU.add))
                    f(nc.vector.reciprocal(RS[:, I, :], RS[:, I, :]))
                    f(nc.vector.tensor_tensor(t2[:, :, :], rvd[:, :, :], bc(s0[:, :]), ALU.mult))
                    f(nc.vector.tensor_tensor(t2[:, :, :], t2[:, :, :], XO[:, I, :, 0:HD], ALU.add))
                    dve.wait_ge(s["Dm"], ONE + m + 1)
                    f(nc.vector.tensor_tensor(t1[:, :, :], OP[:, 0:D].rearrange("p (h d) -> p h d", h=NH), t2[:, :, :], ALU.add))
                    f(nc.vector.tensor_tensor(t1[:, :, :], t1[:, :, :], bc(RS[:, I, :]), ALU.mult))
                    do(nc.vector.tensor_tensor(t1[:, :, :], t1[:, :, :], rv62[:, :, :], ALU.add), "comb", m + 1)
                    dve.wait_ge(s["proj"], ONE + m + 1)
                    f(nc.vector.tensor_tensor(row[:, 0, :], DG[:, D:2 * D], bp[:, :], ALU.add))
                    xrow = G.x[:, m, :]
                    f(nc.vector.tensor_tensor(row[:, 0, :], row[:, 0, :], xrow, ALU.add))
                    do(nc.vector.tensor_scalar(xrow, row[:, 0, :], 1.0, None, ALU.mult), "xz", 1 + m + 1)
                    token_stats(nc, dve, row, st, G.mv[:, bass.ds(m, 1), :], 1, cf)
                    assert cf.k == (I + 1) * 11, cf.k

        @block.tensor
        def _(pe):
            mm = nc.tensor.matmul
            pe.wait_ge(s["const"], ONE + 1)
            with pe.Fori(0, B) as b:
                with pe.Fori(0, TPT) as hp:
                    T = b * TPT + hp
                    for k in range(NS + 2):
                        if k < NS:
                            hh, I = STEPS[k]
                            n = T * NS + k
                            if I == 0:
                                pe.wait_ge(s[f"qin{hh}"], ONE + QIN * (T + 1))
                            pe.wait_ge(s["exp"], ONE + n - 1)
                            pe.wait_ge(s["sel"], ONE + n)
                            if k == 0:
                                pe.wait_ge(s["fin"], ONE + b * TPB * 11)
                            q = Qs[:, hh, I * P:I * P + P]
                            edge = (I + 1) * P
                            cuts = [(KLt, 0, min(edge, 512)), (KLt, 512, edge), (KRt, edge, 512), (KRt, max(edge, 512), S)]
                            for K, lo, hi in cuts:
                                if lo < hi:
                                    mm(SP[:, k % 2, lo:hi], q, K[:, hh, lo:hi], start=True, stop=True)
                            mm(DG[:, 0:P], q, KRt[:, hh, I * P:I * P + P], start=True, stop=True).then_inc(s["S"], 1)
                        if 1 <= k <= NS:
                            v = T * NS + k - 1
                            pe.wait_ge(s["exp"], ONE + v + 1)
                            for half in range(2):
                                pe.wait_ge(s["Ta"] if half == 0 else s["Td"], ONE + v)
                                for q in range(4):
                                    J = 4 * half + q
                                    ins = nc.tensor.transpose(TP[:, half, q * P:q * P + P],
                                                              Pb[:, (k - 1) % 4, 32 + J * P:32 + J * P + P], G.ident[:, :])
                                ins.then_inc(s["T"], 1)
                        if k >= 2:
                            v = T * NS + k - 2
                            hh, I = STEPS[k - 2]
                            pe.wait_ge(s["Ta"], ONE + v + 1)
                            pe.wait_ge(s["Td"], ONE + v + 1)
                            pe.wait_ge(s["Od"], ONE + v)
                            for J in range(TPB):
                                w = HD + 1 if J < I else HD
                                ins = mm(OP[:, 0:w], PT[:, (k - 2) % 2, J, :],
                                         V[:, bass.ds(b * TPB + J, 1), bass.ds(hp * 2 + hh, 1), 0:w].rearrange(
                                             "p t h w -> p (t h w)"), start=J == 0, stop=J == TPB - 1)
                            ins.then_inc(s["O"], 1)
                pe.wait_ge(s["din"], ONE + 16 * TPB * (b + 1))
                pe.wait_ge(s["Od"], ONE + (b + 1) * TPT * NS)
                for I in range(TPB):
                    m = b * TPB + I
                    for half in range(2):
                        pe.wait_ge(s["Da"], ONE + 2 * m - 1 + half)
                        for q in range(4):
                            pair = 4 * half + q
                            ins = nc.tensor.transpose(TP[:, half, q * P:q * P + P],
                                                      Dt[:, I, 2 * pair:2 * pair + 2, :].rearrange("p h m -> p (h m)"),
                                                      G.ident[:, :])
                        ins.then_inc(s["Dtr"], 1)
                    pe.wait_ge(s["Da"], ONE + 2 * m + 2)
                    pe.wait_ge(s["comb"], ONE + m)
                    for pair in range(NH // 2):
                        ins = mm(OP[:, 32 * pair:32 * pair + 32], DT[:, pair, :], BDv[:, pair, :], start=True, stop=True)
                    ins.then_inc(s["Dm"], 1)
                    pe.wait_ge(s["comb"], ONE + m + 1)
                    pe.wait_ge(s["fin"], ONE + m * 11)
                    x_out = t1[:, :, :].rearrange("p h d -> p (h d)")
                    for q in range(KD):
                        ins = nc.tensor.transpose(DG[:, q * P:q * P + P], x_out[:, q * P:q * P + P], G.ident[:, :])
                    ins.then_inc(s["Xtr"], 1)
                    pe.wait_ge(s["Xev"], ONE + m + 1)
                    for q in range(KD):
                        ins = mm(DG[:, D:2 * D], xoT[:, q * P:q * P + P], wpT[:, q, :], start=q == 0, stop=q == KD - 1)
                    ins.then_inc(s["proj"], 1)
class Globals:
    pass


def macaron_kernel(nc, A, out):
    with ExitStack() as ctx:
        sb = lambda n, s, d=F32: ctx.enter_context(nc.sbuf_tensor(n, s, d))
        G = Globals()
        G.x = sb("x", [P, NT, D])
        G.mv = sb("mv", [P, NT, 2])
        G.rstd = sb("rstd", [P, NT])
        G.ident = sb("ident", [P, P])
        with ExitStack() as early:
            sb = lambda n, s, d=F32: early.enter_context(nc.sbuf_tensor(n, s, d))
            G.ones = sb("ones", [P, P])
            G.b1 = sb("b1", [P, MH])
            G.a1 = sb("a1", [P, MH])
            G.a2h = sb("a2h", [P, D])
            G.b2h = sb("b2h", [P, D])
            G.sw1T = sb("sw1T", [P, KD, HID], F16)
            G.sw2T = sb("sw2T", [P, MH, D], F16)
            prep_phase(nc, G, A)
            for ph in PHASES[:3][:STOP]:
                ph(nc, G, A)
        for ph in PHASES[3:STOP]:
            ph(nc, G, A)
        s_out = ctx.enter_context(nc.semaphore("stored"))
        block = ctx.enter_context(nc.Block())

        @block.sync
        def _(sp):
            sp.dma_start(out.rearrange("b (t p) d -> p (b t) d", p=P), G.x[:, :, :]).then_inc(s_out, 16)
            sp.wait_ge(s_out, 16)


STOP = 99
PHASES = [lambda nc, G, A: ffn_phase(nc, G, 0), local_phase, lambda nc, G, A: ffn_phase(nc, G, 1),
          lambda nc, G, A: bit_phase(nc, G, A, 0),
          rel_phase, lambda nc, G, A: bit_phase(nc, G, A, 1)]
_INS = {'x': 'L0_attn_x', 'wq': 'L0_attn_wq', 'wk': 'L0_attn_wk', 'wv': 'L0_attn_wv', 'wgq': 'L0_attn_wgq',
        'wgk': 'L0_attn_wgk', 'wgv': 'L0_attn_wgv', 'r_out_w': 'L0_attn_r_out_w', 'gl': 'L0_attn_gate_local_w',
        'gr': 'L0_attn_gate_remote_w', 'w_out': 'L0_attn_w_out', 'w1': 'L0_ffn_w1', 'b1': 'L0_ffn_b1',
        'w2': 'L0_ffn_w2', 'b2': 'L0_ffn_b2', 'w_qkv': 'L1_attn_w_qkv', 'w_proj': 'L1_attn_w_proj',
        'b_proj': 'L1_attn_b_proj', 'rq': 'L1_attn_rpe_q_table', 'rk': 'L1_attn_rpe_k_table',
        'rv': 'L1_attn_rpe_v_table', 'weight': 'L1_ffn_weight', 'gamma': 'L1_ffn_ln_gamma', 'beta': 'L1_ffn_ln_beta'}


def kernel(**inputs):
    import numpy as _np
    import concourse.bacc as _bacc
    from concourse import mybir as _mybir
    from concourse.bass_utils import run_bass_kernel_spmd as _run

    nc = _bacc.Bacc("TRN2", target_bir_lowering=False, num_devices=1)
    arrays, aps = {}, {}
    for short, name in _INS.items():
        a = _np.ascontiguousarray(inputs[name])
        arrays[f"in_{name}_dram"] = a
        aps[short] = nc.dram_tensor(f"in_{name}_dram", a.shape, _mybir.dt.from_np(a.dtype), kind="ExternalInput").ap()
    out = nc.dram_tensor("out_0_dram", (4, 1024, 256), _mybir.dt.float32, kind="ExternalOutput").ap()
    nc.disable_value_cache = True
    macaron_kernel(nc, aps, out)
    r = _run(nc, [arrays], core_ids=[0])
    return r.results[0]["out_0_dram"]
```

```python
import numpy as np
import concourse.bass as bass
from concourse import mybir
from contextlib import ExitStack

F32 = mybir.dt.float32
F16 = mybir.dt.float16
ALU = mybir.AluOpType
ACT = mybir.ActivationFunctionType
AX = mybir.AxisListType
P = 128
B, S, D = 4, 1024, 256
NT = B * S // P
TPB = S // P
KD = D // P
HID = 1024
MH = HID // P
CT = 4
NC = NT // CT
CW = CT * P


ONE = 16


class Count:

    def __init__(self, sem, base=0, it=None, per=0):
        self.sem, self.k, self.it, self.per = sem, base, it, per

    def value(self):
        return ONE + self.k if self.it is None else ONE + self.it * self.per + self.k


def step(eng, ins, c):
    ins.then_inc(c.sem, 1)
    c.k += 1
    eng.wait_ge(c.sem, c.value())


def arm(sp, s):
    for x in s.values():
        sp.sem_inc(x, ONE)


def sems(nc, ctx, prefix, names):
    s = {n: nc.alloc_semaphore(f"{prefix}_{n}") for n in names.split()}

    def clear():
        with nc.Block() as block:
            @block.sync
            def _(sp):
                for x in s.values():
                    sp.sem_clear(x)
        for x in s.values():
            nc.release_semaphore(x)
    ctx.callback(clear)
    return s


STW = 1 + 4 * 6 + 4 * 2


def token_stats(nc, dve, rows, st, mv_out, n, c):
    sums = st[:, 1:25].rearrange("p (t s) -> p t s", t=4)
    agg = st[:, 25:33].rearrange("p (t s) -> p t s", t=4)
    for t in range(n):
        last = nc.vector.bn_stats(sums[:, t, :], rows[:, t, :])
    step(dve, last, c)
    nc.vector.memset(st[:, 0:1], 0.0)
    for t in range(n):
        last = nc.vector.bn_aggr(agg[:, t, :], sums[:, t, :])
    step(dve, last, c)
    step(dve, nc.vector.tensor_scalar(mv_out, agg[:, 0:n, :], 1.0, None, ALU.mult), c)


def prep_phase(nc, G, A):
    with ExitStack() as ctx:
        sb = lambda n, s, d=F32: ctx.enter_context(nc.sbuf_tensor(n, s, d))
        w1n = sb("w1n", [P, MH, D])
        w2n = sb("w2n", [P, KD, HID])
        pos = sb("pos", [P, 2048])
        sg1 = sb("sg1", [P, MH, D])
        sg2 = sb("sg2", [P, KD, HID])
        a2 = sb("a2", [P, KD])
        diag = sb("diag", [P, KD, P])
        row = sb("row0", [P, 1, D])
        st = sb("st0", [P, STW])
        pt = ctx.enter_context(nc.psum_tensor("pt0", [P, 4, 512], F32))
        pa = ctx.enter_context(nc.psum_tensor("pa0", [P, 512], F32))
        s = sems(nc, ctx, "prep", "x_in w1_in w2_in b_in dve zero ident ones signs diag tr evac bcast")
        block = ctx.enter_context(nc.Block())

        @block.sync
        def _(sp):
            arm(sp, s)
            sp.dma_start(G.x[:, :, :], A["x"].rearrange("b (t p) d -> p (b t) d", p=P)).then_inc(s["x_in"], 16)
            sp.dma_start(w1n[:, :, :], A["w1"].rearrange("(m p) d -> p m d", p=P)).then_inc(s["w1_in"], 16)
            sp.dma_start(w2n[:, :, :], A["w2"].rearrange("(k p) h -> p k h", p=P)).then_inc(s["w2_in"], 16)
            sp.dma_start(G.b1[:, :], A["b1"].rearrange("(m p) -> p m", p=P),
                         allow_slow_non_contiguous=True).then_inc(s["b_in"], 16)
            sp.dma_start(G.b2h[:, :], A["b2"].partition_broadcast(P)).then_inc(s["b_in"], 16)
            sp.wait_ge(s["b_in"], ONE + 32)

        @block.gpsimd
        def _(pool):
            nc.gpsimd.memset(G.ident[:, :], 0.0).then_inc(s["zero"], 1)
            nc.gpsimd.memset(G.ones[:, :], 1.0).then_inc(s["ones"], 1)
            pool.wait_ge(s["zero"], ONE + 1)
            nc.gpsimd.affine_select(out=G.ident[:, :], in_=G.ident[:, :], compare_op=ALU.not_equal, fill=1.0,
                                    base=0, pattern=[[-1, P]], channel_multiplier=1).then_inc(s["ident"], 1)

        @block.vector
        def _(dve):
            c = Count(s["dve"])

            def do(ins):
                step(dve, ins, c)

            def sign(w, out, n):
                flat = pos[:, 0:n]
                do(nc.vector.tensor_scalar(flat, w, 0.0, None, ALU.is_lt))
                do(nc.vector.scalar_tensor_tensor(out, w, 0.0, flat, ALU.is_gt, ALU.subtract))
            dve.wait_ge(s["w1_in"], ONE + 16)
            do(nc.vector.tensor_reduce(G.a1[:, :], w1n[:, :, :], AX.X, ALU.add, apply_absolute_value=True))
            do(nc.vector.tensor_scalar(G.a1[:, :], G.a1[:, :], 1.0 / D, None, ALU.mult))
            sign(w1n[:, :, :].rearrange("p m d -> p (m d)"), sg1[:, :, :].rearrange("p m d -> p (m d)"), MH * D)
            dve.wait_ge(s["w2_in"], ONE + 16)
            do(nc.vector.tensor_reduce(a2[:, :], w2n[:, :, :], AX.X, ALU.add, apply_absolute_value=True))
            do(nc.vector.tensor_scalar(a2[:, :], a2[:, :], 0.5 / HID, None, ALU.mult))
            sign(w2n[:, :, :].rearrange("p m d -> p (m d)"), sg2[:, :, :].rearrange("p m d -> p (m d)"), KD * HID)
            nc.vector.memset(pos[:, 0:1], 0.0).then_inc(s["signs"], 1)
            dve.wait_ge(s["ident"], ONE + 1)
            for k in range(KD):
                do(nc.vector.tensor_scalar(diag[:, k, :], G.ident[:, :], a2[:, k:k + 1], None, ALU.mult))
            nc.vector.memset(pos[:, 0:1], 0.0).then_inc(s["diag"], 1)
            for g in range(8):
                dve.wait_ge(s["tr"], ONE + g + 1)
                if g < 4:
                    dst = G.sw1T[:, g // 2, (g % 2) * 512:(g % 2) * 512 + 512]
                else:
                    dst = G.sw2T[:, 2 * (g - 4):2 * (g - 4) + 2, :].rearrange("p m d -> p (m d)")
                step(dve, nc.vector.tensor_copy(dst, pt[:, g % 4, :]), Count(s["evac"], g))
            dve.wait_ge(s["bcast"], ONE + 1)
            do(nc.vector.tensor_copy(G.a2h[:, :], pa[:, 0:D]))
            dve.wait_ge(s["b_in"], ONE + 32)
            do(nc.vector.tensor_scalar(G.b2h[:, :], G.b2h[:, :], 0.5, None, ALU.mult))
            dve.wait_ge(s["x_in"], ONE + 16)
            with dve.Fori(0, NT) as t:
                cl = Count(s["dve"], c.k, t, 4)
                step(dve, nc.vector.tensor_scalar(row[:, 0, :], G.x[:, t, :], 1.0, None, ALU.mult), cl)
                token_stats(nc, dve, row, st, G.mv[:, bass.ds(t, 1), :], 1, cl)

        @block.tensor
        def _(pe):
            pe.wait_ge(s["ident"], ONE + 1)
            pe.wait_ge(s["signs"], ONE + 1)
            for g in range(8):
                if g >= 4:
                    pe.wait_ge(s["evac"], ONE + g - 3)
                for q in range(4):
                    if g < 4:
                        src = sg1[:, (g % 2) * 4 + q, (g // 2) * P:(g // 2) * P + P]
                    else:
                        m = 2 * (g - 4) + q // 2
                        src = sg2[:, q % 2, m * P:m * P + P]
                    last = nc.tensor.transpose(pt[:, g % 4, q * P:q * P + P], src, G.ident[:, :])
                last.then_inc(s["tr"], 1)
            pe.wait_ge(s["diag"], ONE + 1)
            pe.wait_ge(s["ones"], ONE + 1)
            for k in range(KD):
                last = nc.tensor.matmul(pa[:, k * P:k * P + P], G.ones[:, :], diag[:, k, :], start=True, stop=True)
            last.then_inc(s["bcast"], 1)


def ffn_phase(nc, G, r):
    with ExitStack() as ctx:
        sb = lambda n, s, d=F32: ctx.enter_context(nc.sbuf_tensor(f"f{r}_{n}", s, d))
        ps = lambda n, s: ctx.enter_context(nc.psum_tensor(f"f{r}_{n}", s, F32))
        sd = sb("sd", [P, NT])
        rstd = sb("rstd", [P, NT])
        eps = sb("eps", [P, 1])
        xn = sb("xn", [P, CT, D])
        xhi = sb("xhi", [P, KD, CW], F16)
        xlo = sb("xlo", [P, KD, CW], F16)
        h = sb("h", [P, 2, CW])
        hhi = sb("hhi", [P, 2, CW], F16)
        hlo = sb("hlo", [P, 2, CW], F16)
        y = sb("y", [P, CT, D])
        st = sb("st", [P, STW])
        psT = ps("psT", [P, KD, 512])
        psH = ps("psH", [P, 2, 512])
        psY = ps("psY", [P, CT, 512])
        s = sems(nc, ctx, f"ffn{r}", "eps sd dve xn xT xhi xlo H h hhi hlo Y out")
        block = ctx.enter_context(nc.Block())
        OUT_PER = 7

        @block.sync
        def _(sp):
            arm(sp, s)

        @block.scalar
        def _(act):
            act.wait_ge(s["eps"], ONE + 1)
            nc.scalar.activation(sd[:, :], G.mv[:, :, 1], ACT.Sqrt, bias=eps[:, :]).then_inc(s["sd"], 1)

            def high_parts(i):
                for k in range(KD):
                    act.wait_ge(s["xT"], ONE + i * KD + k + 1)
                    if k == 0:
                        act.wait_ge(s["H"], ONE + i * MH)
                    nc.scalar.activation(xhi[:, k, :], psT[:, k, :], ACT.Copy).then_inc(s["xhi"], 1)

            def chunk(i, more):
                for m in range(MH):
                    n = i * MH + m
                    act.wait_ge(s["H"], ONE + n + 1)
                    act.wait_ge(s["hlo"], ONE + n - 1)
                    nc.scalar.activation(h[:, m % 2, :], psH[:, m % 2, :], ACT.Gelu, bias=G.b1[:, m:m + 1],
                                         scale=G.a1[:, m:m + 1]).then_inc(s["h"], 1)
                    act.wait_ge(s["h"], ONE + n + 1)
                    act.wait_ge(s["Y"], ONE + n - 1)
                    nc.scalar.activation(hhi[:, m % 2, :], h[:, m % 2, :], ACT.Copy).then_inc(s["hhi"], 1)
                if more:
                    high_parts(i + 1)
            high_parts(0)
            with act.Fori(0, NC - 1) as i:
                chunk(i, True)
            chunk(NC - 1, False)

        @block.vector
        def _(dve):
            step(dve, nc.vector.memset(eps[:, :], 1e-5), Count(s["eps"]))
            dve.wait_ge(s["sd"], ONE + 1)
            c = Count(s["dve"])
            step(dve, nc.vector.reciprocal(rstd[:, :], sd[:, :]), c)

            def normalise(i):
                dve.wait_ge(s["xT"], ONE + i * KD)
                for t in range(CT):
                    nc.vector.tensor_scalar(xn[:, t, :], G.x[:, i * CT + t, :], G.mv[:, i * CT + t, 0:1],
                                            rstd[:, bass.ds(i * CT + t, 1)], ALU.subtract,
                                            ALU.mult).then_inc(s["xn"], 1)

            def low_parts(i):
                for k in range(KD):
                    dve.wait_ge(s["xhi"], ONE + i * KD + k + 1)
                    nc.vector.tensor_tensor(xlo[:, k, :], psT[:, k, :], xhi[:, k, :], ALU.subtract).then_inc(s["xlo"], 1)

            def chunk(i, more):
                for m in range(MH):
                    if more and m == MH // 2:
                        normalise(i + 1)
                    dve.wait_ge(s["hhi"], ONE + i * MH + m + 1)
                    nc.vector.tensor_tensor(hlo[:, m % 2, :], h[:, m % 2, :], hhi[:, m % 2, :],
                                            ALU.subtract).then_inc(s["hlo"], 1)
                if more:
                    low_parts(i + 1)
                dve.wait_ge(s["Y"], ONE + i * MH + MH)
                cl = Count(s["out"], 0, i, OUT_PER)
                rows = G.x[:, bass.ds(i * CT, CT), :]
                step(dve, nc.vector.tensor_tensor(y[:, :, :], psY[:, :, 0:D],
                                                  G.a2h[:, :].unsqueeze(1).to_broadcast([P, CT, D]), ALU.mult), cl)
                step(dve, nc.vector.tensor_tensor(y[:, :, :], y[:, :, :],
                                                  G.b2h[:, :].unsqueeze(1).to_broadcast([P, CT, D]), ALU.add), cl)
                step(dve, nc.vector.tensor_tensor(y[:, :, :], y[:, :, :], rows, ALU.add), cl)
                step(dve, nc.vector.tensor_scalar(rows, y[:, :, :], 1.0, None, ALU.mult), cl)
                token_stats(nc, dve, y, st, G.mv[:, bass.ds(i * CT, CT), :], CT, cl)
                assert cl.k == OUT_PER
            normalise(0)
            low_parts(0)
            with dve.Fori(0, NC - 1) as i:
                chunk(i, True)
            chunk(NC - 1, False)

        @block.tensor
        def _(pe):
            def hidden(i, m):
                pe.wait_ge(s["h"], ONE + i * MH + m - 1)
                for k in range(KD):
                    for part, x in enumerate((xhi, xlo)):
                        last = nc.tensor.matmul(psH[:, m % 2, :], G.sw1T[:, k, m * P:m * P + P], x[:, k, :],
                                                start=(k + part == 0), stop=(k == KD - 1 and part == 1))
                last.then_inc(s["H"], 1)

            def down(i, m):
                pe.wait_ge(s["hlo"], ONE + i * MH + m + 1)
                for t in range(CT):
                    for part, x in enumerate((hhi, hlo)):
                        last = nc.tensor.matmul(psY[:, t, 0:D], x[:, m % 2, t * P:t * P + P], G.sw2T[:, m, :],
                                                start=(m + part == 0), stop=(m == MH - 1 and part == 1))
                last.then_inc(s["Y"], 1)

            def transposed(i):
                pe.wait_ge(s["xn"], ONE + i * CT + CT)
                pe.wait_ge(s["xlo"], ONE + i * KD)
                for k in range(KD):
                    for t in range(CT):
                        last = nc.tensor.transpose(psT[:, k, t * P:t * P + P], xn[:, t, k * P:k * P + P],
                                                   G.ident[:, :])
                    last.then_inc(s["xT"], 1)

            def chunk(i, more):
                pe.wait_ge(s["xlo"], ONE + i * KD + KD)
                hidden(i, 0)
                for m in range(MH):
                    if m + 1 < MH:
                        hidden(i, m + 1)
                    elif more:
                        transposed(i + 1)
                    if m == 0:
                        pe.wait_ge(s["out"], ONE + (i - 1) * OUT_PER + 1)
                    down(i, m)
            transposed(0)
            with pe.Fori(0, NC - 1) as i:
                chunk(i, True)
            chunk(NC - 1, False)


NEG = -1e30
WIN = 64
NH, HD = 16, 16
HQ = NH // 4
LH, NL = 8, 64
CHUNK = S // NL
LW = 192


def rstd_phase(nc, G, name, eps_value):
    with ExitStack() as ctx:
        sd = ctx.enter_context(nc.sbuf_tensor(f"{name}_sd", [P, NT], F32))
        eps = ctx.enter_context(nc.sbuf_tensor(f"{name}_eps", [P, 1], F32))
        s = sems(nc, ctx, name, "eps sd rstd")
        block = ctx.enter_context(nc.Block())

        @block.sync
        def _(sp):
            arm(sp, s)

        @block.scalar
        def _(act):
            act.wait_ge(s["eps"], ONE + 1)
            nc.scalar.activation(sd[:, :], G.mv[:, :, 1], ACT.Sqrt, bias=eps[:, :]).then_inc(s["sd"], 1)

        @block.vector
        def _(dve):
            step(dve, nc.vector.memset(eps[:, :], eps_value), Count(s["eps"]))
            dve.wait_ge(s["sd"], ONE + 1)
            step(dve, nc.vector.reciprocal(G.rstd[:, :], sd[:, :]), Count(s["rstd"]))


def local_phase(nc, G, A):
    rstd_phase(nc, G, "a0n", 1e-5)
    with ExitStack() as ctx:
        sb = lambda n, s, d=F32: ctx.enter_context(nc.sbuf_tensor(f"a0_{n}", s, d))
        ps = lambda n, s: ctx.enter_context(nc.psum_tensor(f"a0_{n}", s, F32))
        wq = sb("wq", [P, KD, NH, 32])
        wk = sb("wk", [P, KD, NH, 32])
        wgq = sb("wgq", [P, KD, LH, 32])
        wgk = sb("wgk", [P, KD, LH, 32])
        wv = sb("wv", [P, KD, D])
        wgv = sb("wgv", [P, KD, P])
        wr = sb("wr", [P, D])
        wo = sb("wo", [P, KD, D])
        gates = sb("gates", [P, HQ, 2, NH])
        mask = sb("mask", [P, 2, LW])
        lmask = sb("lmask", [P, TPB, NL])
        xn = sb("xn", [P, TPB, D])
        xT = sb("xT", [P, KD, S])
        xp = sb("xp", [P, KD, 2, NL])
        QT = sb("QT", [P, HQ, S])
        KT = sb("KT", [P, HQ, P + S])
        V = sb("V", [P, TPB, D + HD])
        OT = sb("OT", [P, 2, P])
        GQT = sb("GQT", [P, 2, S])
        GKT = sb("GKT", [P, 2, NL])
        GV = sb("GV", [P, LH // 2, 32])
        gt = sb("gt", [P, TPB, 2 * NH])
        Sm = sb("Sm", [P, 2, 4, LW])
        mx = sb("mx", [P, 2, 4])
        nb = sb("nb", [P, 2, 4])
        Pe = sb("Pe", [P, 2, 4, 256])
        rs = sb("rs", [P, 2, 4])
        ri = sb("ri", [P, 4, 4])
        PT = sb("PT", [P, 2, 1024])
        loc = sb("loc", [P, TPB, D])
        sl = sb("sl", [P, 4, LH, NL])
        lm = sb("lm", [P, 4, LH])
        slT = sb("slT", [P, 4, 512])
        rem = sb("rem", [P, 4, P])
        remT = sb("remT", [P, 4, P])
        o = sb("o", [P, 4, D])
        o2 = sb("o2", [P, 4, D])
        oT = sb("oT", [P, 4, D])
        st = sb("st", [P, STW])
        R = ps("R", [P, 4, 512])
        Z = ps("Z", [P, 4, 512])
        s = sems(nc, ctx, "a0", "w_in zero masks pool xn tr xT pooled pj pj_a pj_d S masked max shift exp T PTa PTd O OTev back recip norm "
                 "gexp gates lS lmasked lmax lsub lexp lsum lrecip B Bev C rem Dt Dev E gated o F Fev out stat")
        block = ctx.enter_context(nc.Block())
        PROJ = ([("q", m, c) for c in range(2) for m in range(HQ)] + [("k", m, c) for c in range(2) for m in range(HQ)]
                + [("gq", m, c) for m in range(2) for c in range(2)] + [("v", t, 0) for t in range(0, TPB, 2)]
                + [("g", 0, 0), ("gate", 0, 0)])
        NPJ = len(PROJ)
        UNITS = [(t, hq) for t in range(TPB) for hq in range(HQ)]
        NU = len(UNITS)

        def pj_done(i, j):
            return i * ((NPJ + 1) // 2) + (j + 2) // 2, i * (NPJ // 2) + (j + 1) // 2

        @block.sync
        def _(sp):
            arm(sp, s)
            sp.wait_ge(s["zero"], ONE + 1)
            with nc.allow_non_contiguous_dma("weights by head, once"):
                for dst, src in ((wq, "wq"), (wk, "wk"), (wgq, "wgq"), (wgk, "wgk")):
                    for k in range(KD):
                        sp.dma_start(dst[:, k, :, 0:HD],
                                     A[src][k * P:(k + 1) * P, :].rearrange("p (h d) -> p h d", d=HD)).then_inc(s["w_in"], 16)
                sp.dma_start(wv[:, :, :], A["wv"].rearrange("(k p) d -> p k d", p=P)).then_inc(s["w_in"], 16)
                sp.dma_start(wgv[:, :, :], A["wgv"].rearrange("(k p) d -> p k d", p=P)).then_inc(s["w_in"], 16)
                sp.dma_start(wr[:, :], A["r_out_w"]).then_inc(s["w_in"], 16)
                sp.dma_start(wo[:, :, :], A["w_out"].rearrange("(k p) d -> p k d", p=P)).then_inc(s["w_in"], 16)
                for n, g in enumerate(("gl", "gr")):
                    for h in range(NH):
                        sp.dma_start(gates[32 * (h % 4):32 * (h % 4) + HD, h // 4, n, h:h + 1],
                                     A[g][h:h + 1, :].rearrange("a d -> d a")).then_inc(s["w_in"], 16)

        NWIN = 16 * (8 + 4 + 2 * NH)

        @block.gpsimd
        def _(pool):
            c = Count(s["pool"])
            nc.gpsimd.memset(wq[:, :, :, :], 0.0)
            nc.gpsimd.memset(wk[:, :, :, :], 0.0)
            nc.gpsimd.memset(wgq[:, :, :, :], 0.0)
            nc.gpsimd.memset(wgk[:, :, :, :], 0.0)
            nc.gpsimd.memset(gates[:, :, :, :], 0.0).then_inc(s["zero"], 1)
            nc.gpsimd.memset(KT[:, :, 0:P], 0.0)
            nc.gpsimd.memset(V[:, :, D:], 0.0)
            nc.gpsimd.memset(Pe[:, :, :, 0:WIN], 0.0)
            nc.gpsimd.memset(GV[:, :, :], 0.0)
            nc.gpsimd.memset(lmask[:, :, :], 0.0)
            step(pool, nc.gpsimd.memset(mask[:, :, :], 0.0), c)
            step(pool, nc.gpsimd.affine_select(out=mask[:, :, :], in_=mask[:, :, :], compare_op=ALU.is_gt, fill=NEG,
                                               base=0, pattern=[[0, 2], [1, LW]], channel_multiplier=-1), c)
            step(pool, nc.gpsimd.affine_select(out=mask[:, :, :], in_=mask[:, :, :], compare_op=ALU.is_ge, fill=NEG,
                                               base=WIN, pattern=[[0, 2], [-1, LW]], channel_multiplier=1), c)
            step(pool, nc.gpsimd.affine_select(out=mask[:, 0, :], in_=mask[:, 0, :], compare_op=ALU.is_ge, fill=NEG,
                                               base=-WIN, pattern=[[1, LW]], channel_multiplier=0), c)
            nc.gpsimd.affine_select(out=lmask[:, :, :], in_=lmask[:, :, :], compare_op=ALU.is_ge, fill=NEG, base=0,
                                    pattern=[[P, TPB], [-CHUNK, NL]], channel_multiplier=1).then_inc(s["masks"], 1)

        def evacuate(i, copy, j, kind, m, c):
            bank = R[:, j % 4, :]
            cols = slice(c * 512, c * 512 + 512)
            if kind == "q":
                return copy(QT[:, m, cols], bank)
            if kind == "k":
                return copy(KT[:, m, P + c * 512:P + c * 512 + 512], bank)
            if kind == "gq":
                return copy(GQT[:, m, cols], bank)
            if kind == "v":
                return copy(V[:, m:m + 2, 0:D], bank.rearrange("p (t d) -> p t d", t=2))
            if kind == "g":
                copy(GKT[:, :, :].rearrange("p m n -> p (m n)"), bank[:, 0:2 * NL])
                gv = bank[:, P:2 * P].rearrange("p (q a d) -> p q a d", a=2, d=HD)
                copy(GV[0:NL, :, 0:HD], gv[0:NL, :, 0, :])
                return copy(GV[NL:P, :, HD:32], gv[NL:P, :, 1, :])
            return copy(gt[:, :, :].rearrange("p t n -> p (t n)"), bank[:, 0:TPB * 2 * NH])

        @block.scalar
        def _(act):
            copy = lambda o_, i_: nc.scalar.activation(o_, i_, ACT.Copy)
            with act.Fori(0, B) as i:
                for g in range(4):
                    act.wait_ge(s["tr"], ONE + i * 4 + g + 1)
                    copy(xT[:, g // 2, (g % 2) * 512:(g % 2) * 512 + 512], Z[:, g, :]).then_inc(s["xT"], 1)
                for j, (kind, m, c) in enumerate(PROJ):
                    if j % 2 == 0:
                        act.wait_ge(s["pj"], ONE + i * NPJ + j + 1)
                        evacuate(i, copy, j, kind, m, c).then_inc(s["pj_a"], 1)
                for u in range(NU + 2):
                    if 1 <= u <= NU:
                        v = u - 1
                        act.wait_ge(s["T"], ONE + 2 * (i * NU + v) + 1)
                        if v >= 2:
                            act.wait_ge(s["O"], ONE + i * NU + v - 1)
                        copy(PT[:, v % 2, 0:512], Z[:, 0, :]).then_inc(s["PTa"], 1)
                    if u < NU:
                        act.wait_ge(s["shift"], ONE + i * NU + u + 1)
                        if u >= 2:
                            act.wait_ge(s["T"], ONE + 2 * (i * NU + u - 1))
                            act.wait_ge(s["recip"], ONE + i * NU + u - 1)
                        for c in range(4):
                            last = nc.scalar.activation(Pe[:, u % 2, c, WIN:256], Sm[:, u % 2, c, :], ACT.Exp,
                                                        bias=nb[:, u % 2, c:c + 1], scale=0.25,
                                                        accum_out=rs[:, u % 2, c:c + 1])
                        last.then_inc(s["exp"], 1)
                    if u >= 2:
                        v = u - 2
                        act.wait_ge(s["O"], ONE + i * NU + v + 1)
                        act.wait_ge(s["back"], ONE + i * NU + v - 1)
                        copy(OT[:, v % 2, :], Z[:, 2, 0:P]).then_inc(s["OTev"], 1)
                for g in range(2):
                    if g == 0:
                        act.wait_ge(s["pj_d"], ONE + i * (NPJ // 2) + NPJ // 2)
                        act.wait_ge(s["pj_a"], ONE + (i + 1) * ((NPJ + 1) // 2))
                        nc.scalar.activation(gt[:, :, :], gt[:, :, :], ACT.Exp, scale=-1.0).then_inc(s["gexp"], 1)
                    for t in range(4 * g, 4 * g + 4):
                        act.wait_ge(s["lsub"], ONE + i * TPB + t + 1)
                        nc.scalar.activation(sl[:, t % 4, :, :], sl[:, t % 4, :, :], ACT.Exp,
                                             scale=0.25).then_inc(s["lexp"], 1)
                    for t in range(4 * g, 4 * g + 4):
                        act.wait_ge(s["B"], ONE + i * TPB + t + 1)
                        copy(slT[:, t % 4, :], Z[:, t % 4, :]).then_inc(s["Bev"], 1)
                    for t in range(4 * g, 4 * g + 4):
                        act.wait_ge(s["Dt"], ONE + i * TPB + t + 1)
                        copy(remT[:, t % 4, :], Z[:, t % 4, 0:P]).then_inc(s["Dev"], 1)
                    for t in range(4 * g, 4 * g + 4):
                        act.wait_ge(s["F"], ONE + i * TPB + t + 1)
                        copy(oT[:, t % 4, :], Z[:, t % 4, 0:D]).then_inc(s["Fev"], 1)

        @block.vector
        def _(dve):
            copy = lambda o_, i_: nc.vector.tensor_copy(o_, i_)

            def do(ins, name, value):
                ins.then_inc(s[name], 1)
                dve.wait_ge(s[name], ONE + value)

            dve.wait_ge(s["masks"], ONE + 1)
            with dve.Fori(0, B) as i:
                for t in range(TPB):
                    nc.vector.tensor_scalar(xn[:, t, :], G.x[:, i * TPB + t, :], G.mv[:, i * TPB + t, 0:1],
                                            G.rstd[:, bass.ds(i * TPB + t, 1)], ALU.subtract,
                                            ALU.mult).then_inc(s["xn"], 1)
                dve.wait_ge(s["xT"], ONE + i * 4 + 4)
                for k in range(KD):
                    ins = nc.vector.tensor_reduce(xp[:, k, 0, :], xT[:, k, :].rearrange("p (n c) -> p n c", c=CHUNK),
                                                  AX.X, ALU.add)
                do(ins, "pooled", i * 3 + 1)
                do(nc.vector.tensor_scalar(xp[:, :, 0, :], xp[:, :, 0, :], 1.0 / CHUNK, None, ALU.mult), "pooled", i * 3 + 2)
                do(nc.vector.tensor_copy(xp[:, :, 1, :], xp[:, :, 0, :]), "pooled", i * 3 + 3)
                for j, (kind, m, c) in enumerate(PROJ):
                    if j % 2 == 1:
                        dve.wait_ge(s["pj"], ONE + i * NPJ + j + 1)
                        evacuate(i, copy, j, kind, m, c).then_inc(s["pj_d"], 1)
                for u in range(NU + 3):
                    if u < NU:
                        t, hq = UNITS[u]
                        b = u % 2
                        dve.wait_ge(s["S"], ONE + i * NU + u + 1)
                        if u >= 2:
                            dve.wait_ge(s["exp"], ONE + i * NU + u - 1)
                        do(nc.vector.tensor_tensor(Sm[:, b, :, :], R[:, :, 0:LW],
                                                   mask[:, min(t, 1), :].unsqueeze(1).to_broadcast([P, 4, LW]),
                                                   ALU.add), "masked", i * NU + u + 1)
                        do(nc.vector.tensor_reduce(mx[:, b, :], Sm[:, b, :, :], AX.X, ALU.max), "max", i * NU + u + 1)
                        nc.vector.tensor_scalar(nb[:, b, :], mx[:, b, :], -0.25, None, ALU.mult).then_inc(s["shift"], 1)
                    if 1 <= u <= NU:
                        v = u - 1
                        dve.wait_ge(s["exp"], ONE + i * NU + v + 1)
                        dve.wait_ge(s["norm"], ONE + i * NU + v - 3)
                        nc.vector.reciprocal(ri[:, v % 4, :], rs[:, v % 2, :]).then_inc(s["recip"], 1)
                        dve.wait_ge(s["T"], ONE + 2 * (i * NU + v) + 2)
                        if v >= 2:
                            dve.wait_ge(s["O"], ONE + i * NU + v - 1)
                        copy(PT[:, v % 2, 512:1024], Z[:, 1, :]).then_inc(s["PTd"], 1)
                    if u >= 3:
                        v = u - 3
                        t, hq = UNITS[v]
                        dve.wait_ge(s["back"], ONE + i * NU + v + 1)
                        dve.wait_ge(s["recip"], ONE + i * NU + v + 1)
                        dst = loc[:, t, hq * 64:hq * 64 + 64].rearrange("p (c d) -> p c d", c=4)
                        nc.vector.tensor_tensor(dst, Z[:, 3, 0:P].rearrange("p (c d) -> p c d", c=4)[:, :, 0:HD],
                                                ri[:, v % 4, :].unsqueeze(2).to_broadcast([P, 4, HD]),
                                                ALU.mult).then_inc(s["norm"], 1)
                dve.wait_ge(s["gexp"], ONE + i + 1)
                do(nc.vector.tensor_scalar(gt[:, :, :], gt[:, :, :], 1.0, None, ALU.add), "gates", i * 2 + 1)
                do(nc.vector.reciprocal(gt[:, :, :], gt[:, :, :]), "gates", i * 2 + 2)
                for g in range(2):
                    tiles = range(4 * g, 4 * g + 4)
                    for t in tiles:
                        q, n = t % 4, i * TPB + t + 1
                        dve.wait_ge(s["lS"], ONE + i * TPB + 4 * g + 4)
                        for m in range(2):
                            ins = nc.vector.tensor_tensor(sl[:, q, 4 * m:4 * m + 4, :],
                                                          R[:, :, (2 * q + m) * NL:(2 * q + m) * NL + NL],
                                                          lmask[:, t, :].unsqueeze(1).to_broadcast([P, 4, NL]), ALU.add)
                        do(ins, "lmasked", n)
                        do(nc.vector.tensor_reduce(lm[:, q, :], sl[:, q, :, :], AX.X, ALU.max), "lmax", n)
                        nc.vector.tensor_tensor(sl[:, q, :, :], sl[:, q, :, :],
                                                lm[:, q, :].unsqueeze(2).to_broadcast([P, LH, NL]),
                                                ALU.subtract).then_inc(s["lsub"], 1)
                    for t in tiles:
                        q, n = t % 4, i * TPB + t + 1
                        dve.wait_ge(s["lexp"], ONE + n)
                        do(nc.vector.tensor_reduce(lm[:, q, :], sl[:, q, :, :], AX.X, ALU.add), "lsum", n)
                        do(nc.vector.reciprocal(lm[:, q, :], lm[:, q, :]), "lrecip", n)
                    for t in tiles:
                        q, n = t % 4, i * TPB + t + 1
                        dve.wait_ge(s["C"], ONE + n)
                        nc.vector.tensor_tensor(rem[:, q, :].rearrange("p (h d) -> p h d", h=LH),
                                                R[:, q, 0:P].rearrange("p (h d) -> p h d", h=LH),
                                                lm[:, q, :].unsqueeze(2).to_broadcast([P, LH, HD]),
                                                ALU.mult).then_inc(s["rem"], 1)
                    for t in tiles:
                        q, n = t % 4, i * TPB + t + 1
                        heads = lambda a: a.rearrange("p (h d) -> p h d", h=NH)
                        gate = lambda w: gt[:, t, w * NH:(w + 1) * NH].unsqueeze(2).to_broadcast([P, NH, HD])
                        dve.wait_ge(s["E"], ONE + n)
                        if t >= 4:
                            dve.wait_ge(s["F"], ONE + n - 4)
                        nc.vector.tensor_tensor(heads(o2[:, q, :]), heads(loc[:, t, :]), gate(0), ALU.mult)
                        do(nc.vector.tensor_tensor(heads(o[:, q, :]), heads(R[:, q, 0:D]), gate(1), ALU.mult), "gated", n)
                        nc.vector.tensor_tensor(o[:, q, :], o[:, q, :], o2[:, q, :], ALU.add).then_inc(s["o"], 1)
                    for t in tiles:
                        q, n = t % 4, i * TPB + t + 1
                        dve.wait_ge(s["out"], ONE + n)
                        cs = Count(s["stat"], 5 * t, i, 5 * TPB)
                        row = G.x[:, i * TPB + t, :]
                        step(dve, nc.vector.tensor_tensor(o2[:, q, :], R[:, q, 0:D], row, ALU.add), cs)
                        step(dve, nc.vector.tensor_scalar(row, o2[:, q, :], 1.0, None, ALU.mult), cs)
                        token_stats(nc, dve, o2[:, q:q + 1, :], st, G.mv[:, bass.ds(i * TPB + t, 1), :], 1, cs)

        @block.tensor
        def _(pe):
            pe.wait_ge(s["w_in"], ONE + NWIN)
            pe.wait_ge(s["masks"], ONE + 1)
            mm = nc.tensor.matmul
            with pe.Fori(0, B) as i:
                pe.wait_ge(s["xn"], ONE + i * TPB + TPB)
                pe.wait_ge(s["Fev"], ONE + i * TPB)
                for g in range(4):
                    for q in range(4):
                        t = (g % 2) * 4 + q
                        ins = nc.tensor.transpose(Z[:, g, q * P:q * P + P], xn[:, t, (g // 2) * P:(g // 2) * P + P],
                                                  G.ident[:, :])
                    ins.then_inc(s["tr"], 1)
                pe.wait_ge(s["xT"], ONE + i * 4 + 4)
                pe.wait_ge(s["stat"], ONE + i * 5 * TPB)
                for j, (kind, m, c) in enumerate(PROJ):
                    if j >= 4:
                        na, nd = pj_done(i, j - 4)
                        pe.wait_ge(s["pj_a"], ONE + na) if j % 2 == 0 else pe.wait_ge(s["pj_d"], ONE + nd)
                    bank = R[:, j % 4, :]
                    for k in range(KD):
                        fl = dict(start=k == 0, stop=k == KD - 1)
                        cols = slice(c * 512, c * 512 + 512)
                        if kind in ("q", "k", "gq"):
                            w = {"q": wq, "k": wk, "gq": wgq}[kind]
                            ins = mm(bank, w[:, k, 4 * m:4 * m + 4, :].rearrange("p h d -> p (h d)"), xT[:, k, cols], **fl)
                    if kind == "v":
                        for t in (m, m + 1):
                            for k in range(KD):
                                ins = mm(bank[:, (t - m) * D:(t - m) * D + D], xT[:, k, t * P:t * P + P], wv[:, k, :],
                                         start=k == 0, stop=k == KD - 1)
                    if kind == "g":
                        pe.wait_ge(s["pooled"], ONE + i * 3 + 3)
                        for mg in range(2):
                            for k in range(KD):
                                ins = mm(bank[:, mg * NL:mg * NL + NL],
                                         wgk[:, k, 4 * mg:4 * mg + 4, :].rearrange("p h d -> p (h d)"), xp[:, k, 0, :],
                                         start=k == 0, stop=k == KD - 1)
                        for k in range(KD):
                            ins = mm(bank[:, P:2 * P], xp[:, k, :, :].rearrange("p a n -> p (a n)"), wgv[:, k, :],
                                     start=k == 0, stop=k == KD - 1)
                    if kind == "gate":
                        for t in range(TPB):
                            for mq in range(HQ):
                                ins = mm(bank[:, t * 32:t * 32 + 32], QT[:, mq, t * P:t * P + P],
                                         gates[:, mq, :, :].rearrange("p a h -> p (a h)"),
                                         start=mq == 0, stop=mq == HQ - 1)
                    ins.then_inc(s["pj"], 1)
                na, nd = pj_done(i, NPJ - 1)
                pe.wait_ge(s["pj_a"], ONE + na)
                pe.wait_ge(s["pj_d"], ONE + nd)
                for u in range(NU + 3):
                    if u < NU:
                        t, hq = UNITS[u]
                        if u >= 1:
                            pe.wait_ge(s["masked"], ONE + i * NU + u)
                        for c in range(4):
                            rows = slice(32 * c, 32 * c + HD)
                            ins = mm(R[:, c, 0:LW],
                                     QT[rows, hq, t * P:t * P + P], KT[rows, hq, t * P + WIN:t * P + WIN + LW],
                                     start=True, stop=True)
                        ins.then_inc(s["S"], 1)
                    if 1 <= u <= NU:
                        v = u - 1
                        pe.wait_ge(s["exp"], ONE + i * NU + v + 1)
                        for half in range(2):
                            if v >= 1:
                                pe.wait_ge(s["PTa"] if half == 0 else s["PTd"], ONE + i * NU + v)
                            for n in range(4):
                                c, w = 2 * half + n // 2, n % 2
                                ins = nc.tensor.transpose(Z[:, half, n * P:n * P + P],
                                                          Pe[:, v % 2, c, w * P:w * P + P], G.ident[:, :])
                            ins.then_inc(s["T"], 1)
                    if 2 <= u <= NU + 1:
                        v = u - 2
                        t, hq = UNITS[v]
                        pe.wait_ge(s["PTa"], ONE + i * NU + v + 1)
                        pe.wait_ge(s["PTd"], ONE + i * NU + v + 1)
                        pe.wait_ge(s["OTev"], ONE + i * NU + v)
                        for c in range(4):
                            cols = slice((4 * hq + c) * HD, (4 * hq + c) * HD + 32)
                            out = Z[32 * c:32 * c + 32, 2, 0:P]
                            if t > 0:
                                mm(out, V[:, t - 1, cols], PT[:, v % 2, c * 256:c * 256 + P], start=True, stop=False)
                            ins = mm(out, V[:, t, cols], PT[:, v % 2, c * 256 + P:c * 256 + 256], start=t == 0, stop=True)
                        ins.then_inc(s["O"], 1)
                    if u >= 3:
                        v = u - 3
                        pe.wait_ge(s["OTev"], ONE + i * NU + v + 1)
                        pe.wait_ge(s["norm"], ONE + i * NU + v)
                        nc.tensor.transpose(Z[:, 3, 0:P], OT[:, v % 2, :], G.ident[:, :]).then_inc(s["back"], 1)
                pe.wait_ge(s["norm"], ONE + i * NU + NU)
                for g in range(2):
                    tiles = range(4 * g, 4 * g + 4)
                    if g:
                        pe.wait_ge(s["Fev"], ONE + i * TPB + 4)
                    for t in tiles:
                        q = t % 4
                        if g:
                            pe.wait_ge(s["stat"], ONE + i * 5 * TPB + 5 * 3 + 1)
                        for h in range(LH):
                            rows = slice(32 * (h % 4), 32 * (h % 4) + HD)
                            at = (2 * q + h // 4) * NL
                            ins = mm(R[:, h % 4, at:at + NL], GQT[rows, h // 4, t * P:t * P + P],
                                     GKT[rows, h // 4, :], start=True, stop=True)
                        ins.then_inc(s["lS"], 1)
                    for t in tiles:
                        q, n = t % 4, i * TPB + t + 1
                        pe.wait_ge(s["lexp"], ONE + n)
                        for a in range(LH // 2):
                            ins = nc.tensor.transpose(Z[:, q, a * P:a * P + P],
                                                      sl[:, q, 2 * a:2 * a + 2, :].rearrange("p h n -> p (h n)"),
                                                      G.ident[:, :])
                        ins.then_inc(s["B"], 1)
                    for t in tiles:
                        q, n = t % 4, i * TPB + t + 1
                        pe.wait_ge(s["Bev"], ONE + n)
                        pe.wait_ge(s["lmasked"], ONE + i * TPB + 4 * g + 4)
                        for a in range(LH // 2):
                            ins = mm(R[:, q, a * 32:a * 32 + 32], slT[:, q, a * P:a * P + P], GV[:, a, :],
                                     start=True, stop=True)
                        ins.then_inc(s["C"], 1)
                    for t in tiles:
                        q, n = t % 4, i * TPB + t + 1
                        pe.wait_ge(s["rem"], ONE + n)
                        nc.tensor.transpose(Z[:, q, 0:P], rem[:, q, :], G.ident[:, :]).then_inc(s["Dt"], 1)
                    for t in tiles:
                        q, n = t % 4, i * TPB + t + 1
                        pe.wait_ge(s["Dev"], ONE + n)
                        mm(R[:, q, 0:D], remT[:, q, :], wr[:, :], start=True, stop=True).then_inc(s["E"], 1)
                    for t in tiles:
                        q, n = t % 4, i * TPB + t + 1
                        pe.wait_ge(s["o"], ONE + n)
                        for k in range(KD):
                            ins = nc.tensor.transpose(Z[:, q, k * P:k * P + P], o[:, q, k * P:k * P + P], G.ident[:, :])
                        ins.then_inc(s["F"], 1)
                    for t in tiles:
                        q, n = t % 4, i * TPB + t + 1
                        pe.wait_ge(s["Fev"], ONE + n)
                        for k in range(KD):
                            ins = mm(R[:, q, 0:D], oT[:, q, k * P:k * P + P], wo[:, k, :],
                                     start=k == 0, stop=k == KD - 1)
                        ins.then_inc(s["out"], 1)


def bit_phase(nc, G, A, r, out=None):
    rstd_phase(nc, G, f"b{r}n", 1e-5)
    QB, CLIP = 128.0, float(np.float32(128.0 - 1e-5))
    with ExitStack() as ctx:
        sb = lambda n, sh, d=F32: ctx.enter_context(nc.sbuf_tensor(f"b{r}_{n}", sh, d))
        ps = lambda n, sh: ctx.enter_context(nc.psum_tensor(f"b{r}_{n}", sh, F32))
        w = sb("w", [P, KD, D])
        wt = sb("wt", [P, KD, D])
        wq = sb("wq", [P, KD, D], F16)
        gm = sb("gm", [P, D])
        bt = sb("bt", [P, D])
        wsum = sb("wsum", [P, 1])
        wall = sb("wall", [P, 1])
        thr = sb("thr", [P, 2])
        scl = sb("scl", [P, NT])
        tmp = sb("tmp", [P, NT])
        tmax = sb("tmax", [P, NC])
        pmax = sb("pmax", [P, 1])
        gall = sb("gall", [P, 1])
        gi = sb("gi", [P, 1])
        osc = sb("osc", [P, 1])
        eps3 = sb("eps3", [P, 1])
        xn = sb("xn", [P, NT, D])
        xq = sb("xq", [P, CT, D])
        xhi = sb("xhi", [P, KD, CW], F16)
        xlo = sb("xlo", [P, KD, CW], F16)
        y = sb("y", [P, CT, D])
        st = sb("st", [P, STW])
        psT = ps("psT", [P, KD, 512])
        psY = ps("psY", [P, CT, 512])
        s = sems(nc, ctx, f"bit{r}", "w_in gb_in wsum wall prep var sd max1 gmax gdve xq xT xhi xlo Y out")
        block = ctx.enter_context(nc.Block())
        OUT_PER = 5

        @block.sync
        def _(sp):
            arm(sp, s)
            sp.dma_start(w[:, :, :], A["weight"].rearrange("(k p) d -> p k d", p=P)).then_inc(s["w_in"], 16)
            sp.dma_start(gm[:, :], A["gamma"].partition_broadcast(P)).then_inc(s["gb_in"], 16)
            sp.dma_start(bt[:, :], A["beta"].partition_broadcast(P)).then_inc(s["gb_in"], 16)
            sp.wait_ge(s["gb_in"], ONE + 32)

        @block.gpsimd
        def _(pool):
            pool.wait_ge(s["wsum"], ONE + 1)
            nc.gpsimd.partition_all_reduce(wall[:, :], wsum[:, :], P, bass.bass_isa.ReduceOp.add).then_inc(s["wall"], 1)
            pool.wait_ge(s["max1"], ONE + 1)
            nc.gpsimd.partition_all_reduce(gall[:, :], pmax[:, :], P, bass.bass_isa.ReduceOp.max).then_inc(s["gmax"], 1)

        @block.scalar
        def _(act):
            act.wait_ge(s["var"], ONE + 1)
            nc.scalar.activation(scl[:, :], tmp[:, :], ACT.Sqrt, bias=eps3[:, :]).then_inc(s["sd"], 1)
            with act.Fori(0, NC) as i:
                for k in range(KD):
                    act.wait_ge(s["xT"], ONE + i * KD + k + 1)
                    nc.scalar.activation(xhi[:, k, :], psT[:, k, :], ACT.Copy).then_inc(s["xhi"], 1)

        @block.vector
        def _(dve):
            c = Count(s["prep"])

            def do(ins):
                step(dve, ins, c)
            dve.wait_ge(s["w_in"], ONE + 16)
            step(dve, nc.vector.tensor_reduce(wsum[:, :], w[:, :, :], AX.XY, ALU.add, apply_absolute_value=True),
                 Count(s["wsum"]))
            do(nc.vector.memset(eps3[:, :], 1e-3))
            do(nc.vector.tensor_tensor(tmp[:, :], G.rstd[:, :], G.rstd[:, :], ALU.mult))
            step(dve, nc.vector.tensor_tensor(tmp[:, :], tmp[:, :], G.mv[:, :, 1], ALU.mult), Count(s["var"]))
            dve.wait_ge(s["wall"], ONE + 1)
            do(nc.vector.tensor_scalar(wall[:, :], wall[:, :], 1.0 / (D * D), None, ALU.mult))
            do(nc.vector.tensor_scalar(thr[:, 0:1], wall[:, :], 1e-5, 0.5, ALU.add, ALU.mult))
            do(nc.vector.tensor_scalar(thr[:, 1:2], thr[:, 0:1], -1.0, None, ALU.mult))
            do(nc.vector.tensor_scalar(wt[:, :, :], w[:, :, :], thr[:, 1:2], None, ALU.is_lt))
            do(nc.vector.scalar_tensor_tensor(wq[:, :, :], w[:, :, :], thr[:, 0:1], wt[:, :, :], ALU.is_gt, ALU.subtract))
            dve.wait_ge(s["sd"], ONE + 1)
            do(nc.vector.reciprocal(scl[:, :], scl[:, :]))
            do(nc.vector.tensor_tensor(scl[:, :], scl[:, :], G.rstd[:, :], ALU.mult))
            dve.wait_ge(s["gb_in"], ONE + 32)
            base = c.k
            with dve.Fori(0, NC) as i:
                cl = Count(s["prep"], base, i, 4)
                rows = xn[:, bass.ds(i * CT, CT), :]
                every = lambda a: a.unsqueeze(1).to_broadcast([P, CT, D])
                for t in range(CT):
                    ins = nc.vector.tensor_scalar(xn[:, i * CT + t, :], G.x[:, i * CT + t, :],
                                                  G.mv[:, i * CT + t, 0:1], scl[:, bass.ds(i * CT + t, 1)],
                                                  ALU.subtract, ALU.mult)
                step(dve, ins, cl)
                step(dve, nc.vector.tensor_tensor(rows, rows, every(gm[:, :]), ALU.mult), cl)
                step(dve, nc.vector.tensor_tensor(rows, rows, every(bt[:, :]), ALU.add), cl)
                step(dve, nc.vector.tensor_reduce(tmax[:, bass.ds(i, 1)], rows, AX.XY, ALU.max,
                                                  apply_absolute_value=True), cl)
            step(dve, nc.vector.tensor_reduce(pmax[:, :], tmax[:, :], AX.X, ALU.max), Count(s["max1"]))
            dve.wait_ge(s["gmax"], ONE + 1)
            g = Count(s["gdve"])
            step(dve, nc.vector.reciprocal(gi[:, :], gall[:, :]), g)
            step(dve, nc.vector.tensor_scalar(gi[:, :], gi[:, :], QB, None, ALU.mult), g)
            step(dve, nc.vector.tensor_tensor(osc[:, :], gall[:, :], wall[:, :], ALU.mult), g)
            step(dve, nc.vector.tensor_scalar(osc[:, :], osc[:, :], 0.5 / QB, None, ALU.mult), g)
            with dve.Fori(0, NC) as i:
                cl = Count(s["xq"], 0, i, 2)
                dve.wait_ge(s["xT"], ONE + i * KD)
                step(dve, nc.vector.tensor_scalar(xq[:, :, :], xn[:, bass.ds(i * CT, CT), :], gi[:, :], CLIP,
                                                  ALU.mult, ALU.min), cl)
                step(dve, nc.vector.tensor_scalar(xq[:, :, :], xq[:, :, :], -CLIP, None, ALU.max), cl)
                dve.wait_ge(s["Y"], ONE + i)
                for k in range(KD):
                    dve.wait_ge(s["xhi"], ONE + i * KD + k + 1)
                    nc.vector.tensor_tensor(xlo[:, k, :], psT[:, k, :], xhi[:, k, :], ALU.subtract).then_inc(s["xlo"], 1)
                dve.wait_ge(s["Y"], ONE + i + 1)
                co = Count(s["out"], 0, i, OUT_PER)
                rows = G.x[:, bass.ds(i * CT, CT), :]
                step(dve, nc.vector.scalar_tensor_tensor(y[:, :, :], psY[:, :, 0:D], osc[:, :], rows, ALU.mult, ALU.add), co)
                step(dve, nc.vector.tensor_scalar(rows, y[:, :, :], 1.0, None, ALU.mult), co)
                token_stats(nc, dve, y, st, G.mv[:, bass.ds(i * CT, CT), :], CT, co)
                assert co.k == OUT_PER

        @block.tensor
        def _(pe):
            with pe.Fori(0, NC) as i:
                pe.wait_ge(s["xq"], ONE + i * 2 + 2)
                pe.wait_ge(s["xlo"], ONE + i * KD)
                for k in range(KD):
                    for t in range(CT):
                        last = nc.tensor.transpose(psT[:, k, t * P:t * P + P], xq[:, t, k * P:k * P + P],
                                                   G.ident[:, :])
                    last.then_inc(s["xT"], 1)
                pe.wait_ge(s["xlo"], ONE + i * KD + KD)
                pe.wait_ge(s["out"], ONE + i * OUT_PER)
                for t in range(CT):
                    for k in range(KD):
                        for part, x in enumerate((xhi, xlo)):
                            last = nc.tensor.matmul(psY[:, t, 0:D], x[:, k, t * P:t * P + P], wq[:, k, :],
                                                    start=(k + part == 0), stop=(k == KD - 1 and part == 1))
                last.then_inc(s["Y"], 1)


NM = 63
HALF = NM // 2
BW = 96
GW = 192
KPAD = B * S + 64
YW = 128
KQ = 70
PADW = 32 + S + 32
VW = HD + 1
LT, LV = 2, 3


def rel_phase(nc, G, A):
    rstd_phase(nc, G, "a1n", 1e-5)
    with ExitStack() as ctx:
        sb = lambda n, sh, d=F32: ctx.enter_context(nc.sbuf_tensor(f"a1_{n}", sh, d))
        V = sb("V", [P, NT, NH, VW])
        wpT = sb("wpT", [P, KD, D])
        BDv = sb("BDv", [P, NH // 2, 32])
        rvd = sb("rvd", [P, NH, HD])
        rv62 = sb("rv62", [P, NH, HD])
        QKD = nc.dram_tensor("a1_qk", [4, D, B * S], F16, kind="Internal").ap()
        END = nc.dram_tensor("a1_ends", [2, 2, 32, B * S], F16, kind="Internal").ap()
        GD = nc.dram_tensor("a1_bias", [B * S, NH, BW], F32, kind="Internal").ap()
        PW = nc.dram_tensor("a1_band", [B * S, NH, GW], F32, kind="Internal").ap()
        with ExitStack() as parts:
            psb = lambda n, sh, d=F32: parts.enter_context(nc.sbuf_tensor(f"a1_{n}", sh, d))
            QH = psb("QH", [P, KD, B * S], F16)
            QL = psb("QL", [P, KD, B * S], F16)
            KH = psb("KH", [P, KD, KPAD], F16)
            KL = psb("KL", [P, KD, KPAD], F16)
            tabs = [psb(n, [P, KD, 8, YW], F16) for n in ("TQH", "TQL", "TKH", "TKL")]
            rel_project(nc, G, A, V, wpT, BDv, rvd, rv62, QH, QL, KH, KL, tabs, QKD, END)
            rel_bias(nc, QH, QL, KH, KL, tabs, GD)
        rel_attend(nc, G, A, V, wpT, BDv, rvd, rv62, QKD, END, GD, PW)


def rel_project(nc, G, A, V, wpT, BDv, rvd, rv62, QH, QL, KH, KL, tabs, QKD, END):
    with ExitStack() as ctx:
        sb = lambda n, sh, d=F32: ctx.enter_context(nc.sbuf_tensor(f"a1p_{n}", sh, d))
        ps = lambda n, sh: ctx.enter_context(nc.psum_tensor(f"a1p_{n}", sh, F32))
        wn = sb("wn", [P, 6, D])
        wpn = sb("wpn", [P, KD, D])
        wT = sb("wT", [P, KD, 3 * D])
        rqk = sb("rqk", [P, 2, KD, NM])
        blk = sb("blk", [P, 8])
        dev = sb("dev", [P, 2, KD, YW])
        full = sb("full", [P, 8, YW])
        BDu = sb("BDu", [P, 2, KD, 2, NH])
        vend = sb("vend", [P, NH // 2, 32])
        xn = sb("xn", [P, CT, D])
        xT = sb("xT", [P, KD, CW])
        qf = sb("qf", [P, 4, CW])
        ehl = sb("ehl", [32, 2, 2, CW], F16)
        psT = ps("psT", [P, 2, 512])
        psQ = ps("psQ", [P, 4, 512])
        psE = ps("psE", [P, 2, 512])
        s = sems(nc, ctx, "a1p", "w_in tab_in rv_in zero const tab wtr wev xn xT xTev Q Qf Qhi Qlo V Vev E Ehi Elo e_out q_out")
        block = ctx.enter_context(nc.Block())

        @block.sync
        def _(sp):
            arm(sp, s)
            with nc.allow_non_contiguous_dma("tables, once"):
                sp.dma_start(wn[:, :, :], A["w_qkv"].rearrange("(n p) k -> p n k", p=P)).then_inc(s["w_in"], 16)
                sp.dma_start(wpn[:, :, :], A["w_proj"].rearrange("(n p) k -> p n k", p=P)).then_inc(s["w_in"], 16)
                for n, src in enumerate(("rk", "rq")):
                    sp.dma_start(rqk[:, n, :, :], A[src].rearrange("(k h) d m -> (h d) k m", k=KD)).then_inc(s["tab_in"], 16)
                sp.wait_ge(s["zero"], ONE + 1)
                for a in range(2):
                    sp.dma_start(BDv[64 * a:64 * a + NM, :, HD * a:HD * a + HD],
                                 A["rv"].rearrange("(q a) m d -> m a q d", a=2)[:, a, :, :]).then_inc(s["rv_in"], 16)
                    for e in range(2):
                        rows = 32 - e
                        sp.dma_start(vend[64 * a + 32 * e:64 * a + 32 * e + rows, :, HD * a:HD * a + HD],
                                     A["rv"].rearrange("(q a) m d -> m a q d", a=2)[e * (NM - 1), a, :, :].partition_broadcast(rows)
                                     ).then_inc(s["rv_in"], 16)
                sp.dma_start(rvd[:, :, :], A["rv"][:, 0, :].partition_broadcast(P)).then_inc(s["rv_in"], 16)
                sp.dma_start(rv62[:, :, :], A["rv"][:, NM - 1, :].partition_broadcast(P)).then_inc(s["rv_in"], 16)
            with sp.Fori(0, B) as b:
                for half in range(2):
                    sp.wait_ge(s["Elo"], ONE + b * 4 + half * 2 + 2)
                    for n in range(2):
                        sp.dma_start(END[n, :, :, bass.ds(b * S + half * CW, CW)].rearrange("l e t -> e l t"),
                                     ehl[:, n, :, :]).then_inc(s["e_out"], 16)
            sp.wait_ge(s["Qlo"], ONE + 4 * NC)
            for n, src in enumerate((QH, QL)):
                sp.dma_start(QKD[n, :, :].rearrange("(k p) t -> p k t", p=P), src[:, :, :]).then_inc(s["q_out"], 16)
            for n, src in enumerate((KH, KL)):
                sp.dma_start(QKD[2 + n, :, :].rearrange("(k p) t -> p k t", p=P),
                             src[:, :, 32:32 + B * S]).then_inc(s["q_out"], 16)
            sp.wait_ge(s["q_out"], ONE + 16 * 4)
            sp.wait_ge(s["e_out"], ONE + 16 * 2 * NC)

        @block.gpsimd
        def _(pool):
            nc.gpsimd.memset(vend[:, :, :], 0.0)
            nc.gpsimd.memset(BDv[:, :, :], 0.0).then_inc(s["zero"], 1)
            nc.gpsimd.memset(KH[:, :, :], 0.0)
            nc.gpsimd.memset(KL[:, :, :], 0.0)
            nc.gpsimd.memset(dev[:, :, :, :], 0.0)
            nc.gpsimd.memset(BDu[:, :, :, :, :], 0.0)
            nc.gpsimd.memset(V[:, :, :, :], 1.0)
            c = Count(s["const"])
            step(pool, nc.gpsimd.memset(blk[:, :], 1.0), c)
            step(pool, nc.gpsimd.affine_select(out=blk[:, :], in_=blk[:, :], compare_op=ALU.is_ge, fill=0.0, base=0,
                                               pattern=[[-HD, 8]], channel_multiplier=1), c)
            step(pool, nc.gpsimd.affine_select(out=blk[:, :], in_=blk[:, :], compare_op=ALU.is_ge, fill=0.0,
                                               base=HD - 1, pattern=[[HD, 8]], channel_multiplier=-1), c)

        @block.scalar
        def _(act):
            with act.Fori(0, B) as b:
                for half in range(2):
                    n = b * 2 + half
                    for k in range(KD):
                        act.wait_ge(s["xT"], ONE + n * KD + k + 1)
                        nc.scalar.activation(xT[:, k, :], psT[:, k, :], ACT.Copy).then_inc(s["xTev"], 1)
                    for m in range(4):
                        act.wait_ge(s["Q"], ONE + n * 4 + m + 1)
                        act.wait_ge(s["E"], ONE + n * 2)
                        nc.scalar.activation(qf[:, m, :], psQ[:, m, :], ACT.Copy,
                                             scale=0.25 if m < 2 else 1.0).then_inc(s["Qf"], 1)
                    for t in range(CT):
                        act.wait_ge(s["V"], ONE + n * CT + t + 1)
                        nc.scalar.activation(V[:, n * CT + t, :, 0:HD],
                                             psQ[:, t, 0:D].rearrange("p (h d) -> p h d", h=NH),
                                             ACT.Copy).then_inc(s["Vev"], 1)

        @block.vector
        def _(dve):
            c = Count(s["tab"])

            def do(ins):
                step(dve, ins, c)
            dve.wait_ge(s["const"], ONE + 3)
            dve.wait_ge(s["tab_in"], ONE + 32)
            do(nc.vector.tensor_scalar(rqk[:, 1, :, :], rqk[:, 1, :, :], 0.25, None, ALU.mult))
            for n in range(2):
                lowend, highend, split = (0, NM - 1, HALF + 1) if n == 0 else (0, NM - 1, HALF)
                for k in range(KD):
                    t = rqk[:, n, k, :]
                    do(nc.vector.tensor_scalar(dev[:, n, k, 32:32 + split], t[:, 0:split], t[:, lowend:lowend + 1], None,
                                               ALU.subtract))
                    do(nc.vector.tensor_scalar(dev[:, n, k, 32 + split:32 + NM], t[:, split:NM],
                                               t[:, highend:highend + 1], None, ALU.subtract))
                    do(nc.vector.tensor_tensor(full[:, :, :], dev[:, n, k, :].unsqueeze(1).to_broadcast([P, 8, YW]),
                                               blk[:, :].unsqueeze(2).to_broadcast([P, 8, YW]), ALU.mult))
                    do(nc.vector.tensor_copy(tabs[2 * n][:, k, :, :], full[:, :, :]))
                    do(nc.vector.tensor_tensor(tabs[2 * n + 1][:, k, :, :], full[:, :, :], tabs[2 * n][:, k, :, :],
                                               ALU.subtract))
                    for e in range(2):
                        col = (0 if e == 0 else NM - 1) if n == 0 else (NM - 1 if e == 0 else 0)
                        do(nc.vector.tensor_scalar(BDu[:, n, k, e, 8 * k:8 * k + 8], blk[:, :], t[:, col:col + 1], None,
                                                   ALU.mult))
            for g in range(4):
                dve.wait_ge(s["wtr"], ONE + g + 1)
                dst = wT[:, :, g * D:g * D + D] if g < 3 else wpT[:, :, :]
                nc.vector.tensor_copy(dst.rearrange("p k (n c) -> p n k c", n=2),
                                      psQ[:, g, :].rearrange("p (n k c) -> p n k c", n=2, k=2)).then_inc(s["wev"], 1)
            dve.wait_ge(s["rv_in"], ONE + 16 * 8)
            do(nc.vector.tensor_tensor(BDv[:, :, :], BDv[:, :, :], vend[:, :, :], ALU.subtract))
            do(nc.vector.tensor_tensor(rvd[:, :, :], rvd[:, :, :], rv62[:, :, :], ALU.subtract))
            with dve.Fori(0, B) as b:
                for half in range(2):
                    n = b * 2 + half
                    dve.wait_ge(s["xT"], ONE + n * KD)
                    for t in range(CT):
                        nc.vector.tensor_scalar(xn[:, t, :], G.x[:, n * CT + t, :], G.mv[:, n * CT + t, 0:1],
                                                G.rstd[:, bass.ds(n * CT + t, 1)], ALU.subtract,
                                                ALU.mult).then_inc(s["xn"], 1)
                    for m in range(4):
                        dve.wait_ge(s["Qf"], ONE + n * 4 + m + 1)
                        if m < 2:
                            hi, lo = (a[:, m, bass.ds(n * CW, CW)] for a in (QH, QL))
                        else:
                            hi, lo = (a[:, m - 2, bass.ds(n * CW + 32, CW)] for a in (KH, KL))
                        ins = nc.vector.tensor_scalar(hi, qf[:, m, :], 1.0, None, ALU.mult)
                        ins.then_inc(s["Qhi"], 1)
                        dve.wait_ge(s["Qhi"], ONE + n * 4 + m + 1)
                        nc.vector.tensor_tensor(lo, qf[:, m, :], hi, ALU.subtract).then_inc(s["Qlo"], 1)
                    for m in range(2):
                        dve.wait_ge(s["E"], ONE + n * 2 + m + 1)
                        dve.wait_ge(s["e_out"], ONE + n * 32)
                        nc.vector.tensor_copy(ehl[:, m, 0, :], psE[0:32, m, :]).then_inc(s["Ehi"], 1)
                        dve.wait_ge(s["Ehi"], ONE + n * 2 + m + 1)
                        nc.vector.tensor_tensor(ehl[:, m, 1, :], psE[0:32, m, :], ehl[:, m, 0, :],
                                                ALU.subtract).then_inc(s["Elo"], 1)

        @block.tensor
        def _(pe):
            mm = nc.tensor.matmul
            pe.wait_ge(s["w_in"], ONE + 32)
            for g in range(4):
                for n in range(2):
                    for k in range(KD):
                        src = wn[:, 2 * g + n, k * P:k * P + P] if g < 3 else wpn[:, n, k * P:k * P + P]
                        ins = nc.tensor.transpose(psQ[:, g, (2 * n + k) * P:(2 * n + k) * P + P], src, G.ident[:, :])
                ins.then_inc(s["wtr"], 1)
            pe.wait_ge(s["wev"], ONE + 4)
            pe.wait_ge(s["tab"], ONE + 31)
            with pe.Fori(0, B) as b:
                for half in range(2):
                    n = b * 2 + half
                    pe.wait_ge(s["xn"], ONE + n * CT + CT)
                    pe.wait_ge(s["xTev"], ONE + n * KD)
                    for k in range(KD):
                        for t in range(CT):
                            ins = nc.tensor.transpose(psT[:, k, t * P:t * P + P], xn[:, t, k * P:k * P + P], G.ident[:, :])
                        ins.then_inc(s["xT"], 1)
                    pe.wait_ge(s["xTev"], ONE + n * KD + KD)
                    pe.wait_ge(s["Vev"], ONE + n * CT)
                    for m in range(4):
                        for k in range(KD):
                            ins = mm(psQ[:, m, :], wT[:, k, m * P:m * P + P], xT[:, k, :], start=k == 0, stop=k == KD - 1)
                        ins.then_inc(s["Q"], 1)
                    for t in range(CT):
                        pe.wait_ge(s["Qf"], ONE + n * 4 + t + 1)
                        for k in range(KD):
                            ins = mm(psQ[:, t, 0:D], xT[:, k, t * P:t * P + P], wT[:, k, 2 * D:3 * D],
                                     start=k == 0, stop=k == KD - 1)
                        ins.then_inc(s["V"], 1)
                    pe.wait_ge(s["Elo"], ONE + n * 2)
                    for m in range(2):
                        for k in range(KD):
                            ins = mm(psE[0:32, m, :], BDu[:, m, k, :, :].rearrange("p e h -> p (e h)"), qf[:, 2 * m + k, :],
                                     start=k == 0, stop=k == KD - 1)
                        ins.then_inc(s["E"], 1)


def rel_bias(nc, QH, QL, KH, KL, tabs, GD):
    with ExitStack() as ctx:
        Gt = ctx.enter_context(nc.sbuf_tensor("a1b_G", [P, 2, 32, 2, BW], F32))
        pq = ctx.enter_context(nc.psum_tensor("a1b_q", [P, 4, 512], F32))
        pk = ctx.enter_context(nc.psum_tensor("a1b_k", [P, 4, 512], F32))
        s = sems(nc, ctx, "a1b", "q qev k kev out0 out1")
        block = ctx.enter_context(nc.Block())
        TQH, TQL, TKH, TKL = tabs
        QB_, KB_ = 16, 12

        @block.sync
        def _(sp):
            arm(sp, s)
            with sp.Fori(0, KD) as m:
                for pair in range(4):
                    sp.wait_ge(s["kev"], ONE + (m * 4 + pair + 1) * KB_)
                    sp.dma_start(GD[:, bass.ds(8 * m + 2 * pair, 2), :].rearrange("(p r) h x -> p r (h x)", r=32),
                                 Gt[:, pair % 2, :, :, :].rearrange("p r h x -> p r (h x)")).then_inc(s[f"out{pair % 2}"], 16)
            for n in range(2):
                sp.wait_ge(s[f"out{n}"], ONE + 16 * 4)

        @block.scalar
        def _(act):
            with act.Fori(0, KD) as m:
                for pair in range(4):
                    n = m * 4 + pair
                    for r in range(QB_):
                        act.wait_ge(s[f"out{pair % 2}"], ONE + 16 * (m * 2 + pair // 2))
                        act.wait_ge(s["q"], ONE + n * QB_ + r + 1)
                        nc.scalar.activation(Gt[:, pair % 2, 2 * r:2 * r + 2, :, :].rearrange("p r h x -> p (r h x)"),
                                             pq[:, r % 4, 0:4 * BW], ACT.Copy).then_inc(s["qev"], 1)

        @block.vector
        def _(dve):
            with dve.Fori(0, KD) as m:
                for pair in range(4):
                    n = m * 4 + pair
                    for x in range(KB_):
                        dve.wait_ge(s["k"], ONE + n * KB_ + x + 1)
                        dve.wait_ge(s["qev"], ONE + (n + 1) * QB_)
                        for h in range(2):
                            g = Gt[:, pair % 2, :, h, 8 * x:8 * x + 8]
                            ins = nc.vector.tensor_tensor(
                                g, pk[:, x % 4, :].rearrange("p (x h r) -> p h r x", x=8, h=2)[:, h, :, :], g, ALU.add)
                        ins.then_inc(s["kev"], 1)

        @block.tensor
        def _(pe):
            mm = nc.tensor.matmul
            for m in range(KD):
                for pair in range(4):
                    n = m * 4 + pair
                    hs = slice(2 * pair, 2 * pair + 2)
                    for r in range(QB_):
                        if r < 4:
                            pe.wait_ge(s["qev"], ONE + n * QB_)
                        else:
                            pe.wait_ge(s["qev"], ONE + n * QB_ + r - 3)
                        for e in range(2):
                            tok = 2 * r + e
                            for p, (a, w) in enumerate(((QH, TQH), (QL, TQH), (QH, TQL))):
                                ins = mm(pq[:, r % 4, 2 * BW * e:2 * BW * e + 2 * BW],
                                         a[:, bass.ds(m, 1), tok:tok + 32 * (P - 1) + 1:32].rearrange("p k t -> p (k t)"),
                                         w[:, bass.ds(m, 1), hs, 31 - tok:31 - tok + BW].rearrange("p k h x -> p (k h) x"),
                                         start=p == 0, stop=p == 2)
                        ins.then_inc(s["q"], 1)
                    for x in range(KB_):
                        if x < 4:
                            pe.wait_ge(s["kev"], ONE + n * KB_)
                        else:
                            pe.wait_ge(s["kev"], ONE + n * KB_ + x - 3)
                        for e in range(8):
                            key = 8 * x + e
                            for p, (a, w) in enumerate(((KH, TKH), (KL, TKH), (KH, TKL))):
                                ins = mm(pk[:, x % 4, 64 * e:64 * e + 64],
                                         a[:, bass.ds(m, 1), key:key + 32 * (P - 1) + 1:32].rearrange("p k t -> p (k t)"),
                                         w[:, bass.ds(m, 1), hs, BW - 1 - key:BW - 1 - key + 32].rearrange("p k h x -> p (k h) x"),
                                         start=p == 0, stop=p == 2)
                        ins.then_inc(s["k"], 1)


def skewed(PW):
    pitch = NH * GW
    return bass.AP(PW.tensor, 1, [[S * pitch, B], [GW, NH], [pitch + 1, P], [P * pitch, TPB], [1, 64]])


def both_parts(QKD, first):
    n, b = D * B * S, B * S
    return bass.AP(QKD.tensor, first * n, [[HD * b, NH], [n, 2], [b, HD], [1, b]])


def ends_of(END):
    b = B * S
    return bass.AP(END.tensor, 0, [[b, NH], [NH * b, 2], [32 * b, 2], [1, b]])


def rel_attend(nc, G, A, V, wpT, BDv, rvd, rv62, QKD, END, GD, PW):
    with ExitStack() as ctx:
        sb = lambda n, sh, d=F32: ctx.enter_context(nc.sbuf_tensor(f"a1c_{n}", sh, d))
        ps = lambda n, sh: ctx.enter_context(nc.psum_tensor(f"a1c_{n}", sh, F32))
        Qs = sb("Qs", [KQ, 2, S], F16)
        KLt = sb("KLt", [KQ, 2, S], F16)
        KRt = sb("KRt", [KQ, 2, S], F16)
        Gw = sb("Gw", [P, 2, TPB, GW])
        upper = sb("upper", [P, P], mybir.dt.int32)
        upf = sb("upf", [P, P])
        lowf = sb("lowf", [P, P])
        Vs = sb("Vs", [P, 2, 2, TPB, VW])
        spare = sb("spare", [P, 1])
        nb = sb("nb", [P, 2])
        zero = sb("zero", [P, 1])
        took = sb("took", [P, 1])
        Pb = sb("Pb", [P, 4, PADW])
        PT = sb("PT", [P, 2, TPB, P])
        junk = sb("junk", [P, P])
        rsl = sb("rsl", [P, 16])
        sdl = sb("sdl", [P, 16])
        RS = sb("RS", [P, TPB, NH])
        SD = sb("SD", [P, TPB, NH])
        XOT = sb("XOT", [P, TPB, NH // 2, P])
        Dt = sb("Dt", [P, TPB, NH, 64])
        DT = sb("DT", [P, NH // 2, P])
        t1s = sb("t1s", [P, 2, NH, HD])
        t2 = sb("t2", [P, NH, HD])
        s0 = sb("s0", [P, NH])
        xoT = sb("xoT", [P, D])
        bp = sb("bp", [P, D])
        row = sb("row", [P, 1, D])
        st = sb("st", [P, STW])
        first = nc.dram_tensor("a1_first", [4, P, 1], F32, kind="Internal").ap()
        SP = ps("S", [P, 2, S])
        DG = ps("DG", [P, 512])
        TP = ps("T", [P, 2, 512])
        OP = ps("O", [P, 512])
        s = sems(nc, ctx, "a1c", "const qin0 qin1 gin0 gin1 bp_in S sel bias shift exp pw0 pw1 pw2 pw3 T Tev O Oev diag coll vals "
                 "din Dtr Dev Otr Dm comb Xtr Xev proj fin xz took pools")
        block = ctx.enter_context(nc.Block())
        NS = 2 * TPB
        FIN = 11
        PARTS = 15
        QIN, GIN = 16 * 11, 16 * 4
        TPT = NH // 2

        @block.sync
        def _(sp):
            arm(sp, {n: x for n, x in s.items() if not n.startswith("pw")})
            sp.dma_start(bp[:, :], A["b_proj"].partition_broadcast(P)).then_inc(s["bp_in"], 16)
            sp.wait_ge(s["const"], ONE + 1)

            def load(b, hp, hh, part):
                turn, h, toks = b * TPT + hp, hp * 2 + hh, bass.ds(b * S, S)
                last = turn * NS - TPB * (1 - hh)
                if part == 0:
                    sp.wait_ge(s["S"], ONE + last)
                if part == 11:
                    sp.wait_ge(s["bias"], ONE + last)
                if part < 2:
                    sp.dma_start(Qs[32 * part:32 * part + 32, hh, :], both_parts(QKD, 0)[bass.ds(h, 1), :, :, toks]
                                 ).then_inc(s[f"qin{hh}"], 16)
                elif part < 4:
                    sp.dma_start((KLt, KRt)[part - 2][0:32, hh, :], both_parts(QKD, 2)[bass.ds(h, 1), :, :, toks]
                                 ).then_inc(s[f"qin{hh}"], 16)
                elif part < 8:
                    K, c = (KLt, KRt)[part % 2], part // 6
                    sp.dma_start(K[32 + 16 * c:48 + 16 * c, hh, :], QKD[3 - c, bass.ds(h * HD, HD), toks]
                                 ).then_inc(s[f"qin{hh}"], 16)
                elif part < 9:
                    sp.dma_start(Qs[4 * HD:4 * HD + 4, hh, :],
                                 ends_of(END)[bass.ds(h, 1), :, :, toks]).then_inc(s[f"qin{hh}"], 16)
                elif part < 11:
                    K, end = ((KLt, h), (KRt, h + NH))[part - 9]
                    sp.dma_start(K[68:70, hh, :], END[1, :, bass.ds(end, 1), toks].rearrange("l e t -> (l e) t")
                                 ).then_inc(s[f"qin{hh}"], 16)
                else:
                    g = part - 11
                    src = GD[toks, bass.ds(h, 1), :].rearrange("(i g r) h x -> g r i (h x)", g=4, r=32)
                    sp.dma_start(Gw[32 * g:32 * g + 32, hh, :, 32 * g:32 * g + BW], src[g]).then_inc(s[f"gin{hh}"], 16)

            def load_band(b, hp, hh):
                for q in range(4):
                    sp.wait_ge(s[f"pw{q}"], ONE + 16 * ((b * TPT + hp) * 4 + 2 * (hh + 1)))
                sp.wait_ge(s["Dtr"], ONE + b * TPB * 2)
                h = bass.ds(hp * 2 + hh, 1)
                sp.dma_start(Dt[:, :, h, :], skewed(PW)[bass.ds(b, 1), h, :, :, :]).then_inc(s["din"], 16)

            with sp.Fori(0, B) as b:
                for hh in range(2):
                    for part in range(PARTS):
                        load(b, 0, hh, part)
                with sp.Fori(0, TPT - 1) as hp:
                    for hh in range(2):
                        for part in range(PARTS):
                            load(b, hp + 1, hh, part)
                        load_band(b, hp, hh)
                for hh in range(2):
                    load_band(b, TPT - 1, hh)
            sp.wait_ge(s["bp_in"], ONE + 16)

        @block.gpsimd
        def _(pool):
            c = Count(s["pools"])
            for t in (Qs, KLt, KRt):
                nc.gpsimd.memset(t[:, :, :], 1.0)
            nc.gpsimd.memset(Pb[:, :, 0:32], 0.0)
            nc.gpsimd.memset(Pb[:, :, 32 + S:PADW], 0.0)
            nc.gpsimd.memset(Gw[:, :, :, :], 0.0)
            nc.gpsimd.memset(XOT[:, :, :, :], 0.0)
            nc.gpsimd.memset(Vs[:, :, :, :, :], 0.0)
            nc.gpsimd.memset(zero[:, :], 0.0)
            step(pool, nc.gpsimd.memset(upf[:, :], 1.0), c)
            step(pool, nc.gpsimd.affine_select(out=KLt[:, :, :], in_=KLt[:, :, :], compare_op=ALU.is_ge, fill=0.0,
                                               base=65, pattern=[[0, 2], [0, S]], channel_multiplier=-1), c)
            step(pool, nc.gpsimd.affine_select(out=KRt[:, :, :], in_=KRt[:, :, :], compare_op=ALU.is_ge, fill=0.0,
                                               base=-66, pattern=[[0, 2], [0, S]], channel_multiplier=1), c)
            nc.gpsimd.affine_select(out=upf[:, :], in_=upf[:, :], compare_op=ALU.is_gt, fill=0.0, base=0,
                                    pattern=[[1, P]], channel_multiplier=-1).then_inc(s["const"], 1)

            def store(b, hp, hh):
                for I in range(TPB):
                    k = hh * TPB + I
                    n = (b * TPT + hp) * NS + k
                    pool.wait_ge(s["took"], ONE + n)
                    pool.wait_ge(s["exp"], ONE + n + 1)
                    nc.gpsimd.tensor_tensor(took[:, :], zero[:, :], zero[:, :], ALU.add).then_inc(s["took"], 1)
                    pool.dma_start(PW[bass.ds(b * S + I * P, P), bass.ds(hp * 2 + hh, 1), :],
                                   Pb[:, k % 4, I * P:I * P + GW].unsqueeze(1)).then_inc(s[f"pw{k % 4}"], 16)
            pool.wait_ge(s["const"], ONE + 1)
            for q in range(4):
                pool.dma_start(first[q], zero[:, :]).then_inc(s[f"pw{q}"], 16)
            with pool.Fori(0, B) as b:
                with pool.Fori(0, TPT) as hp:
                    for hh in range(2):
                        store(b, hp, hh)

        FIRST, REST = range(LV), range(LV, NS + LV)

        @block.scalar
        def _(act):
            def steps(b, hp, ks, more):
                T = b * TPT + hp
                for k in ks:
                    if k >= LT and (k - LT < NS or more):
                        v = T * NS + k - LT
                        for half in range(2):
                            act.wait_ge(s["T"], ONE + 2 * v + half + 1)
                            if half == 0:
                                act.wait_ge(s["O"], ONE + v - 1)
                            nc.scalar.activation(PT[:, (k - LT) % 2, 4 * half:4 * half + 4, :].rearrange("p j q -> p (j q)"),
                                                 TP[:, half, :], ACT.Copy).then_inc(s["Tev"], 1)
                    if k < NS or more:
                        n = T * NS + k
                        act.wait_ge(s["shift"], ONE + n + 1)
                        act.wait_ge(s["T"], ONE + (n - 3) * 2)
                        act.wait_ge(s["diag"], ONE + n - 3)
                        act.wait_ge(s[f"pw{k % 4}"], ONE + 16 * (T * 4 + k // 4))
                        if k % TPB == 0:
                            act.wait_ge(s["coll"], ONE + 2 * T + k // TPB - 1)
                        nc.scalar.activation(Pb[:, k % 4, 32:32 + S], SP[:, k % 2, :], ACT.Exp,
                                             bias=nb[:, k % 2:k % 2 + 1],
                                             accum_out=rsl[:, k % NS:k % NS + 1]).then_inc(s["exp"], 1)
                    if k >= LV:
                        v = T * NS + k - LV
                        hh, I = (k - LV) // TPB, (k - LV) % TPB
                        at = 64 * hh + 32 * (I % 2)
                        act.wait_ge(s["O"], ONE + v + 1)
                        nc.scalar.activation(XOT[at:at + VW, I, bass.ds(hp, 1), :].rearrange("p a q -> p (a q)"),
                                             OP[at:at + VW, 0:P], ACT.Copy).then_inc(s["Oev"], 1)
            with act.Fori(0, B) as b:
                steps(b, 0, FIRST, True)
                with act.Fori(0, TPT - 1) as hp:
                    steps(b, hp, REST, True)
                steps(b, TPT - 1, REST, False)
                for I in range(TPB + 1):
                    m = b * TPB + I
                    if I < TPB:
                        for half in range(2):
                            act.wait_ge(s["Dtr"], ONE + 2 * m + half + 1)
                            if half == 0:
                                act.wait_ge(s["Dm"], ONE + m)
                            nc.scalar.activation(DT[:, 4 * half:4 * half + 4, :].rearrange("p j q -> p (j q)"),
                                                 TP[:, half, :], ACT.Copy).then_inc(s["Dev"], 1)
                    if I >= 1:
                        act.wait_ge(s["Xtr"], ONE + m)
                        act.wait_ge(s["proj"], ONE + m - 1)
                        nc.scalar.activation(xoT[:, :], DG[:, 0:D], ACT.Copy).then_inc(s["Xev"], 1)

        @block.vector
        def _(dve):
            def do(ins, name, value):
                ins.then_inc(s[name], 1)
                dve.wait_ge(s[name], ONE + value)

            def steps(b, hp, ks, more):
                T = b * TPT + hp
                for k in ks:
                    if k < NS or more:
                        hh, I = k // TPB % 2, k % TPB
                        n = T * NS + k
                        p2 = k % 2
                        if I == 0:
                            dve.wait_ge(s[f"gin{hh}"], ONE + GIN * (T + k // NS + 1))
                        dve.wait_ge(s["S"], ONE + n + 1)
                        nc.vector.memset(spare[:, :], 0.0)
                        do(nc.vector.copy_predicated(SP[:, p2, I * P:I * P + P], upper[:, :], DG[:, 0:P]), "sel", n + 1)
                        w0, w1 = (32 if I == 0 else 0), (160 if I == TPB - 1 else GW)
                        band = SP[:, p2, I * P - 32 + w0:I * P - 32 + w1]
                        do(nc.vector.tensor_tensor(band, band, Gw[:, hh, I, w0:w1], ALU.add), "bias", n + 1)
                        dve.wait_ge(s["exp"], ONE + n - 1)
                        nc.vector.tensor_reduce(nb[:, p2:p2 + 1], SP[:, p2, :], AX.X, ALU.max,
                                                negate=True).then_inc(s["shift"], 1)
                    if k >= LT and (k - LT < NS or more):
                        v = T * NS + k - LT
                        I = (k - LT) % TPB
                        dve.wait_ge(s["exp"], ONE + v + 1)
                        dve.wait_ge(s["diag"], ONE + v)
                        nc.vector.tensor_tensor_reduce(out=junk[:, :], in0=Pb[:, (k - LT) % 4, 32 + I * P:32 + I * P + P],
                                                       in1=lowf[:, :], scale=1.0, scalar=0.0, op0=ALU.mult, op1=ALU.add,
                                                       accum_out=sdl[:, (k - LT) % NS:(k - LT) % NS + 1]
                                                       ).then_inc(s["diag"], 1)
                        if I == 0:
                            head, hh = T * 2 + (k - LT) // TPB, (k - LT) // TPB % 2
                            hv = hp * 2 + (k - LT) // TPB
                            dve.wait_ge(s["O"], ONE + v - TPB)
                            for one in range(2):
                                w = VW if one else HD
                                ins = nc.vector.tensor_scalar(Vs[:, hh, one, :, 0:w].unsqueeze(2),
                                                              V[:, bass.ds(b * TPB, TPB), bass.ds(hv, 1), 0:w], 1.0, None,
                                                              ALU.mult)
                            ins.then_inc(s["vals"], 1)
                        if I == TPB - 1:
                            head, hh = T * 2 + (k - LT) // TPB, (k - LT) // TPB
                            dve.wait_ge(s["diag"], ONE + v + 1)
                            for src, dst in ((rsl, RS), (sdl, SD)):
                                ins = nc.vector.tensor_scalar(dst[:, :, bass.ds(hp * 2 + hh, 1)],
                                                              src[:, hh * TPB:hh * TPB + TPB].unsqueeze(2), 1.0, None,
                                                              ALU.mult)
                            do(ins, "coll", head + 1)
            dve.wait_ge(s["const"], ONE + 1)
            nc.vector.tensor_copy(upper[:, :], upf[:, :])
            do(nc.vector.tensor_scalar(lowf[:, :], upf[:, :], -1.0, 1.0, ALU.mult, ALU.add), "xz", 1)
            with dve.Fori(0, B) as b:
                steps(b, 0, FIRST, True)
                with dve.Fori(0, TPT - 1) as hp:
                    steps(b, hp, REST, True)
                steps(b, TPT - 1, REST, False)
                cf = Count(s["fin"], 0, b, TPB * FIN)
                bc = lambda a: a.unsqueeze(2).to_broadcast([P, NH, HD])
                f = lambda ins: step(dve, ins, cf)
                for I in range(TPB + 1):
                    m = b * TPB + I
                    if I < TPB:
                        sums = SP[:, I % 2, :].rearrange("p (h c) -> p h c", h=NH)[:, :, 32 * (I % 2):32 * (I % 2) + VW]
                        t1 = t1s[:, I % 2, :, :]
                        f(nc.vector.reciprocal(RS[:, I, :], RS[:, I, :]))
                        dve.wait_ge(s["Otr"], ONE + m + 1)
                        f(nc.vector.tensor_tensor(s0[:, :], sums[:, :, HD], SD[:, I, :], ALU.add))
                        f(nc.vector.tensor_tensor(t2[:, :, :], rvd[:, :, :], bc(s0[:, :]), ALU.mult))
                        f(nc.vector.tensor_tensor(t2[:, :, :], t2[:, :, :], sums[:, :, 0:HD], ALU.add))
                        dve.wait_ge(s["Dm"], ONE + m + 1)
                        f(nc.vector.tensor_tensor(t1, OP[:, 0:D].rearrange("p (h d) -> p h d", h=NH), t2[:, :, :], ALU.add))
                        f(nc.vector.tensor_tensor(t1, t1, bc(RS[:, I, :]), ALU.mult))
                        do(nc.vector.tensor_tensor(t1, t1, rv62[:, :, :], ALU.add), "comb", m + 1)
                    if I >= 1:
                        dve.wait_ge(s["proj"], ONE + m)
                        f(nc.vector.tensor_tensor(row[:, 0, :], DG[:, D:2 * D], bp[:, :], ALU.add))
                        xrow = G.x[:, m - 1, :]
                        f(nc.vector.tensor_tensor(row[:, 0, :], row[:, 0, :], xrow, ALU.add))
                        do(nc.vector.tensor_scalar(xrow, row[:, 0, :], 1.0, None, ALU.mult), "xz", 1 + m)
                        token_stats(nc, dve, row, st, G.mv[:, bass.ds(m - 1, 1), :], 1, cf)
                assert cf.k == TPB * FIN, cf.k

        @block.tensor
        def _(pe):
            mm = nc.tensor.matmul

            def steps(b, hp, ks, more):
                T = b * TPT + hp
                for k in ks:
                    if k < NS or more:
                        hh, I = k // TPB % 2, k % TPB
                        n = T * NS + k
                        if I == 0:
                            pe.wait_ge(s[f"qin{hh}"], ONE + QIN * (T + k // NS + 1))
                        pe.wait_ge(s["exp"], ONE + n - 1)
                        pe.wait_ge(s["sel"], ONE + n)
                        if ks is FIRST and k == 0:
                            pe.wait_ge(s["xz"], ONE + 1 + b * TPB)
                        q = Qs[:, hh, I * P:I * P + P]
                        edge = (I + 1) * P
                        cuts = [(KLt, 0, min(edge, 512)), (KLt, 512, edge), (KRt, edge, 512), (KRt, max(edge, 512), S)]
                        for K, lo, hi in cuts:
                            if lo < hi:
                                mm(SP[:, k % 2, lo:hi], q, K[:, hh, lo:hi], start=True, stop=True)
                        mm(DG[:, 0:P], q, KRt[:, hh, I * P:I * P + P], start=True, stop=True).then_inc(s["S"], 1)
                    if k >= LT and (k - LT < NS or more):
                        v = T * NS + k - LT
                        pe.wait_ge(s["exp"], ONE + v + 1)
                        for half in range(2):
                            pe.wait_ge(s["Tev"], ONE + 2 * v - 1 + half)
                            for q in range(4):
                                J = 4 * half + q
                                ins = nc.tensor.transpose(TP[:, half, q * P:q * P + P],
                                                          Pb[:, (k - LT) % 4, 32 + J * P:32 + J * P + P], G.ident[:, :])
                            ins.then_inc(s["T"], 1)
                    if k >= LV:
                        v = T * NS + k - LV
                        hh, I = (k - LV) // TPB, (k - LV) % TPB
                        at = 64 * hh + 32 * (I % 2)
                        pe.wait_ge(s["Tev"], ONE + 2 * v + 2)
                        pe.wait_ge(s["Oev"], ONE + v - 1)
                        if I == 0:
                            pe.wait_ge(s["vals"], ONE + T * 2 + hh + 1)
                        for J in range(TPB):
                            ins = mm(OP[at:at + VW, 0:P], Vs[:, hh, int(J < I), J, :], PT[:, (k - LV) % 2, J, :],
                                     start=J == 0, stop=J == TPB - 1)
                        ins.then_inc(s["O"], 1)
            pe.wait_ge(s["const"], ONE + 1)
            with pe.Fori(0, B) as b:
                steps(b, 0, FIRST, True)
                with pe.Fori(0, TPT - 1) as hp:
                    steps(b, hp, REST, True)
                steps(b, TPT - 1, REST, False)
                pe.wait_ge(s["Oev"], ONE + (b + 1) * TPT * NS)
                pe.wait_ge(s["exp"], ONE + (b + 1) * TPT * NS)
                pe.wait_ge(s["din"], ONE + 16 * NH * (b + 1))
                for I in range(TPB + 1):
                    m = b * TPB + I
                    if I < TPB:
                        pe.wait_ge(s["comb"], ONE + m - 1)
                        for pair in range(NH // 2):
                            ins = nc.tensor.transpose(SP[:, I % 2, pair * P:pair * P + P], XOT[:, I, pair, :],
                                                      G.ident[:, :])
                        ins.then_inc(s["Otr"], 1)
                        for half in range(2):
                            pe.wait_ge(s["Dev"], ONE + 2 * m - 1 + half)
                            for q in range(4):
                                pair = 4 * half + q
                                ins = nc.tensor.transpose(TP[:, half, q * P:q * P + P],
                                                          Dt[:, I, 2 * pair:2 * pair + 2, :].rearrange("p h m -> p (h m)"),
                                                          G.ident[:, :])
                            ins.then_inc(s["Dtr"], 1)
                        pe.wait_ge(s["Dev"], ONE + 2 * m + 2)
                        pe.wait_ge(s["comb"], ONE + m)
                        for pair in range(NH // 2):
                            ins = mm(OP[:, 32 * pair:32 * pair + 32], DT[:, pair, :], BDv[:, pair, :], start=True, stop=True)
                        ins.then_inc(s["Dm"], 1)
                    if I >= 1:
                        pe.wait_ge(s["comb"], ONE + m)
                        pe.wait_ge(s["xz"], ONE + m)
                        x_out = t1s[:, (I - 1) % 2, :, :].rearrange("p h d -> p (h d)")
                        for q in range(KD):
                            ins = nc.tensor.transpose(DG[:, q * P:q * P + P], x_out[:, q * P:q * P + P], G.ident[:, :])
                        ins.then_inc(s["Xtr"], 1)
                        pe.wait_ge(s["Xev"], ONE + m)
                        for q in range(KD):
                            ins = mm(DG[:, D:2 * D], xoT[:, q * P:q * P + P], wpT[:, q, :], start=q == 0, stop=q == KD - 1)
                        ins.then_inc(s["proj"], 1)
class Globals:
    pass


def macaron_kernel(nc, A, out):
    with ExitStack() as ctx:
        sb = lambda n, s, d=F32: ctx.enter_context(nc.sbuf_tensor(n, s, d))
        G = Globals()
        G.x = sb("x", [P, NT, D])
        G.mv = sb("mv", [P, NT, 2])
        G.rstd = sb("rstd", [P, NT])
        G.ident = sb("ident", [P, P])
        with ExitStack() as early:
            sb = lambda n, s, d=F32: early.enter_context(nc.sbuf_tensor(n, s, d))
            G.ones = sb("ones", [P, P])
            G.b1 = sb("b1", [P, MH])
            G.a1 = sb("a1", [P, MH])
            G.a2h = sb("a2h", [P, D])
            G.b2h = sb("b2h", [P, D])
            G.sw1T = sb("sw1T", [P, KD, HID], F16)
            G.sw2T = sb("sw2T", [P, MH, D], F16)
            prep_phase(nc, G, A)
            for ph in PHASES[:3][:STOP]:
                ph(nc, G, A)
        for ph in PHASES[3:STOP]:
            ph(nc, G, A)
        s_out = ctx.enter_context(nc.semaphore("stored"))
        block = ctx.enter_context(nc.Block())

        @block.sync
        def _(sp):
            sp.dma_start(out.rearrange("b (t p) d -> p (b t) d", p=P), G.x[:, :, :]).then_inc(s_out, 16)
            sp.wait_ge(s_out, 16)


STOP = 99
PHASES = [lambda nc, G, A: ffn_phase(nc, G, 0), local_phase, lambda nc, G, A: ffn_phase(nc, G, 1),
          lambda nc, G, A: bit_phase(nc, G, A, 0),
          rel_phase, lambda nc, G, A: bit_phase(nc, G, A, 1)]
_INS = {'x': 'L0_attn_x', 'wq': 'L0_attn_wq', 'wk': 'L0_attn_wk', 'wv': 'L0_attn_wv', 'wgq': 'L0_attn_wgq',
        'wgk': 'L0_attn_wgk', 'wgv': 'L0_attn_wgv', 'r_out_w': 'L0_attn_r_out_w', 'gl': 'L0_attn_gate_local_w',
        'gr': 'L0_attn_gate_remote_w', 'w_out': 'L0_attn_w_out', 'w1': 'L0_ffn_w1', 'b1': 'L0_ffn_b1',
        'w2': 'L0_ffn_w2', 'b2': 'L0_ffn_b2', 'w_qkv': 'L1_attn_w_qkv', 'w_proj': 'L1_attn_w_proj',
        'b_proj': 'L1_attn_b_proj', 'rq': 'L1_attn_rpe_q_table', 'rk': 'L1_attn_rpe_k_table',
        'rv': 'L1_attn_rpe_v_table', 'weight': 'L1_ffn_weight', 'gamma': 'L1_ffn_ln_gamma', 'beta': 'L1_ffn_ln_beta'}


def kernel(**inputs):
    import numpy as _np
    import concourse.bacc as _bacc
    from concourse import mybir as _mybir
    from concourse.bass_utils import run_bass_kernel_spmd as _run

    nc = _bacc.Bacc("TRN2", target_bir_lowering=False, num_devices=1)
    arrays, aps = {}, {}
    for short, name in _INS.items():
        a = _np.ascontiguousarray(inputs[name])
        arrays[f"in_{name}_dram"] = a
        aps[short] = nc.dram_tensor(f"in_{name}_dram", a.shape, _mybir.dt.from_np(a.dtype), kind="ExternalInput").ap()
    out = nc.dram_tensor("out_0_dram", (4, 1024, 256), _mybir.dt.float32, kind="ExternalOutput").ap()
    nc.disable_value_cache = True
    macaron_kernel(nc, aps, out)
    r = _run(nc, [arrays], core_ids=[0])
    return r.results[0]["out_0_dram"]
```
